# Optimizing a Trainium2 kernel written in Bass

```python
import numpy as np
import jax
import jax.numpy as jnp

def _softmax(x, axis=-1):
    return jax.nn.softmax(x, axis=axis)

def _gelu(x):
    return jax.nn.gelu(x, approximate=True)

def _silu(x):
    return jax.nn.silu(x)

def _sigmoid(x):
    return jax.nn.sigmoid(x)

def _layernorm(x, axis=-1, eps=1e-05):
    m = jnp.mean(x, axis=axis, keepdims=True)
    v = jnp.var(x, axis=axis, keepdims=True)
    return (x - m) / jnp.sqrt(v + eps)

def _scatter_add(tgt, idx, src, axis=0):
    return tgt.at[idx].add(src)

def _segment_sum(src, seg, n):
    return jax.ops.segment_sum(src, seg, n)
kernel_name = 'mk_decoder_postln_d1_seqx_r8_d88193'

def setup_inputs(seed: int=0):
    np.random.seed(seed)
    _w = jnp.asarray

    def _rec_inputs():
        import jax
        import jax.numpy as jnp
        _rk = jax.random.key(seed)
        x = -0.0002928 + 1 * jax.random.normal(jax.random.fold_in(_rk, 1), (8, 256, 128), jnp.float32)
        _lenS = 256 - jax.random.randint(jax.random.fold_in(_rk, 7), (8,), 0, max(1, 256 // 4) + 1, jnp.int32)
        _lenS2 = 256 - jax.random.randint(jax.random.fold_in(_rk, 8), (8,), 0, max(1, 256 // 4) + 1, jnp.int32)
        _ctx_1024P = jax.random.normal(jax.random.fold_in(_rk, 11), (8, 16, 128), jnp.float32)
        _ctx_1024c = jax.random.dirichlet(jax.random.fold_in(_rk, 511), 0.3 * jnp.ones((16,), jnp.float32), (8, 256))
        _ctx_1024t = jnp.einsum('bsk,bkd->bsd', _ctx_1024c, _ctx_1024P)
        _ctx_1024t = _ctx_1024t * jax.lax.rsqrt(jnp.mean(jnp.square(_ctx_1024t)) + 1e-12) * 0.953939
        ctx_1024 = -1.39393e-06 + 0.999914 * (_ctx_1024t + 0.3 * jax.random.normal(jax.random.fold_in(_rk, 611), (8, 256, 128), jnp.float32))
        return (x, ctx_1024)
    x, ctx_1024 = _rec_inputs()

    def _L0_attn_setup():
        import jax, jax.numpy as jnp
        import numpy as np
        B, L = (2, 128)
        D_MODEL, D_CKV, D_CQ = (128, 32, 64)
        N_HEAD, D_HEAD, D_ROPE = (8, 64, 32)
        N_IDX_HEAD = 4
        K_TS, LW = (96, 64)
        ROPE_BASE = 10000.0

        def _pope(x, angles):
            cos, sin = (jnp.cos(angles), jnp.sin(angles))
            mu1, mu2 = jnp.split(jax.nn.softplus(x), 2, axis=-1)
            return jnp.concatenate([mu1 * cos - mu2 * sin, mu1 * sin + mu2 * cos], axis=-1)

        def _forward(x, W_dkv, W_uk, W_uv, W_dq, W_uq, W_qr, W_kr, W_out, idx_wq, idx_wk, idx_w, raw_delta):
            B_, L_, _ = x.shape
            c_kv = x @ W_dkv
            q_i = (x @ idx_wq).reshape(B_, L_, N_IDX_HEAD, D_HEAD)
            k_i = x @ idx_wk
            s_i = jax.nn.relu(jnp.einsum('bthd,bsd->bths', q_i, k_i))
            I = jnp.einsum('bths,h->bts', s_i, idx_w)
            qpos = jnp.arange(L_)[:, None]
            kpos = jnp.arange(L_)[None, :]
            local = (kpos >= qpos - LW + 1) & (kpos <= qpos)
            causal = kpos > qpos
            I = jnp.where(local[None], jnp.inf, I)
            I = jnp.where(causal[None], -jnp.inf, I)
            kk = min(K_TS, L_)
            _, idx = jax.lax.top_k(I, kk)
            bi = jnp.arange(B_)[:, None, None]
            key_c = (c_kv @ W_uk)[bi, idx].reshape(B_, L_, kk, N_HEAD, D_HEAD)
            value = (c_kv @ W_uv)[bi, idx].reshape(B_, L_, kk, N_HEAD, D_HEAD)
            c_q = x @ W_dq
            query_c = (c_q @ W_uq).reshape(B_, L_, N_HEAD, D_HEAD)
            half = D_ROPE // 2
            theta = 1.0 / ROPE_BASE ** (2.0 * jnp.arange(half, dtype=jnp.float32) / D_ROPE)
            delta = -2.0 * jnp.pi * jax.nn.sigmoid(raw_delta)
            angles_q = jnp.arange(L_, dtype=jnp.float32)[:, None] * theta[None, :] + delta
            query_r = _pope((c_q @ W_qr).reshape(B_, L_, N_HEAD, D_ROPE), angles_q[None, :, None, :])
            kr_sel = (x @ W_kr)[bi, idx]
            angles_k = jnp.arange(kk, dtype=jnp.float32)[:, None] * theta[None, :] + delta
            key_r = _pope(kr_sel, angles_k[None, None, :, :])
            scale = (D_HEAD + D_ROPE) ** (-0.5)
            q_c = query_c.transpose(0, 2, 1, 3)
            q_r = query_r.transpose(0, 2, 1, 3)
            k_c = key_c.transpose(0, 3, 1, 2, 4)
            v = value.transpose(0, 3, 1, 2, 4)
            scores = (jnp.einsum('bhld,bhlkd->bhlk', q_c, k_c) + jnp.einsum('bhld,blkd->bhlk', q_r, key_r)) * scale
            attn = jax.nn.softmax(scores.astype(jnp.float32), axis=-1).astype(v.dtype)
            out = jnp.einsum('bhlk,bhlkd->bhld', attn, v)
            out = out.transpose(0, 2, 1, 3).reshape(B_, L_, N_HEAD * D_HEAD)
            return out @ W_out
        key = jax.random.key(seed)
        ks = jax.random.split(key, 14)

        def w(k, shape, fan_in):
            return jax.random.normal(k, shape, dtype=jnp.float32) * fan_in ** (-0.5)
        return {'x': jax.random.normal(ks[0], (B, L, D_MODEL), dtype=jnp.float32), 'W_dkv': w(ks[1], (D_MODEL, D_CKV), D_MODEL), 'W_uk': w(ks[2], (D_CKV, N_HEAD * D_HEAD), D_CKV), 'W_uv': w(ks[3], (D_CKV, N_HEAD * D_HEAD), D_CKV), 'W_dq': w(ks[4], (D_MODEL, D_CQ), D_MODEL), 'W_uq': w(ks[5], (D_CQ, N_HEAD * D_HEAD), D_CQ), 'W_qr': w(ks[6], (D_CQ, N_HEAD * D_ROPE), D_CQ), 'W_kr': w(ks[7], (D_MODEL, D_ROPE), D_MODEL), 'W_out': w(ks[8], (N_HEAD * D_HEAD, D_MODEL), N_HEAD * D_HEAD), 'idx_wq': w(ks[9], (D_MODEL, N_IDX_HEAD * D_HEAD), D_MODEL), 'idx_wk': w(ks[10], (D_MODEL, D_HEAD), D_MODEL), 'idx_w': jnp.ones((N_IDX_HEAD,), dtype=jnp.float32), 'raw_delta': jax.random.normal(ks[11], (D_ROPE // 2,), dtype=jnp.float32) * 0.1}
    _L0_attn_all = _L0_attn_setup()
    _L0_attn_in = {k: v for k, v in _L0_attn_all.items() if k in ('W_dkv', 'W_uk', 'W_uv', 'W_dq', 'W_uq', 'W_qr', 'W_kr', 'W_out', 'idx_wq', 'idx_wk', 'idx_w', 'raw_delta')}
    del _L0_attn_all

    def _L0_xattn_setup():
        import jax, jax.numpy as jnp
        import numpy as np
        import math
        HIDDEN = 128
        HEADS = 16
        HEAD = HIDDEN // HEADS
        SCALE_BASE = 512.0

        def _gammas(heads):
            return 1.0 - jnp.exp(jnp.linspace(math.log(1.0 / 32.0), math.log(1.0 / 512.0), heads))

        def _xpos(x, downscale):
            S, d = (x.shape[2], x.shape[3])
            half = d // 2
            base_scale = (jnp.arange(0, d, 2, dtype=jnp.float32) + 0.4 * d) / (1.4 * d)
            pos = jnp.arange(S, dtype=jnp.float32)
            scale = base_scale[None, :] ** (pos / SCALE_BASE)[:, None]
            if downscale:
                scale = 1.0 / scale
            inv_freq = 1.0 / 10000.0 ** (jnp.arange(half, dtype=jnp.float32) / half)
            sinusoid = pos[:, None] * inv_freq[None, :]
            sin = jnp.repeat(jnp.sin(sinusoid) * scale, 2, axis=-1)
            cos = jnp.repeat(jnp.cos(sinusoid) * scale, 2, axis=-1)
            x1 = x[..., ::2]
            x2 = x[..., 1::2]
            rot = jnp.stack([-x2, x1], axis=-1).reshape(x.shape)
            return x * cos + rot * sin

        def _decay_mask(S, gammas):
            n = jnp.arange(S)[:, None]
            m = jnp.arange(S)[None, :]
            diff = (n - m).astype(jnp.float32)
            mask = n >= m
            pw = jnp.maximum(diff, 0.0)[None, :, :]
            return jnp.where(mask[None, :, :], gammas[:, None, None] ** pw, 0.0)

        def retention_forward(Q, K, V):
            B, S, _ = Q.shape

            def split(x, hd):
                return x.reshape(B, S, HEADS, hd).transpose(0, 2, 1, 3)
            q = _xpos(split(Q, HEAD), downscale=False)
            k = _xpos(split(K, HEAD), downscale=True)
            v = split(V, HEAD)
            D = _decay_mask(S, _gammas(HEADS).astype(Q.dtype))
            scores = jnp.einsum('bhsd,bhtd->bhst', q, k) * D[None]
            out = jnp.einsum('bhst,bhtd->bhsd', scores, v)
            return out.transpose(0, 2, 1, 3).reshape(B, S, HEADS * HEAD)
        key = jax.random.key(seed)
        kq, kk, kv = jax.random.split(key, 3)
        B, S = (2, 256)
        return {'Q': jax.random.normal(kq, (B, S, HIDDEN), dtype=jnp.float32), 'K': jax.random.normal(kk, (B, S, HIDDEN), dtype=jnp.float32), 'V': jax.random.normal(kv, (B, S, HIDDEN), dtype=jnp.float32)}
    _L0_xattn_all = _L0_xattn_setup()
    _L0_xattn_in = {k: v for k, v in _L0_xattn_all.items() if k in ()}
    del _L0_xattn_all

    def _L0_ffn_setup():
        import jax, jax.numpy as jnp
        import numpy as np
        TEMPERATURE = 1.0
        TOPK = 2
        key = jax.random.key(seed)
        ks = jax.random.split(key, 6)
        S, B, H, F, E = (256, 4, 128, 512, 8)
        x = jax.random.normal(ks[0], (S, B, H), dtype=jnp.float32)
        gate_w = jax.random.normal(ks[1], (E, H), dtype=jnp.float32) * (1.0 / np.sqrt(H))
        w1 = jax.random.normal(ks[2], (E, H, F), dtype=jnp.float32) * (1.0 / np.sqrt(H))
        b1 = jnp.zeros((E, F), dtype=jnp.float32)
        w2 = jax.random.normal(ks[3], (E, F, H), dtype=jnp.float32) * (1.0 / np.sqrt(F))
        b2 = jnp.zeros((E, H), dtype=jnp.float32)
        return {'x': x, 'gate_w': gate_w, 'w1': w1, 'b1': b1, 'w2': w2, 'b2': b2}
    _L0_ffn_all = _L0_ffn_setup()
    _L0_ffn_in = {k: v for k, v in _L0_ffn_all.items() if k in ('gate_w', 'w1', 'b1', 'w2', 'b2')}
    del _L0_ffn_all
    return {'x': x, 'ctx_1024': ctx_1024, 'L0_attn_W_dkv': _L0_attn_in['W_dkv'], 'L0_attn_W_uk': _L0_attn_in['W_uk'], 'L0_attn_W_uv': _L0_attn_in['W_uv'], 'L0_attn_W_dq': _L0_attn_in['W_dq'], 'L0_attn_W_uq': _L0_attn_in['W_uq'], 'L0_attn_W_qr': _L0_attn_in['W_qr'], 'L0_attn_W_kr': _L0_attn_in['W_kr'], 'L0_attn_W_out': _L0_attn_in['W_out'], 'L0_attn_idx_wq': _L0_attn_in['idx_wq'], 'L0_attn_idx_wk': _L0_attn_in['idx_wk'], 'L0_attn_idx_w': _L0_attn_in['idx_w'], 'L0_attn_raw_delta': _L0_attn_in['raw_delta'], 'L0_ffn_gate_w': _L0_ffn_in['gate_w'], 'L0_ffn_w1': _L0_ffn_in['w1'], 'L0_ffn_b1': _L0_ffn_in['b1'], 'L0_ffn_w2': _L0_ffn_in['w2'], 'L0_ffn_b2': _L0_ffn_in['b2']}

def reference(x, ctx_1024, L0_attn_W_dkv, L0_attn_W_uk, L0_attn_W_uv, L0_attn_W_dq, L0_attn_W_uq, L0_attn_W_qr, L0_attn_W_kr, L0_attn_W_out, L0_attn_idx_wq, L0_attn_idx_wk, L0_attn_idx_w, L0_attn_raw_delta, L0_ffn_gate_w, L0_ffn_w1, L0_ffn_b1, L0_ffn_w2, L0_ffn_b2):
    import jax
    import jax.numpy as jnp

    def _L0_attn_ref(x, W_dkv, W_uk, W_uv, W_dq, W_uq, W_qr, W_kr, W_out, idx_wq, idx_wk, idx_w, raw_delta):
        import jax, jax.numpy as jnp
        import numpy as np
        B, L = (2, 128)
        D_MODEL, D_CKV, D_CQ = (128, 32, 64)
        N_HEAD, D_HEAD, D_ROPE = (8, 64, 32)
        N_IDX_HEAD = 4
        K_TS, LW = (96, 64)
        ROPE_BASE = 10000.0

        def _pope(x, angles):
            cos, sin = (jnp.cos(angles), jnp.sin(angles))
            mu1, mu2 = jnp.split(jax.nn.softplus(x), 2, axis=-1)
            return jnp.concatenate([mu1 * cos - mu2 * sin, mu1 * sin + mu2 * cos], axis=-1)

        def _forward(x, W_dkv, W_uk, W_uv, W_dq, W_uq, W_qr, W_kr, W_out, idx_wq, idx_wk, idx_w, raw_delta):
            B_, L_, _ = x.shape
            c_kv = x @ W_dkv
            q_i = (x @ idx_wq).reshape(B_, L_, N_IDX_HEAD, D_HEAD)
            k_i = x @ idx_wk
            s_i = jax.nn.relu(jnp.einsum('bthd,bsd->bths', q_i, k_i))
            I = jnp.einsum('bths,h->bts', s_i, idx_w)
            qpos = jnp.arange(L_)[:, None]
            kpos = jnp.arange(L_)[None, :]
            local = (kpos >= qpos - LW + 1) & (kpos <= qpos)
            causal = kpos > qpos
            I = jnp.where(local[None], jnp.inf, I)
            I = jnp.where(causal[None], -jnp.inf, I)
            kk = min(K_TS, L_)
            _, idx = jax.lax.top_k(I, kk)
            bi = jnp.arange(B_)[:, None, None]
            key_c = (c_kv @ W_uk)[bi, idx].reshape(B_, L_, kk, N_HEAD, D_HEAD)
            value = (c_kv @ W_uv)[bi, idx].reshape(B_, L_, kk, N_HEAD, D_HEAD)
            c_q = x @ W_dq
            query_c = (c_q @ W_uq).reshape(B_, L_, N_HEAD, D_HEAD)
            half = D_ROPE // 2
            theta = 1.0 / ROPE_BASE ** (2.0 * jnp.arange(half, dtype=jnp.float32) / D_ROPE)
            delta = -2.0 * jnp.pi * jax.nn.sigmoid(raw_delta)
            angles_q = jnp.arange(L_, dtype=jnp.float32)[:, None] * theta[None, :] + delta
            query_r = _pope((c_q @ W_qr).reshape(B_, L_, N_HEAD, D_ROPE), angles_q[None, :, None, :])
            kr_sel = (x @ W_kr)[bi, idx]
            angles_k = jnp.arange(kk, dtype=jnp.float32)[:, None] * theta[None, :] + delta
            key_r = _pope(kr_sel, angles_k[None, None, :, :])
            scale = (D_HEAD + D_ROPE) ** (-0.5)
            q_c = query_c.transpose(0, 2, 1, 3)
            q_r = query_r.transpose(0, 2, 1, 3)
            k_c = key_c.transpose(0, 3, 1, 2, 4)
            v = value.transpose(0, 3, 1, 2, 4)
            scores = (jnp.einsum('bhld,bhlkd->bhlk', q_c, k_c) + jnp.einsum('bhld,blkd->bhlk', q_r, key_r)) * scale
            attn = jax.nn.softmax(scores.astype(jnp.float32), axis=-1).astype(v.dtype)
            out = jnp.einsum('bhlk,bhlkd->bhld', attn, v)
            out = out.transpose(0, 2, 1, 3).reshape(B_, L_, N_HEAD * D_HEAD)
            return out @ W_out
        return _forward(x, W_dkv, W_uk, W_uv, W_dq, W_uq, W_qr, W_kr, W_out, idx_wq, idx_wk, idx_w, raw_delta)

    def _L0_xattn_ref(Q, K, V):
        import jax, jax.numpy as jnp
        import numpy as np
        import math
        HIDDEN = 128
        HEADS = 16
        HEAD = HIDDEN // HEADS
        SCALE_BASE = 512.0

        def _gammas(heads):
            return 1.0 - jnp.exp(jnp.linspace(math.log(1.0 / 32.0), math.log(1.0 / 512.0), heads))

        def _xpos(x, downscale):
            S, d = (x.shape[2], x.shape[3])
            half = d // 2
            base_scale = (jnp.arange(0, d, 2, dtype=jnp.float32) + 0.4 * d) / (1.4 * d)
            pos = jnp.arange(S, dtype=jnp.float32)
            scale = base_scale[None, :] ** (pos / SCALE_BASE)[:, None]
            if downscale:
                scale = 1.0 / scale
            inv_freq = 1.0 / 10000.0 ** (jnp.arange(half, dtype=jnp.float32) / half)
            sinusoid = pos[:, None] * inv_freq[None, :]
            sin = jnp.repeat(jnp.sin(sinusoid) * scale, 2, axis=-1)
            cos = jnp.repeat(jnp.cos(sinusoid) * scale, 2, axis=-1)
            x1 = x[..., ::2]
            x2 = x[..., 1::2]
            rot = jnp.stack([-x2, x1], axis=-1).reshape(x.shape)
            return x * cos + rot * sin

        def _decay_mask(S, gammas):
            n = jnp.arange(S)[:, None]
            m = jnp.arange(S)[None, :]
            diff = (n - m).astype(jnp.float32)
            mask = n >= m
            pw = jnp.maximum(diff, 0.0)[None, :, :]
            return jnp.where(mask[None, :, :], gammas[:, None, None] ** pw, 0.0)

        def retention_forward(Q, K, V):
            B, S, _ = Q.shape

            def split(x, hd):
                return x.reshape(B, S, HEADS, hd).transpose(0, 2, 1, 3)
            q = _xpos(split(Q, HEAD), downscale=False)
            k = _xpos(split(K, HEAD), downscale=True)
            v = split(V, HEAD)
            D = _decay_mask(S, _gammas(HEADS).astype(Q.dtype))
            scores = jnp.einsum('bhsd,bhtd->bhst', q, k) * D[None]
            out = jnp.einsum('bhst,bhtd->bhsd', scores, v)
            return out.transpose(0, 2, 1, 3).reshape(B, S, HEADS * HEAD)
        return retention_forward(Q, K, V)

    def _L0_ffn_ref(x, gate_w, w1, b1, w2, b2):
        import jax, jax.numpy as jnp
        import numpy as np
        TEMPERATURE = 1.0
        TOPK = 2
        s, b, h = x.shape
        x_flat = x.reshape(s * b, h)
        logits = x_flat @ gate_w.T
        probs = jax.nn.softmax(logits / TEMPERATURE, axis=-1)
        topk_probs, topk_idx = jax.lax.top_k(probs, TOPK)
        hidden = jax.nn.relu(jnp.einsum('th,ehf->tef', x_flat, w1) + b1[None])
        all_out = jnp.einsum('tef,efh->teh', hidden, w2) + b2[None]
        gathered = jnp.take_along_axis(all_out, topk_idx[:, :, None], axis=1)
        y_flat = jnp.sum(gathered * topk_probs[:, :, None], axis=1)
        return y_flat.reshape(s, b, h)
    x = _layernorm(x + _L0_attn_ref(x, L0_attn_W_dkv, L0_attn_W_uk, L0_attn_W_uv, L0_attn_W_dq, L0_attn_W_uq, L0_attn_W_qr, L0_attn_W_kr, L0_attn_W_out, L0_attn_idx_wq, L0_attn_idx_wk, L0_attn_idx_w, L0_attn_raw_delta), axis=-1)
    x = _layernorm(x + _L0_xattn_ref(x, ctx_1024, ctx_1024), axis=-1)
    x = _layernorm(x + _L0_ffn_ref(x, L0_ffn_gate_w, L0_ffn_w1, L0_ffn_b1, L0_ffn_w2, L0_ffn_b2), axis=-1)
    return x

_drawn_inputs = setup_inputs


def setup_inputs(seed=0):
    import zlib

    import numpy as np

    out = dict(_drawn_inputs(seed))
    spreads = {'L0_attn_idx_w': (1.0, 0.2), 'L0_ffn_b1': (0.0, 0.268), 'L0_ffn_b2': (0.0, 0.1)}
    factors = {'L0_attn_raw_delta': 8.0}
    for name, (base, spread) in spreads.items():
        noise = np.random.default_rng([zlib.crc32(name.encode()), seed]).standard_normal(out[name].shape)
        drawn = base * np.exp(spread * noise) if base else spread * noise
        out[name] = jnp.asarray(drawn.astype(out[name].dtype))
    for name, factor in factors.items():
        out[name] = (out[name] * factor).astype(out[name].dtype)
    return out
```

```python
from contextlib import ExitStack

import numpy as np

import concourse.bass as bass
from concourse import mybir

ALU = mybir.AluOpType
ACT = mybir.ActivationFunctionType
F32 = mybir.dt.float32
BF16 = mybir.dt.bfloat16
U32 = mybir.dt.uint32
AX = mybir.AxisListType.X

NB, L, DM = 8, 256, 128
NH, CKV, DR, DH, CQ = 8, 32, 32, 64, 64
WIN, FAR = 64, 32
NIH = 4
RH, RD = 16, 8
NE, FF = 8, 512
TQ = 16
NT = L // TQ
T0 = WIN // TQ
SLOTS = TQ * FAR
SW = 96 + 4 * FAR
SCALE = (DH + DR) ** -0.5
EPS = 1e-5
TAKEN = -3.4e38
NS = 20


def constants():
    c = {}
    p = np.arange(128)
    c["ident"] = np.eye(128)
    c["key_no"] = np.stack([p, p + 128], 1)
    def cut(t, n):
        s = np.arange(n)[None, :]
        return np.where(s <= t - WIN, 3e38, np.where(s > t, -1e30 * (1 + s / 256.0), -3e38))
    c["cut_a"] = cut(64 + p[:, None], 128)
    c["cut_b"] = cut(192 + p[:64, None], 192)
    half = DR // 2
    theta = 1.0 / 10000.0 ** (2.0 * np.arange(half) / DR)
    t = p[:, None] + 128 * np.arange(2)[None, :]
    pos = np.stack([t, t + np.maximum(0, t - (WIN - 1)), t], 1)
    ang = pos[..., None] * theta
    fac = np.array([SCALE, SCALE, 1.0])[None, :, None, None]
    two = lambda a, b: np.stack([a, b], 3).reshape(128, -1)
    co, si = np.cos(ang) * fac, np.sin(ang) * fac
    c["cos2"], c["sin2"] = two(co, co), two(si, si)
    c["ssin2"], c["scos2"] = two(-si, si), two(-co, co)
    rank = WIN + np.arange(FAR)
    ar = theta[np.arange(32) % half][:, None] * rank[None, :]
    sg = np.where(np.arange(32) < half, -1.0, 1.0)[:, None]
    z = np.zeros((32, FAR))
    c["rank_a"] = np.concatenate([z, np.cos(ar), sg * np.sin(ar), z])
    c["rank_b"] = np.concatenate([z, -np.sin(ar), sg * np.cos(ar), z])
    gam = 1.0 - np.exp(np.linspace(np.log(1 / 32.0), np.log(1 / 512.0), RH))
    base = (np.arange(0, RD, 2) + 0.4 * RD) / (1.4 * RD)
    inv = 1.0 / 10000.0 ** (np.arange(RD // 2) / (RD // 2))
    scale = base[None, None, :] ** (t[..., None] / 512.0)
    an = t[..., None] * inv
    dec = gam[None, :] ** p[:, None]
    def table(f, sc, d):
        x = np.repeat(f(an) * sc, 2, axis=-1)[:, :, None, :] * d[:, None, :, None]
        return x.reshape(128, 2, 128)
    sign = np.tile([-1.0, 1.0], 64)
    for n, sc, d in (("q", scale, dec), ("k", 1 / scale, 1 / dec)):
        c["cos_" + n] = table(np.cos, sc, d).reshape(128, 256)
        c["sin_" + n] = (table(np.sin, sc, d) * sign).reshape(128, 256)
    c["causal"] = (p[None, :] >= p[:, None]) * 1.0
    hd = p // RD
    c["carry"] = (hd[:, None] == hd[None, :]) * (gam[hd] ** 128)[:, None]
    c["variant"] = ((p[:, None] % 32) // RD == np.arange(4)[None, :]) * 1.0
    c["expert_no"] = np.tile(np.arange(8.0), (128, 1))
    return c


class Sig:

    def __init__(self, sem, per, lead=0):
        self.sem, self.per, self.lead = sem, per, lead

    def at(self, n, k):
        return (n + self.lead) * self.per + k


class Own:

    def __init__(self, eng, sig):
        self.eng, self.sig, self.n, self.k = eng, sig, 0, 0

    def begin(self, n):
        assert self.k in (0, self.sig.per), (self.sig.sem.name, self.k, self.sig.per)
        self.n, self.k = n, 0

    def did(self, ins):
        ins.then_inc(self.sig.sem, 1)
        self.k += 1
        return self.k

    def wait(self, k):
        self.eng.wait_ge(self.sig.sem, self.sig.at(self.n, k))


class Inst:

    def __init__(self, n, par, half):
        self.n, self.par, self.half = n, par, half


C_BY = "VAVA" + "V" * 8 + "VAVAV"


def build(nc, io, out):
    ctx = ExitStack()
    with ctx:
        sb = lambda name, shape, dt=F32: ctx.enter_context(nc.sbuf_tensor(name, shape, dt))
        pb = lambda name: ctx.enter_context(nc.psum_tensor(name, [128, 512], F32))

        def sig(name, per, lead=0):
            return Sig(ctx.enter_context(nc.semaphore(name)), per, lead)

        con = constants()
        cat, parts = {}, []
        at = 0
        for name, a in con.items():
            full = np.zeros((128, a.shape[1]), np.float32)
            full[:a.shape[0]] = a
            parts.append(full)
            cat[name] = (at, at + a.shape[1])
            at += a.shape[1]
        con_dram = nc.inline_tensor(np.concatenate(parts, 1), name="shape_constants").ap()
        k = np.arange(TQ)
        pick = (k[:, None] == np.arange(128)[None, :] // NH).astype(np.float32)
        hide = np.zeros((TQ, 2, SW), np.float32)
        for par in range(2):
            off = 16 * par
            r = np.arange(96)[None, :]
            hide[:, par, :96] = np.where((r >= off + 1 + k[:, None]) & (r <= off + 64 + k[:, None]), 0, -1e30)
            hide[:, par, 96:] = np.where(np.arange(128)[None, :] // FAR == k[:, None] % 4, 0, -1e30)
        mask_dram = nc.inline_tensor(np.concatenate([pick, hide.reshape(TQ, -1)], 1), name="mask_constants").ap()
        slots_dram = nc.dram_tensor("far_slots", [2, (L - WIN) * FAR], BF16, kind="Internal").ap()

        cst = sb("cst", [128, at])
        C = lambda name, rows=128: cst[0:rows, cat[name][0]:cat[name][1]]
        mbf = sb("mbf", [TQ, 128 + 2 * SW], BF16)
        pick_w = mbf[:, 0:128]
        hide_m = mbf[:, 128:128 + 2 * SW].rearrange("k (a c) -> k a c", a=2)
        wkv = sb("wkv", [128, 64])
        wdq, wdqT = sb("wdq", [128, CQ]), sb("wdqT", [CQ, 128])
        early_w = sb("early_w", [128, 2, L * NH])
        wuq, wuk, wuv = early_w[0:CQ, 0, 0:512], early_w[0:CKV, 0, 512:1024], early_w[0:CKV, 0, 1024:1536]
        mraw = early_w[0:TQ, 1, 0:128 + 2 * SW]
        ots = early_w[0:CKV, :, :]
        wuqT = sb("wuqT", [128, 4, CQ])
        wukvT = sb("wukvT", [128, 8, CKV])
        wqr = sb("wqr", [CQ, 256])
        wout = sb("wout", [128, 4, DM])
        iwq, iwk = sb("iwq", [128, 256]), sb("iwk", [128, 128])
        idxw = sb("idxw", [128, NIH])
        gate, gateT = sb("gate", [NE, DM]), sb("gateT", [DM, NE])
        b1, b1T, b2 = sb("b1", [32, 128]), sb("b1T", [128, 32]), sb("b2", [NE, DM])
        absq = sb("absq", [CQ, 256])
        wq_all = sb("wq_all", [128, 512])
        wvo = sb("wvo", [CKV, NH, DM])
        dl = sb("dl", [128, 6, 17])
        rot_c, rot_s = sb("rot_c", [128, 3, 2, 32]), sb("rot_s", [128, 3, 2, 32])
        rot_t = sb("rot_t", [128, 192])
        rank_t = sb("rank_t", [96, FAR])
        rank_u = sb("rank_u", [96, FAR])
        xn = sb("xn", [128, 2, 2, DM])
        xT = sb("xT", [128, L])
        qiT = sb("qiT", [128, 2, 192])
        kiT = sb("kiT", [128, 192])
        ra, rb = sb("ra", [128, NIH, 128]), sb("rb", [64, NIH, 192])
        sa, sbb = sb("sa", [128, 128]), sb("sbb", [64, 192])
        va, vb = sb("va", [128, FAR]), sb("vb", [64, FAR])
        ia, ib = sb("ia", [128, FAR], U32), sb("ib", [64, FAR], U32)
        ja, jb = sb("ja", [128, FAR], BF16), sb("jb", [64, FAR], BF16)
        qn = sb("qn", [128, 2, NH, 128])
        pa, pr, pe_ = sb("pa", [128, 2, 256]), sb("pr", [128, 2, 256]), sb("pe_", [128, 2, 256])
        nq = sb("nq", [128, 2, 256])
        g1, g2 = sb("g1", [128, 2, 256]), sb("g2", [128, 2, 256])
        ka, kr = sb("ka", [128, 2, 32]), sb("kr", [128, 2, 32])
        kg1, kg2 = sb("kg1", [128, 2, 32]), sb("kg2", [128, 2, 32])
        ktab = sb("ktab", [128, 2, 96])
        kdn = sb("kdn", [128, 2, 128])
        kres = sb("kres", [128, 192])
        kspl = sb("kspl", [128, 2, 3, 192], BF16)
        ckw = sb("ckw", [96, 2, 6, CKV])
        kd = sb("kd", [128, 2, L])
        qall = sb("qall", [128, 2, L * NH])
        sidx = sb("sidx", [128, 2, (L - WIN) * FAR], BF16)
        oh = sb("oh", [128, 2, 2, 2 * SLOTS], BF16)
        gs = sb("gs", [96, 3, SLOTS])
        nmx, lsum, rls = sb("nmx", [128, 2]), sb("lsum", [128, 2]), sb("rls", [128, 2])
        pp = sb("pp", [128, 2, SW])
        ppn = sb("ppn", [128, 2, SW])
        pts = sb("pts", [128, 2, 256])
        vgs = sb("vgs", [128, 4, 128])
        xr, cn = sb("xr", [128, 2, 2, DM]), sb("cn", [128, 2, 2, DM])
        y1, x1, y2, x2 = (sb(n, [128, 2, DM]) for n in ("y1", "x1", "y2", "x2"))
        bst, mv = sb("bst", [128, 2, 6]), sb("mv", [128, 2, 2])
        lnv = sb("lnv", [128, 6, 2])
        rq1, rq2, rqn = (sb(n, [128, 2, DM]) for n in ("rq1", "rq2", "rqn"))
        rk1, rk2, rkn = (sb(n, [128, 2, DM]) for n in ("rk1", "rk2", "rkn"))
        kT4 = sb("kT4", [128, 4, L])
        qT = sb("qT", [128, L])
        st = sb("st", [128, 128])
        sm = sb("sm", [128, 2, 512])
        x2s = sb("x2s", [128, L])
        lg, ex, pr8, gg = (sb(n, [128, 2, NE]) for n in ("lg", "ex", "pr8", "gg"))
        mx2 = sb("mx2", [128, 3, 2])
        v8, i8, f8 = sb("v8", [128, 2, 8]), sb("i8", [128, 2, 8], U32), sb("f8", [128, 2, 8])
        h1, h2 = sb("h1", [128, 2, NE]), sb("h2", [128, 2, NE])
        gTs = sb("gTs", [NE, L])
        x2T = sb("x2T", [128, NB * L])
        acc = sb("acc", [128, NB * 2, DM])
        gall = sb("gall", [128, NB * 2, NE])
        w1s, w2s = sb("w1s", [128, 2, FF]), sb("w2s", [128, 2, 4, DM])
        b1e = sb("b1e", [128, 2, 4])
        ge = sb("ge", [128, 2, 16])
        hs = qall[:, :, :].rearrange("p a (f t) -> p a f t", f=4)
        fst, fmv, fln = sb("fst", [128, 16, 6]), sb("fmv", [128, 16, 2]), sb("fln", [128, 6, 16])
        fout = x2T[:, :].rearrange("p (n c) -> p n c", n=16)

        bG, bS, bT, bV = pb("bG"), pb("bS"), pb("bT"), pb("bV")
        bW = [pb("bW0"), pb("bW1")]
        bC, bR = pb("bC"), pb("bR")

        d_early, d_late = sig("d_early", 0), sig("d_late", 0)
        d_x = [sig(f"d_x{i}", 16) for i in range(2)]
        d_cx = [sig(f"d_cx{i}", 32) for i in range(2)]
        d_put = [sig(f"d_put{i}", 32, 1) for i in range(2)]
        d_idx = [sig(f"d_idx{i}", 16) for i in range(2)]
        d_w = [sig(f"d_w{i}", 32) for i in range(2)]
        d_out = sig("d_out", 0)
        w_full, w_free = sig("w_full", 7), sig("w_free", 7)
        s_prep = sig("s_prep", 14)
        s_mb, s_rot, s_sin, s_dl = (sig(n, 1) for n in ("s_mb", "s_rot", "s_sin", "s_dl"))
        s_zero = sig("s_zero", 1)
        s_pass = sig("s_pass", 0)
        a_full = sig("a_full", 15, 2)
        a_free = sig("a_free", 15, 2)
        own_aa = sig("own_aa", 6, 1)
        a_soft = sig("a_soft", 3, 1)
        own_va = sig("own_va", 10, 1)
        top_a, top_b = sig("top_a", 11, 1), sig("top_b", 11, 1)
        a_slot = sig("a_slot", 2, 1)
        own_ga = sig("own_ga", 28, 1)
        g_kv, g_q, g_spl = sig("g_kv", 1, 1), sig("g_q", 2, 1), sig("g_spl", 1, 1)
        o_ready = sig("o_ready", 6, 2)
        g_full = sig("g_full", 12, 2)
        g_out = sig("g_out", 12, 1)
        s_full = sig("s_full", 16, 1)
        s_max = sig("s_max", 16, 1)
        s_exp = sig("s_exp", 16, 1)
        s_rec = sig("s_rec", 16, 1)
        s_nrm = sig("s_nrm", 16, 1)
        t_full = sig("t_full", 16, 1)
        t_out = sig("t_out", 16, 1)
        v_full = sig("v_full", 12, 1)
        v_out = sig("v_out", 12, 1)
        o_full = sig("o_full", 16, 2)
        o_out = sig("o_out", 16, 1)
        c_full = sig("c_full", 17, 2)
        c_freeA = sig("c_freeA", C_BY.count("A"), 1)
        c_freeV = sig("c_freeV", C_BY.count("V"), 1)
        r_k, r_q = sig("r_k", 1, 1), sig("r_q", 1, 1)
        ln_st, ln_rs = sig("ln_st", 2, 1), sig("ln_rs", 2, 1)
        own_vc = sig("own_vc", 33, 1)
        own_ac = sig("own_ac", 2, 1)
        own_gc = sig("own_gc", 4, 1)
        c_x1, c_x2 = sig("c_x1", 1, 1), sig("c_x2", 1, 1)
        c_av = sig("c_av", 8, 1)
        c_lm, c_ex = sig("c_lm", 1, 1), sig("c_ex", 1, 1)
        c_gg = sig("c_gg", 1, 1)
        c_all = sig("c_all", 1, 1)
        c_acc = sig("c_acc", 1, 2)
        e_full, e_relu = sig("e_full", 32, 1), sig("e_relu", 32, 1)
        e_y, e_acc = sig("e_y", 8, 1), sig("e_acc", 32, 1)
        e_ge, e_b1 = sig("e_ge", 2, 1), sig("e_b1", 2, 1)
        s_fin, fin, fin_a, f_ln = (sig(n, 0) for n in ("s_fin", "fin", "fin_a", "f_ln"))

        def program(stage_a, stage_b, stage_c, fori):

            def step(a, b, c):
                for f, i in ((stage_a, a), (stage_b, b), (stage_c, c)):
                    if i is not None:
                        f(-1, i)
                for s in range(NS):
                    for at_, f, i in ((s, stage_a, a), (s, stage_c, c), (s, stage_b, b), (s + 0.5, stage_a, a),
                                      (s + 0.5, stage_c, c)):
                        if i is not None:
                            f(at_, i)

            I = lambda n: Inst(n, n % 2, n // 2)
            step(I(0), None, None)
            step(I(1), I(0), None)
            with fori(0, NB // 2 - 1) as i:
                step(Inst(2 * i + 2, 0, i + 1), Inst(2 * i + 1, 1, i), Inst(2 * i, 0, i))
                step(Inst(2 * i + 3, 1, i + 1), Inst(2 * i + 2, 0, i + 1), Inst(2 * i + 1, 1, i))
            step(None, I(NB - 1), I(NB - 2))
            step(None, None, I(NB - 1))

        block = ctx.enter_context(nc.Block())

        @block.sync
        def _(sp):
            for s_ in d_put:
                sp.sem_inc(s_.sem, s_.per * s_.lead)
            early = 0
            for dst, src in (
                (cst[:, :], con_dram), (wuq[:, :], io["W_uq"]), (wuk[:, :], io["W_uk"]),
                (wuv[:, :], io["W_uv"]), (wdq[:, :], io["W_dq"]), (gate[:, :], io["gate_w"]),
                (b1[:, :], io["b1"].rearrange("e (f p) -> (e f) p", p=128)),
                (mraw[:, :], mask_dram),
                (dl[:, 0, 0:16], io["raw_delta"].rearrange("(o n) -> o n", o=1).broadcast_to([128, 16])),
            ):
                sp.dma_start(dst, src).then_inc(d_early.sem, 16)
                early += 16
            for r in range(8):
                sp.dma_start(dl[16 * r:16 * r + 16, 0, 16:17],
                             io["raw_delta"].rearrange("(n o) -> n o", o=1)).then_inc(d_early.sem, 16)
                early += 16
            assert early == EARLY
            late = 0
            for dst, src in (
                (wqr[:, :], io["W_qr"]), (wout[:, :, :], io["W_out"].rearrange("(c p) n -> p c n", p=128)),
                (iwq[:, :], io["idx_wq"]), (iwk[:, 0:64], io["idx_wk"]), (iwk[:, 64:128], io["idx_wk"]),
                (idxw[:, :], io["idx_w"].rearrange("(o n) -> o n", o=1).broadcast_to([128, NIH])),
                (wkv[:, 0:32], io["W_dkv"]), (wkv[:, 32:64], io["W_kr"]), (b2[:, :], io["b2"]),
            ):
                sp.dma_start(dst, src).then_inc(d_late.sem, 16)
                late += 16
            assert late == LATE

            def stage_a(s, i):
                if s < 0:
                    sp.wait_ge(a_full.sem, a_full.at(i.n - 2, 1))
                    sp.dma_start(xn[:, i.par, :, :], io["x"][i.n].rearrange("(t p) d -> p t d", p=128)).then_inc(d_x[i.par].sem, 16)
                if s == 13:
                    row = slots_dram[i.par]
                    put = row[0:128 * FAR].rearrange("(p j) -> p j", j=FAR)
                    sp.wait_ge(a_slot.sem, a_slot.at(i.n, 2))
                    sp.dma_start(put, ja[:, :]).then_inc(d_put[i.par].sem, 16)
                    put = row[128 * FAR:].rearrange("(p j) -> p j", j=FAR)
                    sp.dma_start(put, jb[:, :]).then_inc(d_put[i.par].sem, 16)
                    sp.wait_ge(d_put[i.par].sem, d_put[i.par].at(i.half, 32))
                    sp.wait_ge(o_ready.sem, o_ready.at(i.n - 2, 6))
                    sp.dma_start(sidx[:, i.par, :], row.rearrange("(o n) -> o n", o=1).broadcast_to([128, (L - WIN) * FAR])).then_inc(d_idx[i.par].sem, 16)

            def stage_b(s, i):
                if s == 2:
                    sp.wait_ge(c_acc.sem, c_acc.at(i.n - 2, 1))
                    sp.dma_start(xr[:, i.par, :, :], io["x"][i.n].rearrange("(t p) d -> p t d", p=128)).then_inc(d_cx[i.par].sem, 16)
                    sp.dma_start(cn[:, i.par, :, :], io["ctx"][i.n].rearrange("(t p) d -> p t d", p=128)).then_inc(d_cx[i.par].sem, 16)

            def stage_c(s, i):
                pass

            program(stage_a, stage_b, stage_c, sp.Fori)

            def experts(i):
                for p in range(2):
                    sp.wait_ge(e_y.sem, e_y.at(i - 1, 4 * (p + 1)))
                    e = 2 * i + p
                    sp.dma_start(w1s[:, p, :], io["w1"][e]).then_inc(d_w[p].sem, 16)
                    sp.dma_start(w2s[:, p, :, :], io["w2"][e].rearrange("(f p) n -> p f n", p=128)).then_inc(d_w[p].sem, 16)

            with sp.Fori(0, NE // 2) as i:
                experts(i)
            for h in range(4):
                sp.wait_ge(f_ln.sem, h + 1)
                sp.dma_start(out.rearrange("b (t p) d -> p (b t) d", p=128)[:, 4 * h:4 * h + 4, :],
                             fout[:, 4 * h:4 * h + 4, :]).then_inc(d_out.sem, 16)
            sp.wait_ge(d_out.sem, 64)

        @block.gpsimd
        def _(pool):
            for s_ in (own_ga, g_kv, g_q, g_spl, own_gc, r_k, r_q):
                pool.sem_inc(s_.sem, s_.per * s_.lead)
            nc.gpsimd.memset(kdn[:, :, 32:96], 0.0).then_inc(s_zero.sem, 1)
            pool.wait_ge(s_zero.sem, 1)
            pool.wait_ge(s_rot.sem, 2)
            TT = nc.gpsimd.tensor_tensor
            oa = Own(pool, own_ga)
            oc = Own(pool, own_gc)
            hv = lambda ap: ap.rearrange("p (h a d) -> p h a d", a=2, d=16)

            def stage_a(s, i):
                if s < 0:
                    oa.begin(i.n)
                if s == 6:
                    pool.wait_ge(a_soft.sem, a_soft.at(i.n, 3))
                    pool.wait_ge(a_full.sem, a_full.at(i.n - 1, 11))
                    a = oa.did(TT(ktab[:, :, 32:64], kr[:, :, :], ka[:, :, :], ALU.add))
                    b = oa.did(TT(ktab[:, :, 64:80], kr[:, :, 16:32], ka[:, :, 16:32], ALU.add))
                    b = oa.did(TT(ktab[:, :, 80:96], kr[:, :, 0:16], ka[:, :, 0:16], ALU.add))
                    c = oa.did(nc.gpsimd.tensor_copy(kdn[:, :, 0:32], ktab[:, :, 0:32]))
                    oa.wait(b)
                    d = oa.did(TT(kg1[:, :, :], ktab[:, :, 32:64], rot_c[:, 2, :, :], ALU.mult))
                    e = oa.did(TT(kg2[:, :, :], ktab[:, :, 64:96], rot_s[:, 2, :, :], ALU.mult))
                    oa.wait(e)
                    TT(kdn[:, :, 96:128], kg1[:, :, :], kg2[:, :, :], ALU.add).then_inc(g_kv.sem, 1)
                    kt = ktab[:, :, :].rearrange("p t c -> p (t c)")
                    pool.wait_ge(g_full.sem, g_full.at(i.n - 2, 12))
                    pool.sem_inc(s_pass.sem, 1)
                    f = oa.did(nc.gpsimd.tensor_copy(kspl[:, i.par, 0, :], kt))
                    oa.wait(f)
                    f = oa.did(TT(kres[:, :], kt, kspl[:, i.par, 0, :], ALU.subtract))
                    oa.wait(f)
                    pool.sem_inc(s_pass.sem, 1)
                    f = oa.did(nc.gpsimd.tensor_copy(kspl[:, i.par, 1, :], kres[:, :]))
                    oa.wait(f)
                    f = oa.did(TT(kres[:, :], kres[:, :], kspl[:, i.par, 1, :], ALU.subtract))
                    oa.wait(f)
                    pool.sem_inc(s_pass.sem, 1)
                    nc.gpsimd.tensor_copy(kspl[:, i.par, 2, :], kres[:, :]).then_inc(g_spl.sem, 1)
                if s in (5, 7):
                    t = (s - 5) // 2
                    pool.wait_ge(a_soft.sem, a_soft.at(i.n, t + 1))
                    pool.wait_ge(a_full.sem, a_full.at(i.n, 0))
                    a = oa.did(TT(nq[:, t, :], pr[:, t, :], pe_[:, t, :], ALU.add))
                    oa.wait(a)
                    n4 = hv(nq[:, t, :])
                    for kind in range(2):
                        c4 = hv(rot_c[:, kind, t, :]).broadcast_to([128, NH, 2, 16])
                        s4 = hv(rot_s[:, kind, t, :]).broadcast_to([128, NH, 2, 16])
                        a = oa.did(TT(hv(g1[:, kind, :]), n4, c4, ALU.mult))
                        for h in range(2):
                            b = oa.did(TT(hv(g2[:, kind, :])[:, :, h, :], n4[:, :, 1 - h, :], s4[:, :, h, :], ALU.mult))
                        oa.wait(b)
                        u, v = (g[:, kind, :].rearrange("p (h d) -> p h d", d=32) for g in (g1, g2))
                        if kind == 0:
                            oa.did(TT(qn[:, t, :, 32:64], u, v, ALU.add))
                            oa.did(TT(qn[:, t, :, 64:96], u, v, ALU.add))
                        else:
                            oa.wait(oa.k)
                            TT(qn[:, t, :, 96:128], u, v, ALU.add).then_inc(g_q.sem, 1)

            def stage_b(s, i):
                pass

            def rotate(dst, src, cos, sin, t1, t2, done):
                cs, sn = (C(n).rearrange("p (t c) -> p t c", t=2) for n in (cos, sin))
                pairs = lambda ap: ap.rearrange("p t (c e) -> p t c e", e=2)
                oc.did(TT(t1[:, :, :], src, cs, ALU.mult))
                oc_last = None
                TT(pairs(t2[:, :, :])[:, :, :, 0], pairs(src)[:, :, :, 1], pairs(sn)[:, :, :, 0], ALU.mult)
                oc_last = oc.did(TT(pairs(t2[:, :, :])[:, :, :, 1], pairs(src)[:, :, :, 0], pairs(sn)[:, :, :, 1], ALU.mult))
                oc.wait(oc_last)
                TT(dst, t1[:, :, :], t2[:, :, :], ALU.add).then_inc(done.sem, 1)

            def stage_c(s, i):
                if s < 0:
                    oc.begin(i.n)
                if s == 0:
                    pool.wait_ge(d_cx[i.par].sem, d_cx[i.par].at(i.half, 32))
                    pool.wait_ge(c_full.sem, c_full.at(i.n - 1, 3))
                    rotate(rkn[:, :, :], cn[:, i.par, :, :], "cos_k", "sin_k", rk1, rk2, r_k)
                if s == 3:
                    pool.wait_ge(c_x1.sem, c_x1.at(i.n, 1))
                    rotate(rqn[:, :, :], x1[:, :, :], "cos_q", "sin_q", rq1, rq2, r_q)

            program(stage_a, stage_b, stage_c, pool.Fori)
            assert oa.k == own_ga.per and oc.k == own_gc.per, (oa.k, oc.k)

        @block.tensor
        def _(pe):
            for s_ in (a_full, g_full, s_full, t_full, v_full, o_full, c_full, c_av, e_full, e_y):
                pe.sem_inc(s_.sem, s_.per * s_.lead)
            MM = nc.tensor.matmul
            ident = C("ident")

            def flip(dst, src, n, lo=0):
                return MM(dst, src, ident[lo:lo + n, lo:lo + n], is_transpose=True, start=True, stop=True)

            pe.wait_ge(d_early.sem, EARLY)
            for c in range(4):
                last = flip(bG[:, 64 * c:64 * c + 64], wuq[:, 128 * c:128 * c + 128], CQ)
            last.then_inc(w_full.sem, 1)
            for j, w in enumerate((wuk, wuv)):
                for c in range(4):
                    last = flip(bR[:, 32 * (4 * j + c):32 * (4 * j + c) + 32], w[:, 128 * c:128 * c + 128], CKV)
            last.then_inc(w_full.sem, 1)
            flip(bS[0:CQ, 0:128], wdq[:, :], 128)
            flip(bS[:, 128:136], gate[:, :], NE)
            flip(bS[:, 136:168], b1[:, :], 32).then_inc(w_full.sem, 1)
            pe.wait_ge(w_free.sem, 3)
            for h in range(NH):
                lo = 64 * (h % 2)
                last = MM((bT, bC)[h % 2][0:CQ, 32 * (h // 2):32 * (h // 2) + 32], wuqT[lo:lo + 64, h // 2, :], wukvT[lo:lo + 64, h // 2, :],
                          start=True, stop=True)
            last.then_inc(w_full.sem, 1)
            pe.wait_ge(d_late.sem, LATE)
            for j in range(2):
                for c in range(4):
                    h = 2 * c + j
                    lo = 64 * j
                    last = MM(bW[j][0:CKV, 128 * c:128 * c + 128], wukvT[lo:lo + 64, 4 + h // 2, :],
                              wout[lo:lo + 64, h // 2, :], start=True, stop=True)
                last.then_inc(w_full.sem, 1)
            pe.wait_ge(w_free.sem, 4)
            MM(bV[:, 0:256], wdqT[:, :], absq[:, :], start=True, stop=True)
            MM(bV[:, 256:512], wdqT[:, :], wqr[:, :], start=True, stop=True).then_inc(w_full.sem, 1)
            pe.wait_ge(w_free.sem, 7)
            pe.wait_ge(s_mb.sem, 1)

            def stage_a(s, i):
                p = i.par

                def bank(u):
                    if u >= 2:
                        pe.wait_ge(a_free.sem, a_free.at(i.n, u - 1))
                    else:
                        pe.wait_ge(a_free.sem, a_free.at(i.n - 1, 14 + u))
                    return bW[(u + p) % 2]

                full = lambda ins: ins.then_inc(a_full.sem, 1)
                if s == 0:
                    w = bank(0)
                    pe.wait_ge(d_x[p].sem, d_x[p].at(i.half, 16))
                    pe.wait_ge(w_free.sem, 7)
                    for t in range(2):
                        last = flip(w[:, 128 * t:128 * t + 128], xn[:, p, t, :], 128)
                    full(last)
                if s == 1:
                    w = bank(1)
                    pe.wait_ge(a_free.sem, a_free.at(i.n, 1))
                    for c in range(2):
                        last = MM(w[:, 192 * c:192 * c + 192], iwq[:, 128 * c:128 * c + 128], xT[:, 64:256],
                                  start=True, stop=True)
                    full(last)
                if s == 1.5:
                    w = bank(2)
                    full(MM(w[:, 0:192], iwk[:, :], xT[:, 0:192], start=True, stop=True))
                if s in (2, 3):
                    w = bank(s + 1)
                    lo = 64 * (s - 2)
                    pe.wait_ge(a_free.sem, a_free.at(i.n, 3))
                    for c in range(2):
                        last = MM(w[:, 128 * c:128 * c + 128], qiT[lo:lo + 64, c, 0:128], kiT[lo:lo + 64, 0:128],
                                  start=True, stop=True)
                    full(last)
                if s in (3.5, 4.5):
                    w = bank(int(s) + 2)
                    lo = 64 * (int(s) - 3)
                    pe.sem_inc(s_pass.sem, 1)
                    for c in range(2):
                        last = MM(w[0:64, 192 * c:192 * c + 192], qiT[lo:lo + 64, c, 128:192], kiT[lo:lo + 64, :],
                                  start=True, stop=True)
                    full(last)
                if s in (5, 5.5):
                    for t in [int(2 * s) - 10]:
                        w = bank(7 + t)
                        full(MM(w[:, :], xT[:, 128 * t:128 * t + 128], wq_all[:, :], start=True, stop=True))
                if s == 6:
                    w = bank(9)
                    for t in range(2):
                        MM(w[:, 64 * t:64 * t + 64], xT[:, 128 * t:128 * t + 128], wkv[:, :], start=True, stop=True)
                    for c in range(6):
                        last = MM(w[0:96, 128 + 32 * c:160 + 32 * c], xT[:, 32 * c:32 * c + 96], wkv[:, 0:32],
                                  start=True, stop=True)
                    full(last)
                if s == 9:
                    w = bank(10)
                    pe.wait_ge(g_kv.sem, g_kv.at(i.n, 1))
                    for t in range(2):
                        last = flip(w[:, 128 * t:128 * t + 128], kdn[:, t, :], 128)
                    full(last)
                if s in (12, 12.5, 14, 14.5):
                    t = (int(s) - 12) // 2
                    pe.wait_ge(g_q.sem, g_q.at(i.n, t + 1))
                    for hg in [int(2 * s) % 2]:
                        w = bank(11 + 2 * t + hg)
                        for h in range(4):
                            last = flip(w[:, 128 * h:128 * h + 128], qn[:, t, 4 * hg + h, :], 128)
                        full(last)

            def gather(i, tile):
                p, g = i.par, tile - T0
                if tile % 2 == 0:
                    pe.wait_ge(o_ready.sem, o_ready.at(i.n, g // 2 + 1))
                if g == 0:
                    pe.wait_ge(g_spl.sem, g_spl.at(i.n, 1))
                pe.wait_ge(g_out.sem, g_out.at(i.n, g))
                w = bG
                kts = [0] if tile < 12 else [0, 1]
                n = 0
                for kt in kts:
                    rows = 128 if kt == 0 else 64
                    for part in range(3):
                        last = MM(w[0:96, :], kspl[0:rows, p, part, 96 * kt:96 * kt + 96],
                                  oh[0:rows, (g // 2) % 2, kt, SLOTS * (tile % 2):SLOTS * (tile % 2) + SLOTS],
                                  start=(n == 0), stop=(n == 3 * len(kts) - 1))
                        n += 1
                last.then_inc(g_full.sem, 1)

            def scores(i, tile):
                p, g = i.par, tile - T0
                pe.wait_ge(s_exp.sem, s_exp.at(i.n, tile))
                o = 0
                q = qall[:, p, 128 * tile:128 * tile + 128]
                if tile < T0:
                    MM(bS[:, o:o + 96], q, kd[:, p, 0:96], start=True, stop=True).then_inc(s_full.sem, 1)
                    return
                MM(bS[:, o:o + SW], pick_w, hide_m[:, tile % 2, :], start=True, stop=True,
                   skip_group_check=True)
                k0 = 32 * ((tile - T0) // 2)
                MM(bS[:, o:o + 96], q, kd[:, p, k0:k0 + 96], start=False, stop=True, skip_group_check=True)
                pe.wait_ge(g_out.sem, g_out.at(i.n, g + 1))
                for c in range(4):
                    last = MM(bS[32 * c:32 * c + 32, o + 96:o + SW], qall[0:96, p, 128 * tile + 32 * c:128 * tile + 32 * c + 32],
                              gs[:, g % 3, 128 * c:128 * c + 128], start=False, stop=True, skip_group_check=True)
                last.then_inc(s_full.sem, 1)

            def far_latents(i, tile):
                g = tile - T0
                pe.wait_ge(o_out.sem, o_out.at(i.n, tile - 2))
                pe.sem_inc(s_pass.sem, 1)
                for c in range(4):
                    o = 32 * c
                    last = flip(bV[:, o:o + 32], gs[0:32, g % 3, 128 * c:128 * c + 128], 32)
                last.then_inc(v_full.sem, 1)

            def turn(i, tile):
                pe.wait_ge(s_nrm.sem, s_nrm.at(i.n, tile + 1))
                pe.wait_ge(t_out.sem, t_out.at(i.n, tile))
                w = ppn[:, tile % 2, :]
                if tile < T0:
                    flip(bT[0:96, 0:128], w[:, 0:96], 128).then_inc(t_full.sem, 1)
                else:
                    flip(bT[:, 0:128], w[:, 0:128], 128)
                    flip(bT[:, 128:256], w[:, 96:SW], 128).then_inc(t_full.sem, 1)

            def weigh(i, tile):
                g, p = tile - T0, i.par
                pe.wait_ge(t_out.sem, t_out.at(i.n, tile + 1))
                pe.wait_ge(o_out.sem, o_out.at(i.n, tile))
                if T0 <= tile + 2 < NT:
                    pe.wait_ge(v_out.sem, v_out.at(i.n, g + 3))
                o = 256
                near = ckw[:, p, 0 if g < 0 else g // 2, :]
                last = MM(bV[0:32, o:o + 128], near, pts[0:96, tile % 2, 0:128], start=True, stop=True,
                          skip_group_check=True)
                if g >= 0:
                    pe.wait_ge(v_out.sem, v_out.at(i.n, g + 1))
                    for c in range(4):
                        last = MM(bV[0:32, o + 32 * c:o + 32 * c + 32], vgs[:, g % 4, 32 * c:32 * c + 32],
                                  pts[:, tile % 2, 128 + 32 * c:160 + 32 * c], start=False, stop=True,
                                  skip_group_check=True)
                last.then_inc(o_full.sem, 1)

            def stage_b(s, i):
                if s < 0:
                    return
                if s == 0:
                    pe.wait_ge(a_free.sem, a_free.at(i.n, 15))
                if T0 <= s < NT:
                    far_latents(i, s)
                if T0 <= s + 1 < NT:
                    gather(i, s + 1)
                if s < NT:
                    scores(i, s)
                if 1 <= s <= NT:
                    turn(i, s - 1)
                if 2 <= s <= NT + 1:
                    weigh(i, s - 2)

            def stage_c(s, i):
                p = i.par

                def emptied(u, n=i.n):
                    f = c_freeA if C_BY[u] == "A" else c_freeV
                    pe.wait_ge(f.sem, f.at(n, C_BY[:u + 1].count(C_BY[u])))

                def half(u):
                    if u >= 1:
                        emptied(u - 1)
                    else:
                        emptied(16, i.n - 1)
                    return bC

                full = lambda ins: ins.then_inc(c_full.sem, 1)
                if s == 0:
                    w = half(0)
                    pe.wait_ge(o_out.sem, o_out.at(i.n, 16))
                    o3 = ots[:, p, :].rearrange("c (t h) -> c t h", h=NH)
                    for t in range(2):
                        for h in range(NH):
                            last = MM(w[:, 128 * t:128 * t + 128], o3[:, 128 * t:128 * t + 128, h], wvo[:, h, :],
                                      start=(h == 0), stop=(h == NH - 1))
                    full(last)
                if s == 2:
                    w = half(1)
                    pe.wait_ge(r_k.sem, r_k.at(i.n, 1))
                    for t in range(2):
                        last = flip(w[:, 128 * t:128 * t + 128], rkn[:, t, :], 128)
                    full(last)
                if s == 2.5:
                    w = half(2)
                    full(MM(w[:, 0:128], rkn[:, 0, :], cn[:, p, 0, :], start=True, stop=True))
                if s == 4:
                    w = half(3)
                    pe.wait_ge(r_q.sem, r_q.at(i.n, 1))
                    for t in range(2):
                        last = flip(w[:, 128 * t:128 * t + 128], rqn[:, t, :], 128)
                    full(last)
                if s in range(5, 13):
                    u = s - 5
                    t, g = u // 4, u % 4
                    w = half(4 + u)
                    for v in range(4):
                        last = MM(w[:, 128 * v:128 * v + 128], kT4[32 * g:32 * g + 32, v, 128 * t:128 * t + 128],
                                  qT[32 * g:32 * g + 32, 128 * t:128 * t + 128], start=True, stop=True)
                    full(last)
                if s in range(6, 14):
                    u = s - 6
                    t, g = u // 4, u % 4
                    emptied(4 + u)
                    for v in range(4):
                        h = 4 * g + v
                        last = MM(bR[:, 128 * t + RD * h:128 * t + RD * h + RD], sm[:, u % 2, 128 * v:128 * v + 128],
                                  cn[:, p, t, RD * h:RD * h + RD], start=True, stop=True)
                    last.then_inc(c_av.sem, 1)
                if s == 13.5:
                    w = half(12)
                    full(MM(w[:, 0:128], qT[:, 128:256], st[:, :], start=True, stop=True))
                if s == 17:
                    w = half(13)
                    pe.wait_ge(c_x2.sem, c_x2.at(i.n, 1))
                    for t in range(2):
                        last = flip(w[:, 128 * t:128 * t + 128], x2[:, t, :], 128)
                    full(last)
                if s == 18:
                    w = half(14)
                    for t in range(2):
                        last = MM(w[:, 8 * t:8 * t + 8], x2s[:, 128 * t:128 * t + 128], gateT[:, :], start=True, stop=True)
                    full(last)
                if s == 19:
                    w = half(15)
                    pe.wait_ge(c_gg.sem, c_gg.at(i.n, 1))
                    for t in range(2):
                        last = flip(w[0:NE, 128 * t:128 * t + 128], gg[:, t, :], 128)
                    full(last)
                if s == 19.5:
                    w = half(16)
                    for t in range(2):
                        last = MM(w[:, 128 * t:128 * t + 128], gTs[:, 128 * t:128 * t + 128], b2[:, :], start=True, stop=True)
                    full(last)

            program(stage_a, stage_b, stage_c, pe.Fori)

            hid, res = [bG, bS, bW[0], bW[1]], [bV, bT]
            pe.wait_ge(c_all.sem, c_all.at(NB - 1, 1))
            pe.wait_ge(c_acc.sem, c_acc.at(NB - 1, 1))

            def up(i, j):
                p, tg = j // 4, j % 4
                if tg == 0:
                    pe.wait_ge(d_w[p].sem, d_w[p].at(i, 32))
                for f in range(4):
                    pe.wait_ge(e_relu.sem, e_relu.at(i, 4 * j + f - 3))
                    MM(hid[f][:, :], w1s[:, p, 128 * f:128 * f + 128], x2T[:, 512 * tg:512 * tg + 512],
                       start=True, stop=True).then_inc(e_full.sem, 1)

            def down(i, j):
                p = j // 4
                pe.wait_ge(e_relu.sem, e_relu.at(i, 4 * j + 4))
                pe.wait_ge(e_acc.sem, e_acc.at(i, 4 * j - 4))
                for t in range(4):
                    for f in range(4):
                        last = MM(res[j % 2][:, 128 * t:128 * t + 128], hs[:, j % 2, f, 128 * t:128 * t + 128],
                                  w2s[:, p, f, :], start=(f == 0), stop=(f == 3))
                last.then_inc(e_y.sem, 1)

            with pe.Fori(0, NE // 2) as i:
                for j in range(9):
                    if j < 8:
                        up(i, j)
                    if j >= 1:
                        down(i, j - 1)

        @block.scalar
        def _(act):
            for s_ in (a_free, a_soft, own_aa, e_b1, s_exp, t_out, v_out, o_out, c_freeA, ln_rs, own_ac, c_ex, c_all, e_relu):
                act.sem_inc(s_.sem, s_.per * s_.lead)
            AC = nc.scalar.activation
            copy = nc.scalar.copy
            act.wait_ge(d_early.sem, EARLY)
            AC(dl[:, 1, :], dl[:, 0, :], ACT.Exp, scale=-1.0).then_inc(s_sin.sem, 1)
            act.wait_ge(s_dl.sem, 1)
            AC(dl[:, 4, :], dl[:, 2, :], ACT.Sin).then_inc(s_sin.sem, 1)
            AC(dl[:, 5, :], dl[:, 3, :], ACT.Sin).then_inc(s_sin.sem, 1)

            def empty(k, pairs):
                act.wait_ge(w_full.sem, k)
                for dst, src in pairs:
                    last = copy(dst, src)
                last.then_inc(w_free.sem, 1)

            empty(1, [(wuqT[:, :, :], bG[:, 0:256].rearrange("p (c n) -> p c n", c=4))])
            empty(2, [(wukvT[:, :, :], bR[:, 0:256].rearrange("p (c n) -> p c n", c=8))])
            empty(3, [(wdqT[:, :], bS[0:CQ, 0:128]), (gateT[:, :], bS[:, 128:136]), (b1T[:, :], bS[:, 136:168])])
            act.wait_ge(w_full.sem, 4)
            heads = absq[:, :].rearrange("q (c j n) -> q j c n", j=2, n=CKV)
            for j in range(2):
                last = AC(heads[:, j, :, :], (bT, bC)[j][0:CQ, 0:128].rearrange("q (c n) -> q c n", c=4), ACT.Copy,
                          scale=SCALE)
            last.then_inc(w_free.sem, 1)
            for j in range(2):
                empty(5 + j, [(wvo[:, j::2, :], bW[j][0:CKV, :].rearrange("p (c n) -> p c n", c=4))])
            empty(7, [(wq_all[:, :], bV[:, :])])

            oa = Own(act, own_aa)
            oc = Own(act, own_ac)

            def stage_a(s, i):
                p = i.par
                full = lambda u: act.wait_ge(a_full.sem, a_full.at(i.n, u + 1))
                free = lambda ins: ins.then_inc(a_free.sem, 1)
                ring = lambda u: bW[(u + p) % 2]
                if s < 0:
                    oa.begin(i.n)
                if s == 0:
                    full(0)
                    free(copy(xT[:, :], ring(0)[:, 0:256]))
                if s == 1:
                    full(1)
                    free(copy(qiT[:, :, :], ring(1)[:, 0:384].rearrange("p (c n) -> p c n", c=2)))
                if s == 1.5:
                    full(2)
                    free(copy(kiT[:, :], ring(2)[:, 0:192]))
                if s in (2, 3):
                    full(s + 1)
                    if s == 2:
                        act.wait_ge(own_va.sem, own_va.at(i.n, 0))
                    free(AC(ra[:, s - 2::2, :], ring(s + 1)[:, 0:256].rearrange("p (c n) -> p c n", c=2), ACT.Relu))
                if s in (3.5, 4.5):
                    s = int(s)
                    full(s + 2)
                    free(AC(rb[:, s - 3::2, :], ring(s + 2)[0:64, 0:384].rearrange("p (c n) -> p c n", c=2), ACT.Relu))
                    s = -1
                if s in (5, 5.5):
                    for t in [int(2 * s) - 10]:
                        full(7 + t)
                        w = ring(7 + t)
                        act.wait_ge(g_q.sem, g_q.at(i.n - 1, t + 1))
                        act.wait_ge(a_full.sem, a_full.at(i.n, 0))
                        copy(qn[:, t, :, 0:32], w[:, 0:256].rearrange("p (h c) -> p h c", c=32))
                        k = oa.did(AC(pa[:, t, :], w[:, 256:512], ACT.Abs))
                        free(AC(pr[:, t, :], w[:, 256:512], ACT.Relu))
                        oa.wait(k)
                        k = oa.did(AC(pa[:, t, :], pa[:, t, :], ACT.Exp, scale=-1.0))
                        oa.wait(k)
                        AC(pe_[:, t, :], pa[:, t, :], ACT.Ln, bias=1.0).then_inc(a_soft.sem, 1)
                if s == 6:
                    full(9)
                    w = ring(9)
                    kv = w[:, 0:128].rearrange("p (t c) -> p t c", t=2)
                    act.wait_ge(g_spl.sem, g_spl.at(i.n, 0))
                    copy(ktab[:, :, 0:32], kv[:, :, 0:32])
                    act.wait_ge(o_full.sem, o_full.at(i.n - 2, 16))
                    copy(ckw[:, p, :, :], w[0:96, 128:320].rearrange("p (c n) -> p c n", c=6))
                    k = oa.did(AC(ka[:, :, :], kv[:, :, 32:64], ACT.Abs))
                    free(AC(kr[:, :, :], kv[:, :, 32:64], ACT.Relu))
                    oa.wait(k)
                    k = oa.did(AC(ka[:, :, :], ka[:, :, :], ACT.Exp, scale=-1.0))
                    oa.wait(k)
                    AC(ka[:, :, :], ka[:, :, :], ACT.Ln, bias=1.0).then_inc(a_soft.sem, 1)
                if s == 9:
                    full(10)
                    copy(kd[:, p, :], ring(10)[:, 0:256]).then_inc(a_free.sem, 1)
                if s in (12, 12.5, 14, 14.5):
                    t = (int(s) - 12) // 2
                    for hg in [int(2 * s) % 2]:
                        u = 11 + 2 * t + hg
                        full(u)
                        dst = qall[:, p, 1024 * t:1024 * t + 1024].rearrange("p (t h) -> p h t", h=NH)[:, 4 * hg:4 * hg + 4, :]
                        free(copy(dst, ring(u)[:, :].rearrange("p (h t) -> p h t", h=4)))

            def stage_b(s, i):
                p = i.par
                if s < 0:
                    return
                if T0 <= s < NT:
                    g = s - T0
                    act.wait_ge(v_full.sem, v_full.at(i.n, g + 1))
                    act.wait_ge(o_full.sem, o_full.at(i.n, s - 3))
                    copy(vgs[:, g % 4, :], bV[:, 0:128]).then_inc(v_out.sem, 1)
                if s < NT:
                    act.wait_ge(s_max.sem, s_max.at(i.n, s + 1))
                    act.wait_ge(s_nrm.sem, s_nrm.at(i.n, s - 1))
                    o, w = 0, (96 if s < T0 else SW)
                    AC(pp[:, s % 2, 0:w], bS[:, o:o + w], ACT.Exp, bias=nmx[:, s % 2:s % 2 + 1],
                       accum_out=lsum[:, s % 2:s % 2 + 1]).then_inc(s_exp.sem, 1)
                if 1 <= s <= NT:
                    t = s - 1
                    act.wait_ge(t_full.sem, t_full.at(i.n, t + 1))
                    act.wait_ge(o_full.sem, o_full.at(i.n, t - 1))
                    if t < T0:
                        copy(pts[0:96, t % 2, 0:128], bT[0:96, 0:128]).then_inc(t_out.sem, 1)
                    else:
                        copy(pts[:, t % 2, :], bT[:, 0:256]).then_inc(t_out.sem, 1)
                if 2 <= s <= NT + 1:
                    t = s - 2
                    if t == 0:
                        act.wait_ge(c_full.sem, c_full.at(i.n - 2, 1))
                    act.wait_ge(o_full.sem, o_full.at(i.n, t + 1))
                    o = 256
                    copy(ots[:, p, 128 * t:128 * t + 128], bV[0:32, o:o + 128]).then_inc(o_out.sem, 1)

            def rsqrt_start(i, k):
                act.wait_ge(ln_st.sem, ln_st.at(i.n, k))
                m = oc.did(AC(lnv[:, 1, :], lnv[:, 0, :], ACT.Ln))
                oc.wait(m)
                AC(lnv[:, 2, :], lnv[:, 1, :], ACT.Exp, scale=-0.5).then_inc(ln_rs.sem, 1)

            def stage_c(s, i):
                full = lambda u: act.wait_ge(c_full.sem, c_full.at(i.n, u + 1))
                if s < 0:
                    oc.begin(i.n)
                if s == 1:
                    rsqrt_start(i, 1)
                if s == 2:
                    full(1)
                    for v in range(4):
                        last = AC(kT4[:, v, :], bC[:, 0:256], ACT.Copy, scale=C("variant")[:, v:v + 1])
                    last.then_inc(c_freeA.sem, 1)
                if s == 4:
                    full(3)
                    copy(qT[:, :], bC[:, 0:256]).then_inc(c_freeA.sem, 1)
                if s == 15:
                    rsqrt_start(i, 2)
                if s == 17:
                    full(13)
                    copy(x2T[:, bass.ds(i.n * L, L)], bC[:, 0:256]).then_inc(c_all.sem, 1)
                    copy(x2s[:, :], bC[:, 0:256]).then_inc(c_freeA.sem, 1)
                if s == 18:
                    act.wait_ge(c_freeV.sem, c_freeV.at(i.n, C_BY[:15].count("V")))
                    AC(ex[:, :, :], lg[:, :, :], ACT.Exp).then_inc(c_ex.sem, 1)
                if s == 19:
                    full(15)
                    copy(gTs[:, :], bC[0:NE, 0:256]).then_inc(c_freeA.sem, 1)

            program(stage_a, stage_b, stage_c, act.Fori)
            assert oa.k == own_aa.per and oc.k == own_ac.per, (oa.k, oc.k)

            hid = [bG, bS, bW[0], bW[1]]
            with act.Fori(0, NE // 2) as i:
                for j in range(8):
                    p = j // 4
                    if j % 4 == 0:
                        act.wait_ge(e_relu.sem, e_relu.at(i - 1, 16 * p + 16))
                        copy(b1e[:, p, :], b1T[:, bass.ds(8 * i + 4 * p, 4)]).then_inc(e_b1.sem, 1)
                        act.wait_ge(e_b1.sem, e_b1.at(i, p + 1))
                    act.wait_ge(e_y.sem, e_y.at(i, j - 1))
                    for f in range(4):
                        act.wait_ge(e_full.sem, e_full.at(i, 4 * j + f + 1))
                        AC(hs[:, j % 2, f, :], hid[f][:, :], ACT.Relu, bias=b1e[:, p, f:f + 1]).then_inc(e_relu.sem, 1)
            act.wait_ge(fin.sem, 1)
            AC(fln[:, 1, :], fln[:, 0, :], ACT.Ln).then_inc(fin_a.sem, 1)
            act.wait_ge(fin_a.sem, 1)
            AC(fln[:, 2, :], fln[:, 1, :], ACT.Exp, scale=-0.5).then_inc(fin_a.sem, 1)

        @block.vector
        def _(dve):
            for s_ in (own_va, top_a, top_b, a_slot, o_ready, g_out, s_max, s_rec, s_nrm, c_freeV, ln_st, own_vc,
                       c_x1, c_x2, c_gg, c_acc, e_acc, e_ge):
                dve.sem_inc(s_.sem, s_.per * s_.lead)
            TT, TS, STT = nc.vector.tensor_tensor, nc.vector.tensor_scalar, nc.vector.scalar_tensor_tensor
            prep = Own(dve, s_prep)

            def link(ins):
                prep.wait(prep.did(ins))

            nc.vector.memset(rank_t[0:32, :], 1.0)
            dve.wait_ge(d_early.sem, EARLY)
            nc.vector.tensor_copy(mbf[:, :], mraw[:, :]).then_inc(s_mb.sem, 1)
            dve.wait_ge(s_sin.sem, 1)
            link(TS(dl[:, 2, :], dl[:, 1, :], 1.0, None, ALU.add))
            link(nc.vector.reciprocal(dl[:, 1, :], dl[:, 2, :]))
            link(TS(dl[:, 2, :], dl[:, 1, :], -2 * np.pi, np.pi, ALU.mult, ALU.add))
            link(TS(dl[:, 2, :], dl[:, 2, :], 3.1415925, -3.1415925, ALU.min, ALU.max))
            TS(dl[:, 3, :], dl[:, 1, :], -np.pi, None, ALU.mult).then_inc(s_dl.sem, 1)
            dve.wait_ge(s_sin.sem, 3)
            link(TT(dl[:, 1, :], dl[:, 5, :], dl[:, 5, :], ALU.mult))
            link(TS(dl[:, 0, :], dl[:, 1, :], -2.0, 1.0, ALU.mult, ALU.add))
            link(TS(dl[:, 1, :], dl[:, 4, :], -1.0, None, ALU.mult))
            wide = lambda ap: ap.rearrange("p (g d) -> p g d", d=16)
            cd, sd = (dl[:, k:k + 1, 0:16].broadcast_to([128, 12, 16]) for k in (0, 1))
            rc, rs = (r[:, :, :, :].rearrange("p k t (h d) -> p (k t h) d", d=16) for r in (rot_c, rot_s))
            rt = wide(rot_t[:, :])
            link(TT(rc, wide(C("cos2")), cd, ALU.mult))
            link(TT(rt, wide(C("sin2")), sd, ALU.mult))
            link(TT(rc, rc, rt, ALU.subtract))
            link(TT(rs, wide(C("ssin2")), cd, ALU.mult))
            link(TT(rt, wide(C("scos2")), sd, ALU.mult))
            TT(rs, rs, rt, ALU.add).then_inc(s_rot.sem, 1)
            for lo in (32, 64):
                r = slice(lo, lo + 32)
                link(TS(rank_u[r, :], C("rank_a")[r, :], dl[r, 0, 16:17], None, ALU.mult))
                last = STT(rank_t[r, :], C("rank_b")[r, :], dl[r, 1, 16:17], rank_u[r, :], ALU.mult, ALU.add)
            last.then_inc(s_rot.sem, 1)
            dve.wait_ge(s_rot.sem, 2)
            dve.wait_ge(d_late.sem, LATE)
            assert prep.k == s_prep.per, prep.k

            ov, oc = Own(dve, own_va), Own(dve, own_vc)

            def settled():
                dve.sem_inc(s_pass.sem, 1)

            def weighted(raw, dst, cut, n):
                k = ov.did(TS(dst, raw[:, 0, :], idxw[0:n, 0:1], None, ALU.mult))
                for h in range(1, NIH):
                    ov.wait(k)
                    k = ov.did(STT(dst, raw[:, h, :], idxw[0:n, h:h + 1], dst, ALU.mult, ALU.add))
                ov.wait(k)
                ov.did(TT(dst, dst, cut, ALU.min))

            def top(i, k, sig_, s_, v, idx):
                r, what = k // 3, k % 3
                if k == 0:
                    dve.wait_ge(own_va.sem, own_va.at(i.n, 5 if sig_ is top_a else 10))
                else:
                    dve.wait_ge(sig_.sem, sig_.at(i.n, k))
                settled()
                v8_, i8_ = v[:, 8 * r:8 * r + 8], idx[:, 8 * r:8 * r + 8]
                if what == 0:
                    ins = nc.vector.max(v8_, s_)
                elif what == 1:
                    ins = nc.vector.max_index(i8_, v8_, s_)
                else:
                    ins = nc.vector.match_replace(s_, v8_, s_, TAKEN)
                ins.then_inc(sig_.sem, 1)

            def stage_a(s, i):
                if s < 0:
                    ov.begin(i.n)
                if s == 4:
                    dve.wait_ge(a_free.sem, a_free.at(i.n, 5))
                    weighted(ra, sa[:, :], C("cut_a"), 128)
                if s == 5:
                    dve.wait_ge(a_free.sem, a_free.at(i.n, 7))
                    weighted(rb, sbb[:, :], C("cut_b", 64), 64)
                for d in range(2) if s == int(s) else ():
                    ka_, kb_ = 2 * (s - 5) + d, 2 * (s - 6) + d
                    if 0 <= ka_ < 11:
                        top(i, ka_, top_a, sa[:, :], va, ia)
                    if 0 <= kb_ < 11:
                        top(i, kb_, top_b, sbb[:, :], vb, ib)
                if s == 12:
                    dve.wait_ge(d_put[1 - i.par].sem, d_put[1 - i.par].at(i.half - 1 + i.par, 32))
                    dve.wait_ge(top_a.sem, top_a.at(i.n, 11))
                    nc.vector.tensor_copy(ja[:, :], ia[:, :]).then_inc(a_slot.sem, 1)
                    dve.wait_ge(top_b.sem, top_b.at(i.n, 11))
                    nc.vector.tensor_copy(jb[:, :], ib[:, :]).then_inc(a_slot.sem, 1)

            def stage_b(s, i):
                p = i.par
                if s < 0:
                    return
                if s in (1, 3, 5, 7, 9, 11):
                    c = s // 2
                    if c == 0:
                        dve.wait_ge(d_idx[p].sem, d_idx[p].at(i.half, 16))
                    dve.wait_ge(g_full.sem, g_full.at(i.n, 2 * c - 2))
                    src = sidx[:, p, 2 * SLOTS * c:2 * SLOTS * (c + 1)]
                    last = TS(oh[:, c % 2, 0, :], src, C("key_no")[:, 0:1], None, ALU.is_equal)
                    if c >= 4:
                        last = TS(oh[0:64, c % 2, 1, :], src[0:64, :], C("key_no")[0:64, 1:2], None, ALU.is_equal)
                    last.then_inc(o_ready.sem, 1)
                if 1 <= s <= NT:
                    t = s - 1
                    w = 96 if t < T0 else SW
                    dve.wait_ge(s_exp.sem, s_exp.at(i.n, t + 1))
                    nc.vector.reciprocal(rls[:, t % 2:t % 2 + 1], lsum[:, t % 2:t % 2 + 1]).then_inc(s_rec.sem, 1)
                    dve.wait_ge(t_full.sem, t_full.at(i.n, t - 1))
                    dve.wait_ge(s_rec.sem, s_rec.at(i.n, t + 1))
                    TS(ppn[:, t % 2, 0:w], pp[:, t % 2, 0:w], rls[:, t % 2:t % 2 + 1], None,
                       ALU.mult).then_inc(s_nrm.sem, 1)
                if T0 <= s + 1 < NT:
                    g = s + 1 - T0
                    dve.wait_ge(v_full.sem, v_full.at(i.n, g - 2))
                    dve.wait_ge(g_full.sem, g_full.at(i.n, g + 1))
                    TT(gs[:, g % 3, :].rearrange("p (t j) -> p t j", j=FAR),
                       bG[0:96, :].rearrange("p (t j) -> p t j", j=FAR),
                       rank_t[:, :].rearrange("p (o j) -> p o j", o=1).broadcast_to([96, TQ, FAR]),
                       ALU.mult).then_inc(g_out.sem, 1)
                if s < NT:
                    dve.wait_ge(s_full.sem, s_full.at(i.n, s + 1))
                    o, w = 0, (96 if s < T0 else SW)
                    nc.vector.tensor_reduce(nmx[:, s % 2:s % 2 + 1], bS[:, o:o + w], AX, ALU.max,
                                            negate=True).then_inc(s_max.sem, 1)

            def moments(i, y):
                for t in range(2):
                    k = oc.did(nc.vector.bn_stats(bst[:, t, :], y[:, t, :]))
                oc.wait(k)
                settled()
                for t in range(2):
                    k = oc.did(nc.vector.bn_aggr(mv[:, t, :], bst[:, t, :]))
                oc.wait(k)
                TS(lnv[:, 0, :], mv[:, :, 1], EPS, None, ALU.add).then_inc(ln_st.sem, 1)

            def normalise(i, k, x, y, done):
                dve.wait_ge(ln_rs.sem, ln_rs.at(i.n, k))
                m = oc.did(TT(lnv[:, 3, :], lnv[:, 2, :], lnv[:, 2, :], ALU.mult))
                oc.wait(m)
                m = oc.did(TT(lnv[:, 4, :], lnv[:, 3, :], lnv[:, 0, :], ALU.mult))
                oc.wait(m)
                m = oc.did(TS(lnv[:, 3, :], lnv[:, 4, :], -0.5, 1.5, ALU.mult, ALU.add))
                oc.wait(m)
                m = oc.did(TT(lnv[:, 5, :], lnv[:, 3, :], lnv[:, 2, :], ALU.mult))
                oc.wait(m)
                oc.did(TS(x[:, 0, :], y[:, 0, :], mv[:, 0, 0:1], lnv[:, 5, 0:1], ALU.subtract, ALU.mult))
                TS(x[:, 1, :], y[:, 1, :], mv[:, 1, 0:1], lnv[:, 5, 1:2], ALU.subtract, ALU.mult).then_inc(done.sem, 1)

            def stage_c(s, i):
                p = i.par
                full = lambda u: dve.wait_ge(c_full.sem, c_full.at(i.n, u + 1))
                free = lambda ins: ins.then_inc(c_freeV.sem, 1)
                freed = lambda u: dve.wait_ge(c_freeV.sem, c_freeV.at(i.n, C_BY[:u + 1].count("V")))
                two = lambda ap: ap.rearrange("p (t c) -> p t c", t=2)
                if s < 0:
                    oc.begin(i.n)
                if s == 0:
                    full(0)
                    dve.wait_ge(d_cx[p].sem, d_cx[p].at(i.half, 32))
                    free(TT(y1[:, :, :], two(bC[:, 0:256]), xr[:, p, :, :], ALU.add))
                    freed(0)
                    moments(i, y1)
                if s == 1:
                    normalise(i, 1, x1, y1, c_x1)
                if s == 2.5:
                    full(2)
                    free(TT(st[:, :], bC[:, 0:128], C("carry"), ALU.mult))
                if s in range(5, 13):
                    u = s - 5
                    dve.wait_ge(c_av.sem, c_av.at(i.n, u - 1))
                    full(4 + u)
                    free(TT(sm[:, u % 2, :].rearrange("p (v c) -> p v c", v=4), bC[:, :].rearrange("p (v c) -> p v c", v=4),
                            C("causal").rearrange("p (o c) -> p o c", o=1).broadcast_to([128, 4, 128]), ALU.mult))
                if s == 13.5:
                    full(12)
                    dve.wait_ge(c_x1.sem, c_x1.at(i.n, 1))
                    free(TT(y2[:, 1, :], bC[:, 0:128], x1[:, 1, :], ALU.add))
                if s == 14:
                    dve.wait_ge(c_av.sem, c_av.at(i.n, 8))
                    freed(12)
                    oc.did(TT(y2[:, 0, :], bR[:, 0:128], x1[:, 0, :], ALU.add))
                    k = oc.did(TT(y2[:, 1, :], bR[:, 128:256], y2[:, 1, :], ALU.add))
                    oc.wait(k)
                    moments(i, y2)
                if s == 15:
                    normalise(i, 2, x2, y2, c_x2)
                if s == 18:
                    full(14)
                    k = oc.did(nc.vector.tensor_reduce(mx2[:, 0, :], bC[:, 0:16].rearrange("p (t e) -> p t e", t=2), AX, ALU.max))
                    oc.wait(k)
                    one = lambda r: mx2[:, r, :].rearrange("p (t o) -> p t o", o=1).broadcast_to([128, 2, NE])
                    free(TT(lg[:, :, :], bC[:, 0:16].rearrange("p (t e) -> p t e", t=2), one(0), ALU.subtract))
                    dve.wait_ge(c_ex.sem, c_ex.at(i.n, 1))
                    k = oc.did(nc.vector.tensor_reduce(mx2[:, 1, :], ex[:, :, :], AX, ALU.add))
                    oc.wait(k)
                    k = oc.did(nc.vector.reciprocal(mx2[:, 2, :], mx2[:, 1, :]))
                    oc.wait(k)
                    k = oc.did(TT(pr8[:, :, :], ex[:, :, :], one(2), ALU.mult))
                    for t in range(2):
                        oc.wait(k)
                        settled()
                        m = oc.did(nc.vector.max(v8[:, t, :], pr8[:, t, :]))
                    for t in range(2):
                        oc.wait(m)
                        settled()
                        k = oc.did(nc.vector.max_index(i8[:, t, :], v8[:, t, :], pr8[:, t, :]))
                    oc.wait(k)
                    k = oc.did(nc.vector.tensor_copy(f8[:, :, :], i8[:, :, :]))
                    oc.wait(k)
                    for t in range(2):
                        for h, r in ((h1, 0), (h2, 1)):
                            k = oc.did(TS(h[:, t, :], C("expert_no"), f8[:, t, r:r + 1], v8[:, t, r:r + 1],
                                          ALU.is_equal, ALU.mult))
                    oc.wait(k)
                    TT(gg[:, :, :], h1[:, :, :], h2[:, :, :], ALU.add).then_inc(c_gg.sem, 1)
                if s == 19.5:
                    full(16)
                    dve.wait_ge(c_x2.sem, c_x2.at(i.n, 1))
                    free(TT(acc[:, bass.ds(2 * i.n, 2), :], two(bC[:, 0:256]), x2[:, :, :], ALU.add))
                    dve.wait_ge(c_gg.sem, c_gg.at(i.n, 1))
                    nc.vector.tensor_copy(gall[:, bass.ds(2 * i.n, 2), :], gg[:, :, :]).then_inc(c_acc.sem, 1)

            program(stage_a, stage_b, stage_c, dve.Fori)
            assert ov.k == own_va.per and oc.k == own_vc.per, (ov.k, oc.k)

            res = [bV, bT]
            dve.wait_ge(c_acc.sem, c_acc.at(NB - 1, 1))
            with dve.Fori(0, NE // 2) as i:
                for j in range(8):
                    p, tg = j // 4, j % 4
                    if tg == 0:
                        dve.wait_ge(e_acc.sem, e_acc.at(i - 1, 16 * p + 16))
                        nc.vector.tensor_copy(ge[:, p, :], gall[:, :, bass.ds(2 * i + p, 1)].rearrange("p t o -> p (t o)")).then_inc(e_ge.sem, 1)
                        dve.wait_ge(e_ge.sem, e_ge.at(i, p + 1))
                    dve.wait_ge(e_y.sem, e_y.at(i, j + 1))
                    for t in range(4):
                        n = 4 * tg + t
                        dve.wait_ge(e_acc.sem, e_acc.at(i, 4 * j + t - 15))
                        STT(acc[:, n, :], res[j % 2][:, 128 * t:128 * t + 128], ge[:, p, n:n + 1], acc[:, n, :],
                            ALU.mult, ALU.add).then_inc(e_acc.sem, 1)

            own = Own(dve, s_fin)
            dve.wait_ge(e_acc.sem, e_acc.at(NE // 2 - 1, 32))
            for n in range(16):
                k = own.did(nc.vector.bn_stats(fst[:, n, :], acc[:, n, :]))
            own.wait(k)
            for n in range(16):
                k = own.did(nc.vector.bn_aggr(fmv[:, n, :], fst[:, n, :]))
            own.wait(k)
            TS(fln[:, 0, :], fmv[:, :, 1], EPS, None, ALU.add).then_inc(fin.sem, 1)
            dve.wait_ge(fin_a.sem, 2)
            own.wait(own.did(TT(fln[:, 3, :], fln[:, 2, :], fln[:, 2, :], ALU.mult)))
            own.wait(own.did(TT(fln[:, 4, :], fln[:, 3, :], fln[:, 0, :], ALU.mult)))
            own.wait(own.did(TS(fln[:, 3, :], fln[:, 4, :], -0.5, 1.5, ALU.mult, ALU.add)))
            own.wait(own.did(TT(fln[:, 5, :], fln[:, 3, :], fln[:, 2, :], ALU.mult)))
            for n in range(16):
                last = TS(fout[:, n, :], acc[:, n, :], fmv[:, n, 0:1], fln[:, 5, n:n + 1], ALU.subtract, ALU.mult)
                if n % 4 == 3:
                    last.then_inc(f_ln.sem, 1)


EARLY, LATE = 16 * 17, 16 * 9

_INS = ["x", "ctx_1024"] + ["L0_attn_" + n for n in (
    "W_dkv", "W_uk", "W_uv", "W_dq", "W_uq", "W_qr", "W_kr", "W_out", "idx_wq", "idx_wk", "idx_w", "raw_delta",
)] + ["L0_ffn_" + n for n in ("gate_w", "w1", "b1", "w2", "b2")]


def kernel(**inputs):
    import concourse.bacc as bacc
    from concourse.bass_utils import run_bass_kernel_spmd

    nc = bacc.Bacc("TRN2", target_bir_lowering=False, num_devices=1)
    arrays, io = {}, {}
    for name in _INS:
        a = np.ascontiguousarray(inputs[name])
        arrays["in_" + name] = a
        short = name.replace("L0_attn_", "").replace("L0_ffn_", "").replace("ctx_1024", "ctx")
        io[short] = nc.dram_tensor("in_" + name, a.shape, mybir.dt.from_np(a.dtype), kind="ExternalInput").ap()
    out = nc.dram_tensor("out", (NB, L, DM), F32, kind="ExternalOutput").ap()
    build(nc, io, out)
    r = run_bass_kernel_spmd(nc, [arrays], core_ids=[0])
    return r.results[0]["out"]
```

```python
from contextlib import ExitStack

import numpy as np

import concourse.bass as bass
from concourse import mybir

ALU = mybir.AluOpType
ACT = mybir.ActivationFunctionType
F32 = mybir.dt.float32
BF16 = mybir.dt.bfloat16
U32 = mybir.dt.uint32
F32R = mybir.dt.float32r
AX = mybir.AxisListType.X

NB, L, DM = 8, 256, 128
NH, CKV, DR, DH, CQ = 8, 32, 32, 64, 64
WIN, FAR = 64, 32
NIH = 4
RH, RD = 16, 8
NE, FF = 8, 512
TQ = 16
NT = L // TQ
T0 = WIN // TQ
SLOTS = TQ * FAR
SW = 96 + 4 * FAR
SCALE = (DH + DR) ** -0.5
EPS = 1e-5
TAKEN = -3.4e38
NS = 20
LEAD_A, LEAD_C, LEAD_D = 2, 2, 4


def constants():
    c = {}
    p = np.arange(128)
    c["ident"] = np.eye(128)
    c["key_no"] = np.stack([p, p + 128], 1)
    def cut(t, n):
        s = np.arange(n)[None, :]
        return np.where(s <= t - WIN, 3e38, np.where(s > t, -1e30 * (1 + s / 256.0), -3e38))
    c["cut_a"] = cut(64 + p[:, None], 128)
    c["cut_b"] = cut(192 + p[:64, None], 192)
    half = DR // 2
    theta = 1.0 / 10000.0 ** (2.0 * np.arange(half) / DR)
    t = p[:, None] + 128 * np.arange(2)[None, :]
    pos = np.stack([t, t + np.maximum(0, t - (WIN - 1)), t], 1)
    ang = pos[..., None] * theta
    fac = np.array([SCALE, SCALE, 1.0])[None, :, None, None]
    two = lambda a, b: np.stack([a, b], 3).reshape(128, -1)
    co, si = np.cos(ang) * fac, np.sin(ang) * fac
    c["cos2"], c["sin2"] = two(co, co), two(si, si)
    c["ssin2"], c["scos2"] = two(-si, si), two(-co, co)
    rank = WIN + np.arange(FAR)
    ar = theta[np.arange(32) % half][:, None] * rank[None, :]
    sg = np.where(np.arange(32) < half, -1.0, 1.0)[:, None]
    z = np.zeros((32, FAR))
    c["rank_a"] = np.concatenate([z, np.cos(ar), sg * np.sin(ar), z])
    c["rank_b"] = np.concatenate([z, -np.sin(ar), sg * np.cos(ar), z])
    gam = 1.0 - np.exp(np.linspace(np.log(1 / 32.0), np.log(1 / 512.0), RH))
    base = (np.arange(0, RD, 2) + 0.4 * RD) / (1.4 * RD)
    inv = 1.0 / 10000.0 ** (np.arange(RD // 2) / (RD // 2))
    scale = base[None, None, :] ** (t[..., None] / 512.0)
    an = t[..., None] * inv
    dec = gam[None, :] ** p[:, None]
    def table(f, sc, d):
        x = np.repeat(f(an) * sc, 2, axis=-1)[:, :, None, :] * d[:, None, :, None]
        return x.reshape(128, 2, 128)
    sign = np.tile([-1.0, 1.0], 64)
    for n, sc, d in (("q", scale, dec), ("k", 1 / scale, 1 / dec)):
        c["cos_" + n] = table(np.cos, sc, d).reshape(128, 256)
        c["sin_" + n] = (table(np.sin, sc, d) * sign).reshape(128, 256)
    c["causal"] = (p[None, :] >= p[:, None]) * 1.0
    hd = p // RD
    c["carry"] = (hd[:, None] == hd[None, :]) * (gam[hd] ** 128)[:, None]
    c["variant"] = ((p[:, None] % 32) // RD == np.arange(4)[None, :]) * 1.0
    c["expert_no"] = np.tile(np.arange(8.0), (128, 1))
    return c


class Sig:

    def __init__(self, sem, per, lead=0):
        self.sem, self.per, self.lead = sem, per, lead

    def at(self, n, k):
        return (n + self.lead) * self.per + k


class Own:

    def __init__(self, eng, sig):
        self.eng, self.sig, self.n, self.k = eng, sig, 0, 0

    def batch(self, s, n):
        self.n = n
        if s < 0:
            assert self.k in (0, self.sig.per), (self.sig.sem.name, self.k, self.sig.per)
            self.k = 0

    def did(self, ins):
        ins.then_inc(self.sig.sem, 1)
        self.k += 1
        return self.k

    def wait(self, k):
        self.eng.wait_ge(self.sig.sem, self.sig.at(self.n, k))


class Inst:

    def __init__(self, n, par, half):
        self.n, self.par, self.half = n, par, half
        self.first, self.last = (isinstance(n, int) and n == k for k in (0, NB - 1))


C_BY = "VAVA" + "V" * 8 + "VA"


def build(nc, io, out):
    ctx = ExitStack()
    with ctx:
        sb = lambda name, shape, dt=F32: ctx.enter_context(nc.sbuf_tensor(name, shape, dt))
        pb = lambda name: ctx.enter_context(nc.psum_tensor(name, [128, 512], F32))

        def sig(name, per, lead=0):
            return Sig(ctx.enter_context(nc.semaphore(name)), per, lead)

        con = constants()
        cat, parts = {}, []
        at = 0
        for name, a in con.items():
            full = np.zeros((128, a.shape[1]), np.float32)
            full[:a.shape[0]] = a
            parts.append(full)
            cat[name] = (at, at + a.shape[1])
            at += a.shape[1]
        con_dram = nc.inline_tensor(np.concatenate(parts, 1), name="shape_constants").ap()
        k = np.arange(TQ)
        pick = (k[:, None] == np.arange(128)[None, :] // NH).astype(np.float32)
        hide = np.zeros((TQ, 2, SW), np.float32)
        for par in range(2):
            off = 16 * par
            r = np.arange(96)[None, :]
            hide[:, par, :96] = np.where((r >= off + 1 + k[:, None]) & (r <= off + 64 + k[:, None]), 0, -1e30)
            hide[:, par, 96:] = np.where(np.arange(128)[None, :] // FAR == k[:, None] % 4, 0, -1e30)
        mask_dram = nc.inline_tensor(np.concatenate([pick, hide.reshape(TQ, -1)], 1), name="mask_constants").ap()
        slots_dram = nc.dram_tensor("far_slots", [2, (L - WIN) * FAR], BF16, kind="Internal").ap()

        cst = sb("cst", [128, at])
        C = lambda name, rows=128: cst[0:rows, cat[name][0]:cat[name][1]]
        mbf = sb("mbf", [TQ, 128 + 2 * SW], BF16)
        pick_w = mbf[:, 0:128]
        hide_m = mbf[:, 128:128 + 2 * SW].rearrange("k (a c) -> k a c", a=2)
        wkv = sb("wkv", [128, 64])
        wdq, wdqT = sb("wdq", [128, CQ]), sb("wdqT", [CQ, 128])
        hs = sb("hs", [128, 2, 4, L])
        early_w = hs[:, :, :, :].rearrange("p a f t -> p (a f t)")
        wuq, wuk, wuv = early_w[0:CQ, 0:512], early_w[0:CKV, 512:1024], early_w[0:CKV, 1024:1536]
        wuqT = sb("wuqT", [128, 4, CQ])
        wukvT = sb("wukvT", [128, 8, CKV])
        wqr = sb("wqr", [CQ, 256])
        wout = sb("wout", [128, 4, DM])
        iwq, iwk = sb("iwq", [128, 256]), sb("iwk", [128, 128])
        idxw = sb("idxw", [128, NIH])
        gate, gateT = sb("gate", [NE, DM]), sb("gateT", [DM, NE])
        b1, b1T, b2 = sb("b1", [32, 128]), sb("b1T", [128, 32]), sb("b2", [NE, DM])
        absq = sb("absq", [CQ, 256])
        wq_all = sb("wq_all", [128, 512])
        wvo = sb("wvo", [64, 4, DM])
        dl = sb("dl", [128, 6, 17])
        rot_c, rot_s = sb("rot_c", [128, 3, 2, 32]), sb("rot_s", [128, 3, 2, 32])
        rot_t = sb("rot_t", [128, 192])
        rank_t = sb("rank_t", [96, FAR])
        rank_u = sb("rank_u", [96, FAR])
        xn = sb("xn", [128, 2, 2, DM])
        xT = sb("xT", [128, L])
        qiT = sb("qiT", [128, 2, 192])
        kiT = sb("kiT", [128, 192])
        ra, rb = sb("ra", [128, NIH, 128]), sb("rb", [64, NIH, 192])
        sa, sbb = sb("sa", [128, 128]), sb("sbb", [64, 192])
        va, vb = sb("va", [128, FAR]), sb("vb", [64, FAR])
        ia, ib = sb("ia", [128, FAR], U32), sb("ib", [64, FAR], U32)
        ja, jb = sb("ja", [128, FAR], BF16), sb("jb", [64, FAR], BF16)
        qn = sb("qn", [128, 2, NH, 128])
        pa, pr, pe_ = sb("pa", [128, 2, 256]), sb("pr", [128, 2, 256]), sb("pe_", [128, 2, 256])
        nq = sb("nq", [128, 2, 256])
        g1, g2 = sb("g1", [128, 2, 256]), sb("g2", [128, 2, 256])
        ka, kr = sb("ka", [128, 2, 32]), sb("kr", [128, 2, 32])
        kg1, kg2 = sb("kg1", [128, 2, 32]), sb("kg2", [128, 2, 32])
        ktab = sb("ktab", [128, 2, 96])
        kdn = sb("kdn", [128, 2, 128])
        kspl = sb("kspl", [128, 2, 2, 192], F32R)
        ktop = sb("ktop", [128, 192])
        high = sb("high", [128, 1], U32)
        ckw = sb("ckw", [96, 2, 6, CKV])
        kd = sb("kd", [128, 2, L])
        qall = sb("qall", [128, 2, L * NH])
        sidx = sb("sidx", [128, (L - WIN) * FAR], BF16)
        oh = sb("oh", [128, 2, 2, 2 * SLOTS], F32R)
        gs = sb("gs", [96, 2, SLOTS])
        nmx, lsum, rls = sb("nmx", [128, 2]), sb("lsum", [128, 2]), sb("rls", [128, 2])
        pp = sb("pp", [128, 2, SW])
        ppn = sb("ppn", [128, 2, SW])
        pts = sb("pts", [128, 256])
        vgs = sb("vgs", [128, 2, 128])
        ots = sb("ots", [64, 4, L])
        xr, cn = sb("xr", [128, 2, 2, DM]), sb("cn", [128, 2, 2, DM])
        y1, x1, y2, x2 = (sb(n, [128, 2, DM]) for n in ("y1", "x1", "y2", "x2"))
        bst, mv = sb("bst", [128, 2, 6]), sb("mv", [128, 2, 2])
        lnv = sb("lnv", [128, 6, 2])
        rq1, rq2, rqn = (sb(n, [128, 2, DM]) for n in ("rq1", "rq2", "rqn"))
        rk1, rk2, rkn = (sb(n, [128, 2, DM]) for n in ("rk1", "rk2", "rkn"))
        kT4 = sb("kT4", [128, 4, L])
        qT = sb("qT", [128, L])
        st = sb("st", [128, 128])
        sm = sb("sm", [128, 4, 512])
        cnm = sb("cnm", [128, 2, 4, DM])
        rT = sb("rT", [128, L])
        mraw = sm[0:TQ, :, :].rearrange("p a c -> p (a c)")[:, 0:128 + 2 * SW]
        lg, ex, pr8 = (sb(n, [128, 2, NE]) for n in ("lg", "ex", "pr8"))
        mx2 = sb("mx2", [128, 3, 2])
        v8, i8, f8 = sb("v8", [128, 2, 8]), sb("i8", [128, 2, 8], U32), sb("f8", [128, 2, 8])
        h1, h2 = sb("h1", [128, 2, NE]), sb("h2", [128, 2, NE])
        gTs = sb("gTs", [NE, L])
        x2T = sb("x2T", [128, 2, L])
        acc = sb("acc", [128, 2, 2, DM])
        gg = sb("gg", [128, 2, NE])
        w1s, w2s = sb("w1s", [128, NE, FF]), sb("w2s", [128, NE, 4, DM])
        fst, fmv, fln = sb("fst", [128, 2, 6]), sb("fmv", [128, 2, 2]), sb("fln", [128, 6, 2])

        bG, bS = pb("bG"), pb("bS")
        bM = pb("bM")
        TURNED, LATENT, WEIGHED = 0, 256, 384
        bW = [pb("bW0"), pb("bW1")]
        bC = pb("bC")
        bH = pb("bH")
        bR = pb("bR")

        d_early, d_late = sig("d_early", 0), sig("d_late", 0)
        d_x = [sig(f"d_x{i}", 16) for i in range(2)]
        d_cx = [sig(f"d_cx{i}", 32) for i in range(2)]
        d_put = [sig(f"d_put{i}", 32, 1) for i in range(2)]
        d_idx = [sig(f"d_idx{i}", 16) for i in range(2)]
        d_experts = sig("d_experts", 0)
        d_out = [sig(f"d_out{i}", 16, 1) for i in range(2)]
        w_full, w_free = sig("w_full", 7), sig("w_free", 7)
        s_prep = sig("s_prep", 14)
        s_mb, s_rot, s_sin, s_dl = (sig(n, 1) for n in ("s_mb", "s_rot", "s_sin", "s_dl"))
        s_zero = sig("s_zero", 1)
        s_pass = sig("s_pass", 0)
        a_full = sig("a_full", 15, 2)
        a_free = sig("a_free", 15, 2)
        own_aa = sig("own_aa", 6, 1)
        a_soft = sig("a_soft", 3, 1)
        own_va = sig("own_va", 10, 1)
        top_a, top_b = sig("top_a", 11, 1), sig("top_b", 11, 1)
        a_slot = sig("a_slot", 2, 1)
        own_ga = sig("own_ga", 24, 1)
        g_kv, g_q = sig("g_kv", 1, 1), sig("g_q", 2, 1)
        g_spl = sig("g_spl", 3, 1)
        o_ready = sig("o_ready", 6, 2)
        g_full = sig("g_full", 12, 2)
        g_out = sig("g_out", 12, 1)
        s_full = sig("s_full", 16, 1)
        s_max = sig("s_max", 16, 1)
        s_exp = sig("s_exp", 16, 1)
        s_rec = sig("s_rec", 16, 1)
        s_nrm = sig("s_nrm", 16, 1)
        m_full = sig("m_full", 17, 2)
        m_out = sig("m_out", 17, 1)
        c_full = sig("c_full", 14, 2)
        c_freeA = sig("c_freeA", C_BY.count("A"), 1)
        c_freeV = sig("c_freeV", C_BY.count("V"), 1)
        r_k, r_q = sig("r_k", 1, 1), sig("r_q", 1, 1)
        ln_st, ln_rs = sig("ln_st", 2, 1), sig("ln_rs", 2, 1)
        own_vc = sig("own_vc", 18, 1)
        own_ac = sig("own_ac", 2, 1)
        own_gc = sig("own_gc", 4, 1)
        r_v = sig("r_v", 4, 1)
        c_x1, c_x2 = sig("c_x1", 1, 1), sig("c_x2", 1, 1)
        c_av = sig("c_av", 2, 2)
        c_ret = sig("c_ret", 2, 1)
        r_full = sig("r_full", 3, 1)
        r_lg, r_ex, r_gg, r_gt = (sig(n, 1, 1) for n in ("r_lg", "r_ex", "r_gg", "r_gt"))
        r_acc = sig("r_acc", 1, 2)
        e_full = sig("e_full", 16, 2)
        e_relu = sig("e_relu", 16, 1)
        e_y = sig("e_y", 16, 1)
        e_acc = sig("e_acc", 16, 1)
        own_vd, own_vf, own_ad = sig("own_vd", 13, 1), sig("own_vf", 9, 1), sig("own_ad", 1, 1)
        f_st, f_rs, f_ln = (sig(n, 1, 1) for n in ("f_st", "f_rs", "f_ln"))

        def program(stage_a, stage_b, stage_c, stage_d, fori):

            def step(batch):
                for s in range(NS):
                    def run(f, at_, k, lead):
                        for own, i in ((at_ + lead, batch(k)), (at_ + lead - NS, batch(k + 1))):
                            if i is not None and own >= 0:
                                if own == 0:
                                    f(-1, i)
                                f(own, i)

                    run(stage_a, s, 1, LEAD_A)
                    run(stage_c, s, -1, LEAD_C)
                    run(stage_b, s, 0, 0)
                    run(stage_d, s, -2, LEAD_D)
                    run(stage_b, s + 0.25, 0, 0)
                    run(stage_a, s + 0.5, 1, LEAD_A)
                    run(stage_c, s + 0.5, -1, LEAD_C)
                    run(stage_d, s + 0.5, -2, LEAD_D)

            def plain(s):
                step(lambda k: Inst(s + k, (s + k) % 2, (s + k) // 2) if 0 <= s + k < NB else None)

            for s in (-2, -1, 0, 1):
                plain(s)
            with fori(0, NB // 2 - 2) as i:
                for s in (2, 3):
                    step(lambda k: Inst(2 * i + s + k, (s + k) % 2, i + (s + k) // 2))
            for s in (NB - 2, NB - 1, NB, NB + 1):
                plain(s)

        block = ctx.enter_context(nc.Block())

        @block.sync
        def _(sp):
            for s_ in d_put + d_out:
                sp.sem_inc(s_.sem, s_.per * s_.lead)
            early = 0
            for dst, src in (
                (cst[:, :], con_dram), (wuq[:, :], io["W_uq"]), (wuk[:, :], io["W_uk"]),
                (wuv[:, :], io["W_uv"]), (wdq[:, :], io["W_dq"]), (gate[:, :], io["gate_w"]),
                (b1[:, :], io["b1"].rearrange("e (f p) -> (e f) p", p=128)),
                (mraw[:, :], mask_dram),
                (dl[:, 0, 0:16], io["raw_delta"].rearrange("(o n) -> o n", o=1).broadcast_to([128, 16])),
            ):
                sp.dma_start(dst, src).then_inc(d_early.sem, 16)
                early += 16
            for r in range(8):
                sp.dma_start(dl[16 * r:16 * r + 16, 0, 16:17],
                             io["raw_delta"].rearrange("(n o) -> n o", o=1)).then_inc(d_early.sem, 16)
                early += 16
            assert early == EARLY
            late = 0
            for dst, src in (
                (wqr[:, :], io["W_qr"]), (wout[:, :, :], io["W_out"].rearrange("(c p) n -> p c n", p=128)),
                (iwq[:, :], io["idx_wq"]), (iwk[:, 0:64], io["idx_wk"]), (iwk[:, 64:128], io["idx_wk"]),
                (idxw[:, :], io["idx_w"].rearrange("(o n) -> o n", o=1).broadcast_to([128, NIH])),
                (wkv[:, 0:32], io["W_dkv"]), (wkv[:, 32:64], io["W_kr"]), (b2[:, :], io["b2"]),
            ):
                sp.dma_start(dst, src).then_inc(d_late.sem, 16)
                late += 16
            assert late == LATE

            def stage_a(s, i):
                if s < 0 and i.first:
                    sp.dma_start(xn[:, 0, :, :], io["x"][0].rearrange("(t p) d -> p t d", p=128)).then_inc(d_x[0].sem, 16)
                if s == 2 and not i.last:
                    q = 1 - i.par
                    sp.wait_ge(a_full.sem, a_full.at(i.n - 1, 1))
                    sp.dma_start(xn[:, q, :, :], io["x"][i.n + 1].rearrange("(t p) d -> p t d", p=128)).then_inc(d_x[q].sem, 16)
                if s == 13:
                    row = slots_dram[i.par]
                    put = row[0:128 * FAR].rearrange("(p j) -> p j", j=FAR)
                    sp.wait_ge(a_slot.sem, a_slot.at(i.n, 2))
                    sp.dma_start(put, ja[:, :]).then_inc(d_put[i.par].sem, 16)
                    put = row[128 * FAR:].rearrange("(p j) -> p j", j=FAR)
                    sp.dma_start(put, jb[:, :]).then_inc(d_put[i.par].sem, 16)
                    sp.wait_ge(d_put[i.par].sem, d_put[i.par].at(i.half, 32))
                    sp.wait_ge(o_ready.sem, o_ready.at(i.n - 1, 6))
                    sp.dma_start(sidx[:, :], row.rearrange("(o n) -> o n", o=1).broadcast_to([128, (L - WIN) * FAR])).then_inc(d_idx[i.par].sem, 16)

            def stage_b(s, i):
                if s == 0 and i.first:
                    for q in range(4):
                        e = slice(2 * q, 2 * q + 2)
                        sp.dma_start(w1s[:, e, :], io["w1"][e].rearrange("e p f -> p e f")).then_inc(d_experts.sem, 16)
                        for h in (2 * q, 2 * q + 1):
                            sp.dma_start(w2s[:, h, :, :],
                                         io["w2"][h].rearrange("(f p) n -> p f n", p=128)).then_inc(d_experts.sem, 16)
                if s == 2:
                    sp.wait_ge(c_av.sem, c_av.at(i.n - 2, 2))
                    sp.dma_start(xr[:, i.par, :, :], io["x"][i.n].rearrange("(t p) d -> p t d", p=128)).then_inc(d_cx[i.par].sem, 16)
                    sp.dma_start(cn[:, i.par, :, :], io["ctx"][i.n].rearrange("(t p) d -> p t d", p=128)).then_inc(d_cx[i.par].sem, 16)

            def stage_c(s, i):
                pass

            def stage_d(s, i):
                if s == 21:
                    sp.wait_ge(f_ln.sem, f_ln.at(i.n, 1))
                    sp.dma_start(out[i.n].rearrange("(t p) d -> p t d", p=128), acc[:, i.par, :, :]).then_inc(d_out[i.par].sem, 16)

            program(stage_a, stage_b, stage_c, stage_d, sp.Fori)
            for s_ in d_out:
                sp.wait_ge(s_.sem, s_.at(NB // 2 - 1, 16))

        @block.gpsimd
        def _(pool):
            for s_ in (own_ga, g_kv, g_q, own_gc, r_k, r_q, r_v):
                pool.sem_inc(s_.sem, s_.per * s_.lead)
            nc.gpsimd.memset(kdn[:, :, 32:96], 0.0).then_inc(s_zero.sem, 1)
            nc.gpsimd.memset(cnm[:, :, :, :], 0.0).then_inc(s_zero.sem, 1)
            nc.gpsimd.memset(high[:, :], 0xFFFFF000).then_inc(s_zero.sem, 1)
            pool.wait_ge(s_zero.sem, 3)
            pool.wait_ge(s_rot.sem, 2)
            TT = nc.gpsimd.tensor_tensor
            oa = Own(pool, own_ga)
            oc = Own(pool, own_gc)
            hv = lambda ap: ap.rearrange("p (h a d) -> p h a d", a=2, d=16)

            def stage_a(s, i):
                oa.batch(s, i.n)
                if s == 6:
                    pool.wait_ge(a_soft.sem, a_soft.at(i.n, 3))
                    pool.wait_ge(a_full.sem, a_full.at(i.n - 1, 11))
                    pool.wait_ge(g_spl.sem, g_spl.at(i.n - 1, 3))
                    a = oa.did(TT(ktab[:, :, 32:64], kr[:, :, :], ka[:, :, :], ALU.add))
                    b = oa.did(TT(ktab[:, :, 64:80], kr[:, :, 16:32], ka[:, :, 16:32], ALU.add))
                    b = oa.did(TT(ktab[:, :, 80:96], kr[:, :, 0:16], ka[:, :, 0:16], ALU.add))
                    c = oa.did(nc.gpsimd.tensor_copy(kdn[:, :, 0:32], ktab[:, :, 0:32]))
                    oa.wait(b)
                    d = oa.did(TT(kg1[:, :, :], ktab[:, :, 32:64], rot_c[:, 2, :, :], ALU.mult))
                    e = oa.did(TT(kg2[:, :, :], ktab[:, :, 64:96], rot_s[:, 2, :, :], ALU.mult))
                    oa.wait(e)
                    TT(kdn[:, :, 96:128], kg1[:, :, :], kg2[:, :, :], ALU.add).then_inc(g_kv.sem, 1)
                if s in (5, 7):
                    t = (s - 5) // 2
                    pool.wait_ge(a_soft.sem, a_soft.at(i.n, t + 1))
                    pool.wait_ge(a_full.sem, a_full.at(i.n, 0))
                    a = oa.did(TT(nq[:, t, :], pr[:, t, :], pe_[:, t, :], ALU.add))
                    oa.wait(a)
                    n4 = hv(nq[:, t, :])
                    for kind in range(2):
                        c4 = hv(rot_c[:, kind, t, :]).broadcast_to([128, NH, 2, 16])
                        s4 = hv(rot_s[:, kind, t, :]).broadcast_to([128, NH, 2, 16])
                        a = oa.did(TT(hv(g1[:, kind, :]), n4, c4, ALU.mult))
                        for h in range(2):
                            b = oa.did(TT(hv(g2[:, kind, :])[:, :, h, :], n4[:, :, 1 - h, :], s4[:, :, h, :], ALU.mult))
                        oa.wait(b)
                        u, v = (g[:, kind, :].rearrange("p (h d) -> p h d", d=32) for g in (g1, g2))
                        if kind == 0:
                            oa.did(TT(qn[:, t, :, 32:64], u, v, ALU.add))
                            oa.did(TT(qn[:, t, :, 64:96], u, v, ALU.add))
                        else:
                            oa.wait(oa.k)
                            TT(qn[:, t, :, 96:128], u, v, ALU.add).then_inc(g_q.sem, 1)

            def stage_b(s, i):
                pass

            def rotate(dst, src, cos, sin, t1, t2, done):
                cs, sn = (C(n).rearrange("p (t c) -> p t c", t=2) for n in (cos, sin))
                pairs = lambda ap: ap.rearrange("p t (c e) -> p t c e", e=2)
                oc.did(TT(t1[:, :, :], src, cs, ALU.mult))
                oc_last = None
                TT(pairs(t2[:, :, :])[:, :, :, 0], pairs(src)[:, :, :, 1], pairs(sn)[:, :, :, 0], ALU.mult)
                oc_last = oc.did(TT(pairs(t2[:, :, :])[:, :, :, 1], pairs(src)[:, :, :, 0], pairs(sn)[:, :, :, 1], ALU.mult))
                oc.wait(oc_last)
                TT(dst, t1[:, :, :], t2[:, :, :], ALU.add).then_inc(done.sem, 1)

            def stage_c(s, i):
                oc.batch(s, i.n)
                if s == 0:
                    pool.wait_ge(d_cx[i.par].sem, d_cx[i.par].at(i.half, 32))
                    pool.wait_ge(c_full.sem, c_full.at(i.n - 1, 3))
                    rotate(rkn[:, :, :], cn[:, i.par, :, :], "cos_k", "sin_k", rk1, rk2, r_k)
                    pool.wait_ge(c_av.sem, c_av.at(i.n - 1, 2))
                    pool.sem_inc(s_pass.sem, 1)
                    heads = lambda ap: ap.rearrange("p t (g v e) -> p t g v e", v=4, e=RD)
                    for v in range(4):
                        nc.gpsimd.tensor_copy(heads(cnm[:, :, v, :])[:, :, :, v, :],
                                              heads(cn[:, i.par, :, :])[:, :, :, v, :]).then_inc(r_v.sem, 1)
                if s == 3:
                    pool.wait_ge(c_x1.sem, c_x1.at(i.n, 1))
                    rotate(rqn[:, :, :], x1[:, :, :], "cos_q", "sin_q", rq1, rq2, r_q)

            def stage_d(s, i):
                pass

            program(stage_a, stage_b, stage_c, stage_d, pool.Fori)
            assert (oa.k, oc.k) == (own_ga.per, own_gc.per), ("own_ga", oa.k, own_ga.per)

        @block.tensor
        def _(pe):
            for s_ in (a_full, g_full, s_full, m_full, c_full, c_av, r_full, e_full, e_y):
                pe.sem_inc(s_.sem, s_.per * s_.lead)
            MM = nc.tensor.matmul
            ident = C("ident")

            def flip(dst, src, n, lo=0):
                return MM(dst, src, ident[lo:lo + n, lo:lo + n], is_transpose=True, start=True, stop=True)

            pe.wait_ge(d_early.sem, EARLY)
            for c in range(4):
                last = flip(bG[:, 64 * c:64 * c + 64], wuq[:, 128 * c:128 * c + 128], CQ)
            last.then_inc(w_full.sem, 1)
            for j, w in enumerate((wuk, wuv)):
                for c in range(4):
                    last = flip(bR[:, 32 * (4 * j + c):32 * (4 * j + c) + 32], w[:, 128 * c:128 * c + 128], CKV)
            last.then_inc(w_full.sem, 1)
            flip(bS[0:CQ, 0:128], wdq[:, :], 128)
            flip(bS[:, 128:136], gate[:, :], NE)
            flip(bS[:, 136:168], b1[:, :], 32).then_inc(w_full.sem, 1)
            pe.wait_ge(w_free.sem, 3)
            for h in range(NH):
                lo = 64 * (h % 2)
                last = MM((bM, bC)[h % 2][0:CQ, 32 * (h // 2):32 * (h // 2) + 32], wuqT[lo:lo + 64, h // 2, :], wukvT[lo:lo + 64, h // 2, :],
                          start=True, stop=True)
            last.then_inc(w_full.sem, 1)
            pe.wait_ge(d_late.sem, LATE)
            for j in range(2):
                for h in range(j, NH, 2):
                    lo, r = 64 * j, 32 * j
                    last = MM(bW[j][r:r + CKV, 128 * (h // 2):128 * (h // 2) + 128], wukvT[lo:lo + 64, 4 + h // 2, :],
                              wout[lo:lo + 64, h // 2, :], start=True, stop=True)
                last.then_inc(w_full.sem, 1)
            pe.wait_ge(w_free.sem, 4)
            MM(bG[:, 0:256], wdqT[:, :], absq[:, :], start=True, stop=True)
            MM(bG[:, 256:512], wdqT[:, :], wqr[:, :], start=True, stop=True).then_inc(w_full.sem, 1)
            pe.wait_ge(w_free.sem, 7)
            pe.wait_ge(s_mb.sem, 1)

            def stage_a(s, i):
                p = i.par

                def bank(u):
                    if u >= 2:
                        pe.wait_ge(a_free.sem, a_free.at(i.n, u - 1))
                    else:
                        pe.wait_ge(a_free.sem, a_free.at(i.n - 1, 14 + u))
                    return bW[(u + p) % 2]

                full = lambda ins: ins.then_inc(a_full.sem, 1)
                if s == 0:
                    w = bank(0)
                    pe.wait_ge(d_x[p].sem, d_x[p].at(i.half, 16))
                    pe.wait_ge(w_free.sem, 7)
                    for t in range(2):
                        last = flip(w[:, 128 * t:128 * t + 128], xn[:, p, t, :], 128)
                    full(last)
                if s == 1:
                    w = bank(1)
                    pe.wait_ge(a_free.sem, a_free.at(i.n, 1))
                    for c in range(2):
                        last = MM(w[:, 192 * c:192 * c + 192], iwq[:, 128 * c:128 * c + 128], xT[:, 64:256],
                                  start=True, stop=True)
                    full(last)
                if s == 1.5:
                    w = bank(2)
                    full(MM(w[:, 0:192], iwk[:, :], xT[:, 0:192], start=True, stop=True))
                if s in (2, 3):
                    w = bank(s + 1)
                    lo = 64 * (s - 2)
                    pe.wait_ge(a_free.sem, a_free.at(i.n, 3))
                    for c in range(2):
                        last = MM(w[:, 128 * c:128 * c + 128], qiT[lo:lo + 64, c, 0:128], kiT[lo:lo + 64, 0:128],
                                  start=True, stop=True)
                    full(last)
                if s in (3.5, 4.5):
                    w = bank(int(s) + 2)
                    lo = 64 * (int(s) - 3)
                    pe.sem_inc(s_pass.sem, 1)
                    for c in range(2):
                        last = MM(w[0:64, 192 * c:192 * c + 192], qiT[lo:lo + 64, c, 128:192], kiT[lo:lo + 64, :],
                                  start=True, stop=True)
                    full(last)
                if s in (5, 5.5):
                    for t in [int(2 * s) - 10]:
                        w = bank(7 + t)
                        full(MM(w[:, :], xT[:, 128 * t:128 * t + 128], wq_all[:, :], start=True, stop=True))
                if s == 6:
                    w = bank(9)
                    for t in range(2):
                        MM(w[:, 64 * t:64 * t + 64], xT[:, 128 * t:128 * t + 128], wkv[:, :], start=True, stop=True)
                    for c in range(6):
                        last = MM(w[0:96, 128 + 32 * c:160 + 32 * c], xT[:, 32 * c:32 * c + 96], wkv[:, 0:32],
                                  start=True, stop=True)
                    full(last)
                if s == 9:
                    w = bank(10)
                    pe.wait_ge(g_kv.sem, g_kv.at(i.n, 1))
                    for t in range(2):
                        last = flip(w[:, 128 * t:128 * t + 128], kdn[:, t, :], 128)
                    full(last)
                if s in (12, 12.5, 14, 14.5):
                    t = (int(s) - 12) // 2
                    pe.wait_ge(g_q.sem, g_q.at(i.n, t + 1))
                    for hg in [int(2 * s) % 2]:
                        w = bank(11 + 2 * t + hg)
                        for h in range(4):
                            last = flip(w[:, 128 * h:128 * h + 128], qn[:, t, 4 * hg + h, :], 128)
                        full(last)

            def gather(i, tile):
                p, g = i.par, tile - T0
                if tile % 2 == 0:
                    pe.wait_ge(o_ready.sem, o_ready.at(i.n, g // 2 + 1))
                if g == 0:
                    pe.wait_ge(g_spl.sem, g_spl.at(i.n, 3))
                pe.wait_ge(g_out.sem, g_out.at(i.n, g))
                w = bG
                kts = [0] if tile < 12 else [0, 1]
                n = 0
                for kt in kts:
                    rows = 128 if kt == 0 else 64
                    for part in range(2):
                        last = MM(w[0:96, :], kspl[0:rows, p, part, 96 * kt:96 * kt + 96],
                                  oh[0:rows, (g // 2) % 2, kt, SLOTS * (tile % 2):SLOTS * (tile % 2) + SLOTS],
                                  start=(n == 0), stop=(n == 2 * len(kts) - 1))
                        n += 1
                last.then_inc(g_full.sem, 1)

            def scores(i, tile):
                p, g = i.par, tile - T0
                pe.wait_ge(s_exp.sem, s_exp.at(i.n, tile))
                o = 0
                q = qall[:, p, 128 * tile:128 * tile + 128]
                if tile < T0:
                    MM(bS[:, o:o + 96], q, kd[:, p, 0:96], start=True, stop=True).then_inc(s_full.sem, 1)
                    return
                MM(bS[:, o:o + SW], pick_w, hide_m[:, tile % 2, :], start=True, stop=True,
                   skip_group_check=True)
                k0 = 32 * ((tile - T0) // 2)
                MM(bS[:, o:o + 96], q, kd[:, p, k0:k0 + 96], start=False, stop=True, skip_group_check=True)
                pe.wait_ge(g_out.sem, g_out.at(i.n, g + 1))
                for c in range(4):
                    last = MM(bS[32 * c:32 * c + 32, o + 96:o + SW], qall[0:96, p, 128 * tile + 32 * c:128 * tile + 32 * c + 32],
                              gs[:, g % 2, 128 * c:128 * c + 128], start=False, stop=True, skip_group_check=True)
                last.then_inc(s_full.sem, 1)

            def far_latents(i, tile):
                g = tile - T0
                for c in range(4):
                    o = LATENT + 32 * c
                    flip(bM[:, o:o + 32], gs[0:32, g % 2, 128 * c:128 * c + 128], 32)

            def turn(i, tile):
                pe.wait_ge(s_nrm.sem, s_nrm.at(i.n, tile + 1))
                w = ppn[:, tile % 2, :]
                if tile < T0:
                    return flip(bM[0:96, 0:128], w[:, 0:96], 128)
                flip(bM[:, 0:128], w[:, 0:128], 128)
                return flip(bM[:, 128:256], w[:, 96:SW], 128)

            def weigh(i, tile):
                g, p = tile - T0, i.par
                near = ckw[:, p, 0 if g < 0 else g // 2, :]
                for j in range(2):
                    last = MM(bM[32 * j:32 * j + 32, WEIGHED:WEIGHED + 64], near,
                              pts[0:96, 0:128].rearrange("p (q a b) -> p b a q", a=4, b=2)[:, j, :, :],
                              start=True, stop=True, skip_group_check=True)
                for c in range(4) if g >= 0 else ():
                    for j in range(2):
                        last = MM(bM[32 * j:32 * j + 32, WEIGHED:WEIGHED + 64].rearrange("p (a q) -> p a q", a=4)[:, :, 4 * c:4 * c + 4],
                                  vgs[:, g % 2, 32 * c:32 * c + 32],
                                  pts[:, 128 + 32 * c:160 + 32 * c].rearrange("p (q a b) -> p b a q", a=4, b=2)[:, j, :, :],
                                  start=False, stop=True, skip_group_check=True)
                return last

            def stage_b(s, i):
                if s < 0:
                    return
                if s == 0:
                    pe.wait_ge(a_free.sem, a_free.at(i.n, 15))
                if s == int(s):
                    if s < NT:
                        scores(i, s)
                    if T0 <= s + 1 < NT:
                        gather(i, s + 1)
                    return
                s = int(s)
                if 1 <= s <= NT + 1:
                    pe.wait_ge(m_out.sem, m_out.at(i.n, s - 1))
                    pe.sem_inc(s_pass.sem, 1)
                    if 2 <= s:
                        last = weigh(i, s - 2)
                    if T0 <= s < NT:
                        far_latents(i, s)
                    if s <= NT:
                        last = turn(i, s - 1)
                    last.then_inc(m_full.sem, 1)

            def stage_c(s, i):
                p = i.par

                def emptied(u, n=i.n):
                    f = c_freeA if C_BY[u] == "A" else c_freeV
                    pe.wait_ge(f.sem, f.at(n, C_BY[:u + 1].count(C_BY[u])))

                def half(u):
                    if u >= 1:
                        emptied(u - 1)
                    else:
                        emptied(13, i.n - 1)
                    return bC

                full = lambda ins: ins.then_inc(c_full.sem, 1)
                if s == 0:
                    w = half(0)
                    pe.wait_ge(m_out.sem, m_out.at(i.n, 17))
                    for t in range(2):
                        for h in range(4):
                            last = MM(w[:, 128 * t:128 * t + 128], ots[:, h, 128 * t:128 * t + 128], wvo[:, h, :],
                                      start=(h == 0), stop=(h == 3))
                    full(last)
                if s == 2:
                    w = half(1)
                    pe.wait_ge(r_k.sem, r_k.at(i.n, 1))
                    for t in range(2):
                        last = flip(w[:, 128 * t:128 * t + 128], rkn[:, t, :], 128)
                    full(last)
                if s == 2.5:
                    w = half(2)
                    full(MM(w[:, 0:128], rkn[:, 0, :], cn[:, p, 0, :], start=True, stop=True))
                if s == 4:
                    w = half(3)
                    pe.wait_ge(r_q.sem, r_q.at(i.n, 1))
                    for t in range(2):
                        last = flip(w[:, 128 * t:128 * t + 128], rqn[:, t, :], 128)
                    full(last)
                if s in (9, 13):
                    t = (s - 9) // 4
                    emptied(4 * t + 7)
                    pe.wait_ge(r_v.sem, r_v.at(i.n, 4))
                    pe.wait_ge(e_acc.sem, e_acc.at(i.n - 1, s - 4 + LEAD_D - LEAD_C))
                    o = 256 + 128 * t
                    if t == 1:
                        MM(bR[:, o:o + 128], st[:, :], qT[:, 128:256], start=True, stop=True, skip_group_check=True)
                    for v in range(4):
                        for g in range(4):
                            last = MM(bR[32 * g:32 * g + 32, o:o + 128], cnm[:, t, v, 32 * g:32 * g + 32],
                                      sm[:, g, 128 * v:128 * v + 128], start=(t == 0 and v == 0), stop=True,
                                      skip_group_check=True)
                    last.then_inc(c_av.sem, 1)
                if s in range(5, 13):
                    u = s - 5
                    t, g = u // 4, u % 4
                    w = half(4 + u)
                    for v in range(4):
                        last = MM(w[:, 128 * v:128 * v + 128], kT4[32 * g:32 * g + 32, v, 128 * t:128 * t + 128],
                                  qT[32 * g:32 * g + 32, 128 * t:128 * t + 128], start=True, stop=True)
                    full(last)
                if s == 14:
                    w = half(12)
                    pe.wait_ge(c_ret.sem, c_ret.at(i.n, 2))
                    for t in range(2):
                        last = flip(w[:, 128 * t:128 * t + 128], rT[:, 128 * t:128 * t + 128], 128)
                    full(last)
                if s == 17:
                    w = half(13)
                    pe.wait_ge(c_x2.sem, c_x2.at(i.n, 1))
                    for t in range(2):
                        last = flip(w[:, 128 * t:128 * t + 128], x2[:, t, :], 128)
                    full(last)
            def stage_d(s, i):
                p = i.par
                if s == 0:
                    if i.first:
                        pe.wait_ge(d_experts.sem, EXPERTS)
                    pe.wait_ge(c_freeA.sem, c_freeA.at(i.n, C_BY.count("A")))
                    pe.wait_ge(e_acc.sem, e_acc.at(i.n - 1, 16))
                    for t in range(2):
                        last = MM(bR[:, 8 * t:8 * t + 8], x2T[:, p, 128 * t:128 * t + 128], gateT[:, :], start=True, stop=True)
                    last.then_inc(r_full.sem, 1)
                if s == 2:
                    pe.wait_ge(r_gg.sem, r_gg.at(i.n, 1))
                    for t in range(2):
                        last = flip(bR[0:NE, 128 * t:128 * t + 128], gg[:, t, :], 128)
                    last.then_inc(r_full.sem, 1)
                if s == 3:
                    pe.wait_ge(r_gt.sem, r_gt.at(i.n, 1))
                    for t in range(2):
                        last = MM(bR[:, 128 * t:128 * t + 128], gTs[:, 128 * t:128 * t + 128], b2[:, :], start=True, stop=True)
                    last.then_inc(r_full.sem, 1)
                if s in range(4, 2 * NE + 4):
                    e, t = (s - 4) // 2, s % 2
                    pe.wait_ge(e_relu.sem, e_relu.at(i.n, 2 * e + 2))
                    if s == 4:
                        pe.wait_ge(r_acc.sem, r_acc.at(i.n, 1))
                    else:
                        pe.wait_ge(e_acc.sem, e_acc.at(i.n, s - 4))
                    if s - LEAD_D + LEAD_C in (9, 13) and not i.last:
                        pe.wait_ge(c_ret.sem, c_ret.at(i.n + 1, (s - LEAD_D + LEAD_C) // 4 - 1))
                    for f in range(4):
                        last = MM(bR[:, 128 * t:128 * t + 128], hs[:, e % 2, f, 128 * t:128 * t + 128], w2s[:, e, f, :],
                                  start=(f == 0), stop=(f == 3))
                    last.then_inc(e_y.sem, 1)
                if s in range(1, 2 * NE + 1):
                    e, half = (s - 1) // 2, (s - 1) % 2
                    pe.wait_ge(e_relu.sem, e_relu.at(i.n, s - 1))
                    for f in (2 * half, 2 * half + 1):
                        last = MM(bH[:, 256 * (f % 2):256 * (f % 2) + 256], w1s[:, e, 128 * f:128 * f + 128], x2T[:, p, :],
                                  start=True, stop=True)
                    last.then_inc(e_full.sem, 1)

            program(stage_a, stage_b, stage_c, stage_d, pe.Fori)

        @block.scalar
        def _(act):
            for s_ in (a_free, a_soft, own_aa, s_exp, m_out, c_freeA, c_ret, ln_rs, own_ac, r_ex, r_gt, e_relu, own_ad, f_rs):
                act.sem_inc(s_.sem, s_.per * s_.lead)
            AC = nc.scalar.activation
            copy = nc.scalar.copy
            act.wait_ge(d_early.sem, EARLY)
            AC(dl[:, 1, :], dl[:, 0, :], ACT.Exp, scale=-1.0).then_inc(s_sin.sem, 1)
            act.wait_ge(s_dl.sem, 1)
            AC(dl[:, 4, :], dl[:, 2, :], ACT.Sin).then_inc(s_sin.sem, 1)
            AC(dl[:, 5, :], dl[:, 3, :], ACT.Sin).then_inc(s_sin.sem, 1)

            def empty(k, pairs):
                act.wait_ge(w_full.sem, k)
                for dst, src in pairs:
                    last = copy(dst, src)
                last.then_inc(w_free.sem, 1)

            empty(1, [(wuqT[:, :, :], bG[:, 0:256].rearrange("p (c n) -> p c n", c=4))])
            empty(2, [(wukvT[:, :, :], bR[:, 0:256].rearrange("p (c n) -> p c n", c=8))])
            empty(3, [(wdqT[:, :], bS[0:CQ, 0:128]), (gateT[:, :], bS[:, 128:136]), (b1T[:, :], bS[:, 136:168])])
            act.wait_ge(w_full.sem, 4)
            heads = absq[:, :].rearrange("q (c j n) -> q j c n", j=2, n=CKV)
            for j in range(2):
                last = AC(heads[:, j, :, :], (bM, bC)[j][0:CQ, 0:128].rearrange("q (c n) -> q c n", c=4), ACT.Copy,
                          scale=SCALE)
            last.then_inc(w_free.sem, 1)
            for j in range(2):
                r = slice(32 * j, 32 * j + CKV)
                empty(5 + j, [(wvo[r, :, :], bW[j][r, :].rearrange("p (c n) -> p c n", c=4))])
            empty(7, [(wq_all[:, :], bG[:, :])])

            nc.scalar.preload_act_table_set("natural_log_exp_and_others")
            oa = Own(act, own_aa)
            oc = Own(act, own_ac)

            def stage_a(s, i):
                p = i.par
                full = lambda u: act.wait_ge(a_full.sem, a_full.at(i.n, u + 1))
                free = lambda ins: ins.then_inc(a_free.sem, 1)
                ring = lambda u: bW[(u + p) % 2]
                oa.batch(s, i.n)
                if s == 0:
                    full(0)
                    free(copy(xT[:, :], ring(0)[:, 0:256]))
                if s == 1:
                    full(1)
                    free(copy(qiT[:, :, :], ring(1)[:, 0:384].rearrange("p (c n) -> p c n", c=2)))
                if s == 1.5:
                    full(2)
                    free(copy(kiT[:, :], ring(2)[:, 0:192]))
                if s in (2, 3):
                    full(s + 1)
                    if s == 2:
                        act.wait_ge(own_va.sem, own_va.at(i.n, 0))
                    free(AC(ra[:, s - 2::2, :], ring(s + 1)[:, 0:256].rearrange("p (c n) -> p c n", c=2), ACT.Relu))
                if s in (3.5, 4.5):
                    s = int(s)
                    full(s + 2)
                    free(AC(rb[:, s - 3::2, :], ring(s + 2)[0:64, 0:384].rearrange("p (c n) -> p c n", c=2), ACT.Relu))
                    s = -1
                if s in (5, 5.5):
                    for t in [int(2 * s) - 10]:
                        full(7 + t)
                        w = ring(7 + t)
                        act.wait_ge(g_q.sem, g_q.at(i.n - 1, t + 1))
                        act.wait_ge(a_full.sem, a_full.at(i.n, 0))
                        copy(qn[:, t, :, 0:32], w[:, 0:256].rearrange("p (h c) -> p h c", c=32))
                        k = oa.did(AC(pa[:, t, :], w[:, 256:512], ACT.Abs))
                        free(AC(pr[:, t, :], w[:, 256:512], ACT.Relu))
                        oa.wait(k)
                        k = oa.did(AC(pa[:, t, :], pa[:, t, :], ACT.Exp, scale=-1.0))
                        oa.wait(k)
                        AC(pe_[:, t, :], pa[:, t, :], ACT.Ln, bias=1.0).then_inc(a_soft.sem, 1)
                if s == 6:
                    full(9)
                    w = ring(9)
                    kv = w[:, 0:128].rearrange("p (t c) -> p t c", t=2)
                    act.wait_ge(g_spl.sem, g_spl.at(i.n, 0))
                    copy(ktab[:, :, 0:32], kv[:, :, 0:32])
                    act.wait_ge(m_full.sem, m_full.at(i.n - 2, 17))
                    copy(ckw[:, p, :, :], w[0:96, 128:320].rearrange("p (c n) -> p c n", c=6))
                    k = oa.did(AC(ka[:, :, :], kv[:, :, 32:64], ACT.Abs))
                    free(AC(kr[:, :, :], kv[:, :, 32:64], ACT.Relu))
                    oa.wait(k)
                    k = oa.did(AC(ka[:, :, :], ka[:, :, :], ACT.Exp, scale=-1.0))
                    oa.wait(k)
                    AC(ka[:, :, :], ka[:, :, :], ACT.Ln, bias=1.0).then_inc(a_soft.sem, 1)
                if s == 9:
                    full(10)
                    copy(kd[:, p, :], ring(10)[:, 0:256]).then_inc(a_free.sem, 1)
                if s in (12, 12.5, 14, 14.5):
                    t = (int(s) - 12) // 2
                    for hg in [int(2 * s) % 2]:
                        u = 11 + 2 * t + hg
                        full(u)
                        dst = qall[:, p, 1024 * t:1024 * t + 1024].rearrange("p (t h) -> p h t", h=NH)[:, 4 * hg:4 * hg + 4, :]
                        free(copy(dst, ring(u)[:, :].rearrange("p (h t) -> p h t", h=4)))

            def stage_b(s, i):
                p = i.par
                if s < 0:
                    return
                if s == int(s):
                    if s < NT:
                        act.wait_ge(s_max.sem, s_max.at(i.n, s + 1))
                        act.wait_ge(s_nrm.sem, s_nrm.at(i.n, s - 1))
                        w = 96 if s < T0 else SW
                        AC(pp[:, s % 2, 0:w], bS[:, 0:w], ACT.Exp, bias=nmx[:, s % 2:s % 2 + 1],
                           accum_out=lsum[:, s % 2:s % 2 + 1]).then_inc(s_exp.sem, 1)
                    return
                s = int(s)
                if 1 <= s <= NT + 1:
                    act.wait_ge(m_full.sem, m_full.at(i.n, s))
                    if s <= T0:
                        last = copy(pts[0:96, 0:128], bM[0:96, 0:128])
                    elif s <= NT:
                        last = copy(pts[:, :], bM[:, 0:256])
                    if T0 <= s < NT:
                        last = copy(vgs[:, s % 2, :], bM[:, LATENT:LATENT + 128])
                    if 2 <= s:
                        t = s - 2
                        if t == 0:
                            act.wait_ge(c_full.sem, c_full.at(i.n - 1, 1))
                        last = copy(ots[:, :, TQ * t:TQ * t + TQ], bM[0:64, WEIGHED:WEIGHED + 64].rearrange("p (a q) -> p a q", a=4))
                    last.then_inc(m_out.sem, 1)

            def rsqrt_start(i, k):
                act.wait_ge(ln_st.sem, ln_st.at(i.n, k))
                m = oc.did(AC(lnv[:, 1, :], lnv[:, 0, :], ACT.Ln))
                oc.wait(m)
                AC(lnv[:, 2, :], lnv[:, 1, :], ACT.Exp, scale=-0.5).then_inc(ln_rs.sem, 1)

            def stage_c(s, i):
                full = lambda u: act.wait_ge(c_full.sem, c_full.at(i.n, u + 1))
                oc.batch(s, i.n)
                if s == 1:
                    rsqrt_start(i, 1)
                if s == 2:
                    full(1)
                    for v in range(4):
                        last = AC(kT4[:, v, :], bC[:, 0:256], ACT.Copy, scale=C("variant")[:, v:v + 1])
                    last.then_inc(c_freeA.sem, 1)
                if s == 4:
                    full(3)
                    copy(qT[:, :], bC[:, 0:256]).then_inc(c_freeA.sem, 1)
                if s in (9, 13):
                    t = (s - 9) // 4
                    act.wait_ge(c_av.sem, c_av.at(i.n, t + 1))
                    act.wait_ge(c_full.sem, c_full.at(i.n - 1, 13))
                    copy(rT[:, 128 * t:128 * t + 128], bR[:, 256 + 128 * t:384 + 128 * t]).then_inc(c_ret.sem, 1)
                if s == 15:
                    rsqrt_start(i, 2)
                if s == 17:
                    full(13)
                    act.wait_ge(e_full.sem, e_full.at(i.n - 2, 16))
                    copy(x2T[:, i.par, :], bC[:, 0:256]).then_inc(c_freeA.sem, 1)
            od = Own(act, own_ad)

            def stage_d(s, i):
                if s == 0:
                    act.wait_ge(r_lg.sem, r_lg.at(i.n, 1))
                    AC(ex[:, :, :], lg[:, :, :], ACT.Exp).then_inc(r_ex.sem, 1)
                if s == 2:
                    act.wait_ge(r_full.sem, r_full.at(i.n, 2))
                    copy(gTs[:, :], bR[0:NE, 0:256]).then_inc(r_gt.sem, 1)
                if s in range(1, 2 * NE + 1):
                    e, half = (s - 1) // 2, (s - 1) % 2
                    act.wait_ge(e_full.sem, e_full.at(i.n, s))
                    act.wait_ge(e_y.sem, e_y.at(i.n, max(0, 2 * e - 2)))
                    for f in (2 * half, 2 * half + 1):
                        last = AC(hs[:, e % 2, f, :], bH[:, 256 * (f % 2):256 * (f % 2) + 256], ACT.Relu,
                                  bias=b1T[:, 4 * e + f:4 * e + f + 1])
                    last.then_inc(e_relu.sem, 1)
                if s == 20:
                    act.wait_ge(f_st.sem, f_st.at(i.n, 1))
                    od.batch(-1, i.n)
                    od.wait(od.did(AC(fln[:, 1, :], fln[:, 0, :], ACT.Ln)))
                    AC(fln[:, 2, :], fln[:, 1, :], ACT.Exp, scale=-0.5).then_inc(f_rs.sem, 1)

            program(stage_a, stage_b, stage_c, stage_d, act.Fori)
            assert oa.k == own_aa.per and oc.k == own_ac.per, (oa.k, oc.k)

        @block.vector
        def _(dve):
            for s_ in (own_va, g_spl, top_a, top_b, a_slot, o_ready, g_out, s_max, s_rec, s_nrm, c_freeV, ln_st, own_vc,
                       c_x1, c_x2, r_lg, r_gg, r_acc, e_acc, own_vd, own_vf, f_st, f_ln):
                dve.sem_inc(s_.sem, s_.per * s_.lead)
            TT, TS, STT = nc.vector.tensor_tensor, nc.vector.tensor_scalar, nc.vector.scalar_tensor_tensor
            prep = Own(dve, s_prep)

            def link(ins):
                prep.wait(prep.did(ins))

            dve.wait_ge(s_zero.sem, 3)
            nc.vector.memset(rank_t[0:32, :], 1.0)
            dve.wait_ge(d_early.sem, EARLY)
            nc.vector.tensor_copy(mbf[:, :], mraw[:, :]).then_inc(s_mb.sem, 1)
            dve.wait_ge(s_sin.sem, 1)
            link(TS(dl[:, 2, :], dl[:, 1, :], 1.0, None, ALU.add))
            link(nc.vector.reciprocal(dl[:, 1, :], dl[:, 2, :]))
            link(TS(dl[:, 2, :], dl[:, 1, :], -2 * np.pi, np.pi, ALU.mult, ALU.add))
            link(TS(dl[:, 2, :], dl[:, 2, :], 3.1415925, -3.1415925, ALU.min, ALU.max))
            TS(dl[:, 3, :], dl[:, 1, :], -np.pi, None, ALU.mult).then_inc(s_dl.sem, 1)
            dve.wait_ge(s_sin.sem, 3)
            link(TT(dl[:, 1, :], dl[:, 5, :], dl[:, 5, :], ALU.mult))
            link(TS(dl[:, 0, :], dl[:, 1, :], -2.0, 1.0, ALU.mult, ALU.add))
            link(TS(dl[:, 1, :], dl[:, 4, :], -1.0, None, ALU.mult))
            wide = lambda ap: ap.rearrange("p (g d) -> p g d", d=16)
            cd, sd = (dl[:, k:k + 1, 0:16].broadcast_to([128, 12, 16]) for k in (0, 1))
            rc, rs = (r[:, :, :, :].rearrange("p k t (h d) -> p (k t h) d", d=16) for r in (rot_c, rot_s))
            rt = wide(rot_t[:, :])
            link(TT(rc, wide(C("cos2")), cd, ALU.mult))
            link(TT(rt, wide(C("sin2")), sd, ALU.mult))
            link(TT(rc, rc, rt, ALU.subtract))
            link(TT(rs, wide(C("ssin2")), cd, ALU.mult))
            link(TT(rt, wide(C("scos2")), sd, ALU.mult))
            TT(rs, rs, rt, ALU.add).then_inc(s_rot.sem, 1)
            for lo in (32, 64):
                r = slice(lo, lo + 32)
                link(TS(rank_u[r, :], C("rank_a")[r, :], dl[r, 0, 16:17], None, ALU.mult))
                last = STT(rank_t[r, :], C("rank_b")[r, :], dl[r, 1, 16:17], rank_u[r, :], ALU.mult, ALU.add)
            last.then_inc(s_rot.sem, 1)
            dve.wait_ge(s_rot.sem, 2)
            dve.wait_ge(d_late.sem, LATE)
            assert prep.k == s_prep.per, prep.k

            ov, oc = Own(dve, own_va), Own(dve, own_vc)

            def settled():
                dve.sem_inc(s_pass.sem, 1)

            def split(parts, top, x, done, first):
                TT(top.bitcast(U32), x.bitcast(U32), high[:, 0:1].broadcast_to([128, x.shape[1]]),
                   ALU.bitwise_and).then_inc(done.sem, 1)
                dve.wait_ge(done.sem, first)
                TT(parts[:, 1, :], x, top, ALU.subtract).then_inc(done.sem, 1)
                nc.vector.tensor_copy(parts[:, 0, :], top).then_inc(done.sem, 1)

            def weighted(raw, dst, cut, n):
                k = ov.did(TS(dst, raw[:, 0, :], idxw[0:n, 0:1], None, ALU.mult))
                for h in range(1, NIH):
                    ov.wait(k)
                    k = ov.did(STT(dst, raw[:, h, :], idxw[0:n, h:h + 1], dst, ALU.mult, ALU.add))
                ov.wait(k)
                ov.did(TT(dst, dst, cut, ALU.min))

            def top(i, k, sig_, s_, v, idx):
                r, what = k // 3, k % 3
                if k == 0:
                    dve.wait_ge(own_va.sem, own_va.at(i.n, 5 if sig_ is top_a else 10))
                else:
                    dve.wait_ge(sig_.sem, sig_.at(i.n, k))
                settled()
                v8_, i8_ = v[:, 8 * r:8 * r + 8], idx[:, 8 * r:8 * r + 8]
                if what == 0:
                    ins = nc.vector.max(v8_, s_)
                elif what == 1:
                    ins = nc.vector.max_index(i8_, v8_, s_)
                else:
                    ins = nc.vector.match_replace(s_, v8_, s_, TAKEN)
                ins.then_inc(sig_.sem, 1)

            def stage_a(s, i):
                ov.batch(s, i.n)
                if s == 4:
                    dve.wait_ge(a_free.sem, a_free.at(i.n, 5))
                    weighted(ra, sa[:, :], C("cut_a"), 128)
                if s == 5:
                    dve.wait_ge(a_free.sem, a_free.at(i.n, 7))
                    weighted(rb, sbb[:, :], C("cut_b", 64), 64)
                if s == 8:
                    dve.wait_ge(g_kv.sem, g_kv.at(i.n, 1))
                    dve.wait_ge(g_full.sem, g_full.at(i.n - 2, 12))
                    split(kspl[:, i.par, :, :], ktop[:, :], ktab[:, :, :].rearrange("p t c -> p (t c)"), g_spl, g_spl.at(i.n, 1))
                for d in range(2) if s == int(s) else ():
                    ka_, kb_ = 2 * (s - 5) + d, 2 * (s - 6) + d
                    if 0 <= ka_ < 11:
                        top(i, ka_, top_a, sa[:, :], va, ia)
                    if 0 <= kb_ < 11:
                        top(i, kb_, top_b, sbb[:, :], vb, ib)
                if s == 12:
                    dve.wait_ge(d_put[1 - i.par].sem, d_put[1 - i.par].at(i.half - 1 + i.par, 32))
                    dve.wait_ge(top_a.sem, top_a.at(i.n, 11))
                    nc.vector.tensor_copy(ja[:, :], ia[:, :]).then_inc(a_slot.sem, 1)
                    dve.wait_ge(top_b.sem, top_b.at(i.n, 11))
                    nc.vector.tensor_copy(jb[:, :], ib[:, :]).then_inc(a_slot.sem, 1)

            def stage_b(s, i):
                p = i.par
                if s < 0:
                    return
                if s in (1.25, 3.25, 5.25, 7.25, 9.25, 11.25):
                    s = int(s)
                    c = s // 2
                    if c == 0:
                        dve.wait_ge(d_idx[p].sem, d_idx[p].at(i.half, 16))
                    dve.wait_ge(g_full.sem, g_full.at(i.n, 2 * c - 2))
                    src = sidx[:, 2 * SLOTS * c:2 * SLOTS * (c + 1)]
                    last = TS(oh[:, c % 2, 0, :], src, C("key_no")[:, 0:1], None, ALU.is_equal)
                    if c >= 4:
                        last = TS(oh[0:64, c % 2, 1, :], src[0:64, :], C("key_no")[0:64, 1:2], None, ALU.is_equal)
                    last.then_inc(o_ready.sem, 1)
                    return
                if s != int(s):
                    return
                if 1 <= s <= NT:
                    t = s - 1
                    w = 96 if t < T0 else SW
                    dve.wait_ge(s_exp.sem, s_exp.at(i.n, t + 1))
                    nc.vector.reciprocal(rls[:, t % 2:t % 2 + 1], lsum[:, t % 2:t % 2 + 1]).then_inc(s_rec.sem, 1)
                    dve.wait_ge(m_full.sem, m_full.at(i.n, max(0, t - 1)))
                    dve.wait_ge(s_rec.sem, s_rec.at(i.n, t + 1))
                    TS(ppn[:, t % 2, 0:w], pp[:, t % 2, 0:w], rls[:, t % 2:t % 2 + 1], None,
                       ALU.mult).then_inc(s_nrm.sem, 1)
                if s < NT:
                    dve.wait_ge(s_full.sem, s_full.at(i.n, s + 1))
                    w = 96 if s < T0 else SW
                    nc.vector.tensor_reduce(nmx[:, s % 2:s % 2 + 1], bS[:, 0:w], AX, ALU.max,
                                            negate=True).then_inc(s_max.sem, 1)
                if T0 <= s + 1 < NT:
                    g = s + 1 - T0
                    dve.wait_ge(m_full.sem, m_full.at(i.n, s - 1))
                    dve.wait_ge(g_full.sem, g_full.at(i.n, g + 1))
                    TT(gs[:, g % 2, :].rearrange("p (t j) -> p t j", j=FAR),
                       bG[0:96, :].rearrange("p (t j) -> p t j", j=FAR),
                       rank_t[:, :].rearrange("p (o j) -> p o j", o=1).broadcast_to([96, TQ, FAR]),
                       ALU.mult).then_inc(g_out.sem, 1)

            def moments(own, y, stats, m, ln, done):
                for t in range(2):
                    k = own.did(nc.vector.bn_stats(stats[:, t, :], y[:, t, :]))
                own.wait(k)
                settled()
                for t in range(2):
                    k = own.did(nc.vector.bn_aggr(m[:, t, :], stats[:, t, :]))
                own.wait(k)
                TS(ln[:, 0, :], m[:, :, 1], EPS, None, ALU.add).then_inc(done.sem, 1)

            def normalise(own, x, y, m, ln, done):
                own.wait(own.did(TT(ln[:, 3, :], ln[:, 2, :], ln[:, 2, :], ALU.mult)))
                own.wait(own.did(TT(ln[:, 4, :], ln[:, 3, :], ln[:, 0, :], ALU.mult)))
                own.wait(own.did(TS(ln[:, 3, :], ln[:, 4, :], -0.5, 1.5, ALU.mult, ALU.add)))
                own.wait(own.did(TT(ln[:, 5, :], ln[:, 3, :], ln[:, 2, :], ALU.mult)))
                own.did(TS(x[:, 0, :], y[:, 0, :], m[:, 0, 0:1], ln[:, 5, 0:1], ALU.subtract, ALU.mult))
                TS(x[:, 1, :], y[:, 1, :], m[:, 1, 0:1], ln[:, 5, 1:2], ALU.subtract, ALU.mult).then_inc(done.sem, 1)

            def stage_c(s, i):
                p = i.par
                full = lambda u: dve.wait_ge(c_full.sem, c_full.at(i.n, u + 1))
                free = lambda ins: ins.then_inc(c_freeV.sem, 1)
                freed = lambda u: dve.wait_ge(c_freeV.sem, c_freeV.at(i.n, C_BY[:u + 1].count("V")))
                two = lambda ap: ap.rearrange("p (t c) -> p t c", t=2)
                oc.batch(s, i.n)
                if s == 0:
                    full(0)
                    dve.wait_ge(d_cx[p].sem, d_cx[p].at(i.half, 32))
                    free(TT(y1[:, :, :], two(bC[:, 0:256]), xr[:, p, :, :], ALU.add))
                    freed(0)
                    moments(oc, y1, bst, mv, lnv, ln_st)
                if s == 1:
                    dve.wait_ge(ln_rs.sem, ln_rs.at(i.n, 1))
                    normalise(oc, x1, y1, mv, lnv, c_x1)
                if s == 2.5:
                    full(2)
                    free(TT(st[:, :], bC[:, 0:128], C("carry"), ALU.mult))
                if s in range(5, 13):
                    u = s - 5
                    dve.wait_ge(c_av.sem, c_av.at(i.n, u // 4))
                    full(4 + u)
                    free(TT(sm[:, u % 4, :].rearrange("p (v c) -> p v c", v=4), bC[:, :].rearrange("p (v c) -> p v c", v=4),
                            C("causal").rearrange("p (o c) -> p o c", o=1).broadcast_to([128, 4, 128]), ALU.mult))
                if s == 14:
                    full(12)
                    dve.wait_ge(c_x1.sem, c_x1.at(i.n, 1))
                    free(TT(y2[:, :, :], two(bC[:, 0:256]), x1[:, :, :], ALU.add))
                    freed(12)
                    moments(oc, y2, bst, mv, lnv, ln_st)
                if s == 15:
                    dve.wait_ge(ln_rs.sem, ln_rs.at(i.n, 2))
                    normalise(oc, x2, y2, mv, lnv, c_x2)
            od, of = Own(dve, own_vd), Own(dve, own_vf)

            def over_experts(r):
                return mx2[:, r, :].rearrange("p (t o) -> p t o", o=1).broadcast_to([128, 2, NE])

            def router(i):
                dve.wait_ge(r_ex.sem, r_ex.at(i.n, 1))
                k = od.did(nc.vector.tensor_reduce(mx2[:, 1, :], ex[:, :, :], AX, ALU.add))
                od.wait(k)
                k = od.did(nc.vector.reciprocal(mx2[:, 2, :], mx2[:, 1, :]))
                od.wait(k)
                k = od.did(TT(pr8[:, :, :], ex[:, :, :], over_experts(2), ALU.mult))
                for t in range(2):
                    od.wait(k)
                    settled()
                    m = od.did(nc.vector.max(v8[:, t, :], pr8[:, t, :]))
                for t in range(2):
                    od.wait(m)
                    settled()
                    k = od.did(nc.vector.max_index(i8[:, t, :], v8[:, t, :], pr8[:, t, :]))
                od.wait(k)
                k = od.did(nc.vector.tensor_copy(f8[:, :, :], i8[:, :, :]))
                od.wait(k)
                for t in range(2):
                    for h, r in ((h1, 0), (h2, 1)):
                        k = od.did(TS(h[:, t, :], C("expert_no"), f8[:, t, r:r + 1], v8[:, t, r:r + 1],
                                      ALU.is_equal, ALU.mult))
                od.wait(k)
                TT(gg[:, :, :], h1[:, :, :], h2[:, :, :], ALU.add).then_inc(r_gg.sem, 1)

            def stage_d(s, i):
                p = i.par
                od.batch(s, i.n)
                if s == 0:
                    dve.wait_ge(r_full.sem, r_full.at(i.n, 1))
                    k = od.did(nc.vector.tensor_reduce(mx2[:, 0, :], bR[:, 0:16].rearrange("p (t e) -> p t e", t=2), AX, ALU.max))
                    od.wait(k)
                    TT(lg[:, :, :], bR[:, 0:16].rearrange("p (t e) -> p t e", t=2), over_experts(0), ALU.subtract).then_inc(r_lg.sem, 1)
                if s == 1:
                    router(i)
                if s == 3:
                    dve.wait_ge(r_full.sem, r_full.at(i.n, 3))
                    dve.wait_ge(c_x2.sem, c_x2.at(i.n, 1))
                    dve.wait_ge(d_out[p].sem, d_out[p].at(i.half - 1, 16))
                    TT(acc[:, p, :, :], bR[:, 0:256].rearrange("p (t c) -> p t c", t=2), x2[:, :, :], ALU.add).then_inc(r_acc.sem, 1)
                if s in range(4, 2 * NE + 4):
                    e, t = (s - 4) // 2, s % 2
                    dve.wait_ge(e_y.sem, e_y.at(i.n, s - 3))
                    if s < 6:
                        dve.wait_ge(r_acc.sem, r_acc.at(i.n, 1))
                    else:
                        dve.wait_ge(e_acc.sem, e_acc.at(i.n, s - 5))
                    STT(acc[:, p, t, :], bR[:, 128 * t:128 * t + 128], gg[:, t, e:e + 1], acc[:, p, t, :],
                        ALU.mult, ALU.add).then_inc(e_acc.sem, 1)
                if s == 20:
                    dve.wait_ge(e_acc.sem, e_acc.at(i.n, 16))
                    settled()
                    of.batch(-1, i.n)
                    moments(of, acc[:, p, :, :], fst, fmv, fln, f_st)
                if s == 21:
                    dve.wait_ge(f_rs.sem, f_rs.at(i.n, 1))
                    normalise(of, acc[:, p, :, :], acc[:, p, :, :], fmv, fln, f_ln)

            program(stage_a, stage_b, stage_c, stage_d, dve.Fori)
            assert ov.k == own_va.per and oc.k == own_vc.per, (ov.k, oc.k)


EARLY, LATE, EXPERTS = 16 * 17, 16 * 9, 16 * 12

_INS = ["x", "ctx_1024"] + ["L0_attn_" + n for n in (
    "W_dkv", "W_uk", "W_uv", "W_dq", "W_uq", "W_qr", "W_kr", "W_out", "idx_wq", "idx_wk", "idx_w", "raw_delta",
)] + ["L0_ffn_" + n for n in ("gate_w", "w1", "b1", "w2", "b2")]


def kernel(**inputs):
    import concourse.bacc as bacc
    from concourse.bass_utils import run_bass_kernel_spmd

    nc = bacc.Bacc("TRN2", target_bir_lowering=False, num_devices=1)
    arrays, io = {}, {}
    for name in _INS:
        a = np.ascontiguousarray(inputs[name])
        arrays["in_" + name] = a
        short = name.replace("L0_attn_", "").replace("L0_ffn_", "").replace("ctx_1024", "ctx")
        io[short] = nc.dram_tensor("in_" + name, a.shape, mybir.dt.from_np(a.dtype), kind="ExternalInput").ap()
    out = nc.dram_tensor("out", (NB, L, DM), F32, kind="ExternalOutput").ap()
    build(nc, io, out)
    r = run_bass_kernel_spmd(nc, [arrays], core_ids=[0])
    return r.results[0]["out"]
```

```python
from contextlib import ExitStack

import numpy as np

import concourse.bass as bass
from concourse import mybir

ALU = mybir.AluOpType
ACT = mybir.ActivationFunctionType
F32 = mybir.dt.float32
BF16 = mybir.dt.bfloat16
U32 = mybir.dt.uint32
F32R = mybir.dt.float32r
AX = mybir.AxisListType.X

NB, L, DM = 8, 256, 128
NH, CKV, DR, DH, CQ = 8, 32, 32, 64, 64
WIN, FAR = 64, 32
NIH = 4
RH, RD = 16, 8
NE, FF = 8, 512
TQ = 16
NT = L // TQ
T0 = WIN // TQ
SLOTS = TQ * FAR
SW = 96 + 4 * FAR
SCALE = (DH + DR) ** -0.5
EPS = 1e-5
TAKEN = -3.4e38
NS = 20
SCORES_AT = (5.5, 6, 7, 8, 9.5, 10.5, 11.5, 12.5)
LEAD_A, LEAD_C, LEAD_D = 2, 2, 4


def constants():
    c = {}
    p = np.arange(128)
    c["ident"] = np.eye(128)
    c["key_no"] = np.stack([p, p % 64, 128 + p % 64], 1)
    def cut(t, n):
        s = np.arange(n)[None, :]
        return np.where(s <= t - WIN, 3e38, np.where(s > t, -1e30 * (1 + s / 256.0), -3e38))
    c["cut_a"] = cut(64 + p[:, None], 128)
    c["cut_b"] = cut(192 + p[:64, None], 192)
    half = DR // 2
    theta = 1.0 / 10000.0 ** (2.0 * np.arange(half) / DR)
    t = p[:, None] + 128 * np.arange(2)[None, :]
    pos = np.stack([t, t + np.maximum(0, t - (WIN - 1)), t], 1)
    ang = pos[..., None] * theta
    fac = np.array([SCALE, SCALE, 1.0])[None, :, None, None]
    two = lambda a, b: np.stack([a, b], 3).reshape(128, -1)
    co, si = np.cos(ang) * fac, np.sin(ang) * fac
    c["cos2"], c["sin2"] = two(co, co), two(si, si)
    c["ssin2"], c["scos2"] = two(-si, si), two(-co, co)
    rank = WIN + np.arange(FAR)
    ar = theta[np.arange(32) % half][:, None] * rank[None, :]
    sg = np.where(np.arange(32) < half, -1.0, 1.0)[:, None]
    z = np.zeros((32, FAR))
    c["rank_a"] = np.concatenate([z, np.cos(ar), sg * np.sin(ar), z])
    c["rank_b"] = np.concatenate([z, -np.sin(ar), sg * np.cos(ar), z])
    gam = 1.0 - np.exp(np.linspace(np.log(1 / 32.0), np.log(1 / 512.0), RH))
    base = (np.arange(0, RD, 2) + 0.4 * RD) / (1.4 * RD)
    inv = 1.0 / 10000.0 ** (np.arange(RD // 2) / (RD // 2))
    scale = base[None, None, :] ** (t[..., None] / 512.0)
    an = t[..., None] * inv
    dec = gam[None, :] ** p[:, None]
    def table(f, sc, d):
        x = np.repeat(f(an) * sc, 2, axis=-1)[:, :, None, :] * d[:, None, :, None]
        return x.reshape(128, 2, 128)
    sign = np.tile([-1.0, 1.0], 64)
    for n, sc, d in (("q", scale, dec), ("k", 1 / scale, 1 / dec)):
        c["cos_" + n] = table(np.cos, sc, d).reshape(128, 256)
        c["sin_" + n] = (table(np.sin, sc, d) * sign).reshape(128, 256)
    c["causal"] = (p[None, :] >= p[:, None]) * 1.0
    hd = p // RD
    c["carry"] = (hd[:, None] == hd[None, :]) * (gam[hd] ** 128)[:, None]
    c["variant"] = ((p[:, None] % 32) // RD == np.arange(4)[None, :]) * 1.0
    c["expert_no"] = np.tile(np.arange(8.0), (128, 1))
    return c


class Sig:

    def __init__(self, sem, per, lead=0):
        self.sem, self.per, self.lead = sem, per, lead

    def at(self, n, k):
        return (n + self.lead) * self.per + k


class Own:

    def __init__(self, eng, sig):
        self.eng, self.sig, self.n, self.k = eng, sig, 0, 0

    def batch(self, s, n):
        self.n = n
        if s < 0:
            assert self.k in (0, self.sig.per), (self.sig.sem.name, self.k, self.sig.per)
            self.k = 0

    def did(self, ins):
        ins.then_inc(self.sig.sem, 1)
        self.k += 1
        return self.k

    def wait(self, k):
        self.eng.wait_ge(self.sig.sem, self.sig.at(self.n, k))


class Inst:

    def __init__(self, n, par, half):
        self.n, self.par, self.half = n, par, half
        self.first, self.last = (isinstance(n, int) and n == k for k in (0, NB - 1))


C_USES = (("out", "V"), ("keys0", "A"), ("state", "V"), ("keys1", "A"), ("query_dims", "A"), ("queries0", "A"),
          ("scores0", "V"), ("scores1", "V"), ("scores2", "V"), ("scores3", "V"), ("queries1", "A"),
          ("scores4", "V"), ("scores5", "V"), ("scores6", "V"), ("scores7", "V"), ("retained", "V"), ("tokens", "A"))
C_AT = {name: k for k, (name, _) in enumerate(C_USES)}
C_BY = "".join(by for _, by in C_USES)


def build(nc, io, out):
    ctx = ExitStack()
    with ctx:
        sb = lambda name, shape, dt=F32: ctx.enter_context(nc.sbuf_tensor(name, shape, dt))
        pb = lambda name: ctx.enter_context(nc.psum_tensor(name, [128, 512], F32))

        def sig(name, per, lead=0):
            return Sig(ctx.enter_context(nc.semaphore(name)), per, lead)

        con = constants()
        cat, parts = {}, []
        at = 0
        for name, a in con.items():
            full = np.zeros((128, a.shape[1]), np.float32)
            full[:a.shape[0]] = a
            parts.append(full)
            cat[name] = (at, at + a.shape[1])
            at += a.shape[1]
        con_dram = nc.inline_tensor(np.concatenate(parts, 1), name="shape_constants").ap()
        k = np.arange(TQ)
        pick = (k[:, None] == np.arange(128)[None, :] // NH).astype(np.float32)
        hide = np.zeros((TQ, 2, SW), np.float32)
        for par in range(2):
            off = 16 * par
            r = np.arange(96)[None, :]
            hide[:, par, :96] = np.where((r >= off + 1 + k[:, None]) & (r <= off + 64 + k[:, None]), 0, -1e30)
            hide[:, par, 96:] = np.where(np.arange(128)[None, :] // FAR == k[:, None] % 4, 0, -1e30)
        mask_dram = nc.inline_tensor(np.concatenate([pick, hide.reshape(TQ, -1)], 1), name="mask_constants").ap()
        slots_dram = nc.dram_tensor("far_slots", [2, (L - WIN) * FAR], BF16, kind="Internal").ap()

        cst = sb("cst", [128, at])
        C = lambda name, rows=128: cst[0:rows, cat[name][0]:cat[name][1]]
        mbf = sb("mbf", [TQ, 128 + 2 * SW], BF16)
        pick_w = mbf[:, 0:128]
        hide_m = mbf[:, 128:128 + 2 * SW].rearrange("k (a c) -> k a c", a=2)
        wkv = sb("wkv", [128, 64])
        hs = sb("hs", [128, 2, 4, L])
        early_w = hs[:, :, :, :].rearrange("p a f t -> p (a f t)")
        wuq, wuk, wuv = early_w[0:CQ, 0:512], early_w[0:CKV, 512:1024], early_w[0:CKV, 1024:1536]
        sm = sb("sm", [128, 4, 512])
        early_s = sm[:, :, :].rearrange("p a c -> p (a c)")
        mraw = early_s[0:TQ, 0:128 + 2 * SW]
        wuqT = early_s[:, 576:832].rearrange("p (a c) -> p a c", c=CQ)
        wukvT = early_s[:, 832:1088].rearrange("p (a c) -> p a c", c=CKV)
        wout = early_s[:, 1088:1600].rearrange("p (a c) -> p a c", c=DM)
        wqr = early_s[0:CQ, 1600:1856]
        iwq, iwk = sb("iwq", [128, 256]), sb("iwk", [128, 128])
        idxw = sb("idxw", [128, NIH])
        gate, gateT = sb("gate", [NE, DM]), sb("gateT", [DM, NE])
        b1, b1T, b2 = sb("b1", [32, 128]), sb("b1T", [128, 32]), sb("b2", [NE, DM])
        absq = early_w[0:CQ, 1536:1792]
        wdq, wdqT = early_w[:, 1792:1856], early_w[0:CQ, 1856:1984]
        wq_all = sb("wq_all", [128, 512])
        wvo = sb("wvo", [64, 4, DM])
        dl = sb("dl", [128, 6, 17])
        rot_c, rot_s = sb("rot_c", [128, 3, 2, 32]), sb("rot_s", [128, 3, 2, 32])
        rank_t = sb("rank_t", [96, FAR])
        rank_u = sb("rank_u", [96, FAR])
        xn = sb("xn", [128, 2, 2, DM])
        xT = sb("xT", [128, L])
        qiT = sb("qiT", [128, 2, 192])
        kiT = sb("kiT", [128, 192])
        ra, rb = sb("ra", [128, NIH, 128]), sb("rb", [64, NIH, 192])
        sa, sbb = sb("sa", [128, 128]), sb("sbb", [64, 192])
        va, vb = sb("va", [128, FAR]), sb("vb", [64, FAR])
        ia, ib = sb("ia", [128, FAR], U32), sb("ib", [64, FAR], U32)
        ja, jb = sb("ja", [128, FAR], BF16), sb("jb", [64, FAR], BF16)
        qn = sb("qn", [128, 2, NH, 128])
        pa, pr = sb("pa", [128, 2, 256]), sb("pr", [128, 2, 256])
        g1, g2 = sb("g1", [128, 256]), sb("g2", [128, 256])
        ka, kr = sb("ka", [128, 2, 32]), sb("kr", [128, 2, 32])
        kg1, kg2 = sb("kg1", [128, 2, 32]), sb("kg2", [128, 2, 32])
        ktab = sb("ktab", [128, 2, 96])
        kdn = sb("kdn", [128, 2, 128])
        ktop, krest = sb("ktop", [128, 192]), sb("krest", [128, 192])
        kspl = sb("kspl", [128, 2, 2, 96], F32R)
        kstk = sb("kstk", [128, 2, 2, 96], F32R)
        high = sb("high", [128, 1], U32)
        ckw = sb("ckw", [96, 2, 6, CKV])
        kd = sb("kd", [128, 2, L])
        qall = sb("qall", [128, 2, L * NH])
        rot_t = g1[:, 0:192]
        sidx = sb("sidx", [128, (L - WIN) * FAR], BF16)
        oh = sb("oh", [128, 2, 2, 2 * SLOTS], F32R)
        gs = sb("gs", [96, 2, SLOTS])
        nmx, lsum, rls = sb("nmx", [128, 2]), sb("lsum", [128, 2]), sb("rls", [128, 2])
        pp = sb("pp", [128, 2, SW])
        ppn = sb("ppn", [128, 2, SW])
        pts = sb("pts", [128, 256])
        vgs = sb("vgs", [128, 2, 128])
        ots = sb("ots", [64, 4, L])
        xr, cn = sb("xr", [128, 2, 2, DM]), sb("cn", [128, 2, 2, DM])
        y, x1, x2 = (sb(n, [128, 2, DM]) for n in ("y", "x1", "x2"))
        bst, mv = sb("bst", [128, 2, 6]), sb("mv", [128, 2, 2])
        lnv = sb("lnv", [128, 6, 2])
        rqn = sb("rqn", [128, 2, DM])
        r1, r2, rkn = (sb(n, [128, 2, DM]) for n in ("r1", "r2", "rkn"))
        rks, rqs = sb("rks", [128, 2, 4, 4, 32]), sb("rqs", [128, 2, 4, 4, 32])
        kS, qV = sb("kS", [128, 2, 4, 128], F32R), sb("qV", [128, 4, 4, 128], F32R)
        qT = sb("qT", [128, 128])
        st = sb("st", [128, 128])
        cnm = sb("cnm", [128, 2, 4, DM])
        rT = sb("rT", [128, L])
        lg, ex, pr8 = (sb(n, [128, 2, NE]) for n in ("lg", "ex", "pr8"))
        mx2 = sb("mx2", [128, 3, 2])
        v8, i8, f8 = sb("v8", [128, 2, 8]), sb("i8", [128, 2, 8], U32), sb("f8", [128, 2, 8])
        h1, h2 = sb("h1", [128, 2, NE]), sb("h2", [128, 2, NE])
        gTs = sb("gTs", [NE, L])
        x2T = sb("x2T", [128, 2, L])
        acc = sb("acc", [128, 2, 2, DM])
        gg = sb("gg", [128, 2, NE])
        w1s, w2s = sb("w1s", [128, NE, FF]), sb("w2s", [128, NE, 4, DM])
        fst, fmv, fln = sb("fst", [128, 2, 6]), sb("fmv", [128, 2, 2]), sb("fln", [128, 6, 2])

        bG, bS = pb("bG"), pb("bS")
        bM = pb("bM")
        LATENT, WEIGHED = 256, 384
        bW = [pb("bW0"), pb("bW1")]
        bC = pb("bC")
        bH = pb("bH")
        bR = pb("bR")

        d_weights, d_out_weights, d_delta, d_late, d_tables = (
            sig(n, 0) for n in ("d_weights", "d_out_weights", "d_delta", "d_late", "d_tables"))
        d_x = [sig(f"d_x{i}", 16) for i in range(2)]
        d_cx = [sig(f"d_cx{i}", 32) for i in range(2)]
        d_put = [sig(f"d_put{i}", 32, 1) for i in range(2)]
        d_idx = [sig(f"d_idx{i}", 16) for i in range(2)]
        d_experts = sig("d_experts", 0)
        d_out = [sig(f"d_out{i}", 16, 1) for i in range(2)]
        w_full, w_free = sig("w_full", 7), sig("w_free", 7)
        s_prep = sig("s_prep", 14)
        s_mb, s_rot, s_sin, s_dl = (sig(n, 1) for n in ("s_mb", "s_rot", "s_sin", "s_dl"))
        s_zero = sig("s_zero", 1)
        s_pass = sig("s_pass", 0)
        a_full = sig("a_full", 15, 2)
        a_free = sig("a_free", 15, 2)
        own_aa = sig("own_aa", 6, 1)
        a_soft = sig("a_soft", 3, 1)
        own_va = sig("own_va", 10, 1)
        top_a, top_b = sig("top_a", 11, 1), sig("top_b", 11, 1)
        a_slot = sig("a_slot", 2, 1)
        own_ga = sig("own_ga", 24, 1)
        g_kv, g_q = sig("g_kv", 1, 1), sig("g_q", 2, 1)
        g_spl = sig("g_spl", 6, 1)
        o_ready = sig("o_ready", 6, 2)
        g_full = sig("g_full", 12, 2)
        g_out = sig("g_out", 12, 1)
        s_full = sig("s_full", 16, 1)
        s_max = sig("s_max", 16, 1)
        s_exp = sig("s_exp", 16, 1)
        s_rec = sig("s_rec", 16, 1)
        s_nrm = sig("s_nrm", 16, 1)
        m_full = sig("m_full", 17, 2)
        m_out = sig("m_out", 17, 1)
        c_full = sig("c_full", len(C_USES), 2)
        c_freeA = sig("c_freeA", C_BY.count("A"), 1)
        c_freeV = sig("c_freeV", C_BY.count("V"), 1)
        r_ks, r_qs = sig("r_ks", 2, 1), sig("r_qs", 2, 1)
        r_k, r_q = sig("r_k", 1, 1), sig("r_q", 1, 1)
        ln_st, ln_rs = sig("ln_st", 2, 1), sig("ln_rs", 2, 1)
        own_vc = sig("own_vc", 18, 1)
        own_ac = sig("own_ac", 2, 1)
        own_gc = sig("own_gc", 4, 1)
        r_v = sig("r_v", 4, 1)
        c_x1, c_x2 = sig("c_x1", 1, 1), sig("c_x2", 1, 1)
        c_av = sig("c_av", 2, 2)
        c_ret = sig("c_ret", 2, 1)
        r_full = sig("r_full", 3, 1)
        r_lg, r_ex, r_gg, r_gt = (sig(n, 1, 1) for n in ("r_lg", "r_ex", "r_gg", "r_gt"))
        r_acc = sig("r_acc", 1, 2)
        e_full = sig("e_full", 16, 2)
        e_relu = sig("e_relu", 16, 1)
        e_y = sig("e_y", 16, 1)
        e_acc = sig("e_acc", 16, 1)
        own_vd, own_vf, own_ad = sig("own_vd", 13, 1), sig("own_vf", 9, 1), sig("own_ad", 1, 1)
        f_st, f_rs, f_ln = (sig(n, 1, 1) for n in ("f_st", "f_rs", "f_ln"))

        def program(stage_a, stage_b, stage_c, stage_d, fori):

            def step(batch):
                for s in range(NS):
                    def run(f, at_, k, lead):
                        for own, i in ((at_ + lead, batch(k)), (at_ + lead - NS, batch(k + 1))):
                            if i is not None and own >= 0:
                                if own == 0:
                                    f(-1, i)
                                f(own, i)

                    run(stage_a, s, 1, LEAD_A)
                    run(stage_c, s, -1, LEAD_C)
                    run(stage_b, s, 0, 0)
                    run(stage_d, s, -2, LEAD_D)
                    run(stage_b, s + 0.25, 0, 0)
                    run(stage_a, s + 0.5, 1, LEAD_A)
                    run(stage_c, s + 0.5, -1, LEAD_C)
                    run(stage_d, s + 0.5, -2, LEAD_D)
                    run(stage_b, s + 0.75, 0, 0)

            def plain(s):
                step(lambda k: Inst(s + k, (s + k) % 2, (s + k) // 2) if 0 <= s + k < NB else None)

            for s in (-2, -1, 0, 1):
                plain(s)
            with fori(0, NB // 2 - 2) as i:
                for s in (2, 3):
                    step(lambda k: Inst(2 * i + s + k, (s + k) % 2, i + (s + k) // 2))
            for s in (NB - 2, NB - 1, NB, NB + 1):
                plain(s)

        block = ctx.enter_context(nc.Block())

        @block.sync
        def _(sp):
            for s_ in d_put + d_out:
                sp.sem_inc(s_.sem, s_.per * s_.lead)
            def load(group, count, pairs):
                for dst, src in pairs:
                    sp.dma_start(dst, src).then_inc(group.sem, 16)
                assert 16 * len(pairs) == count

            at_ = cat["ident"]
            raw = io["raw_delta"].rearrange("(o n) -> o n", o=1)
            load(d_delta, DELTA, (
                (dl[:, 0, 0:16], raw.broadcast_to([128, 16])),
                (dl[:, 0, 16:17], raw.rearrange("o (n k) -> o n k", k=1).broadcast_to([8, 16, 1])),
            ))
            load(d_weights, WEIGHTS, (
                (cst[:, at_[0]:at_[1]], con_dram[:, at_[0]:at_[1]]), (wuq[:, :], io["W_uq"]), (wuk[:, :], io["W_uk"]),
                (wuv[:, :], io["W_uv"]), (wdq[:, :], io["W_dq"]), (gate[:, :], io["gate_w"]),
                (b1[:, :], io["b1"].rearrange("e (f p) -> (e f) p", p=128)),
            ))
            load(d_out_weights, OUT_WEIGHTS, (
                (wqr[:, :], io["W_qr"]), (wout[:, :, :], io["W_out"].rearrange("(c p) n -> p c n", p=128)),
            ))
            sp.dma_start(xn[:, 0, :, :], io["x"][0].rearrange("(t p) d -> p t d", p=128)).then_inc(d_x[0].sem, 16)
            load(d_late, LATE, (
                (iwq[:, :], io["idx_wq"]), (iwk[:, 0:64], io["idx_wk"]), (iwk[:, 64:128], io["idx_wk"]),
                (wkv[:, 0:32], io["W_dkv"]), (wkv[:, 32:64], io["W_kr"]),
            ))
            load(d_tables, TABLES, (
                (cst[:, at_[1]:], con_dram[:, at_[1]:]), (mraw[:, :], mask_dram),
                (idxw[:, :], io["idx_w"].rearrange("(o n) -> o n", o=1).broadcast_to([128, NIH])), (b2[:, :], io["b2"]),
            ))

            def stage_a(s, i):
                if s == 2 and not i.last:
                    q = 1 - i.par
                    sp.wait_ge(a_full.sem, a_full.at(i.n - 1, 1))
                    sp.dma_start(xn[:, q, :, :], io["x"][i.n + 1].rearrange("(t p) d -> p t d", p=128)).then_inc(d_x[q].sem, 16)
                if s == 13:
                    row = slots_dram[i.par]
                    put = row[0:128 * FAR].rearrange("(p j) -> p j", j=FAR)
                    sp.wait_ge(a_slot.sem, a_slot.at(i.n, 2))
                    sp.dma_start(put, ja[:, :]).then_inc(d_put[i.par].sem, 16)
                    put = row[128 * FAR:].rearrange("(p j) -> p j", j=FAR)
                    sp.dma_start(put, jb[:, :]).then_inc(d_put[i.par].sem, 16)
                    sp.wait_ge(d_put[i.par].sem, d_put[i.par].at(i.half, 32))
                    sp.wait_ge(o_ready.sem, o_ready.at(i.n - 1, 6))
                    sp.dma_start(sidx[:, :], row.rearrange("(o n) -> o n", o=1).broadcast_to([128, (L - WIN) * FAR])).then_inc(d_idx[i.par].sem, 16)

            def stage_b(s, i):
                if s == 0 and i.first:
                    for q in range(4):
                        e = slice(2 * q, 2 * q + 2)
                        sp.dma_start(w1s[:, e, :], io["w1"][e].rearrange("e p f -> p e f")).then_inc(d_experts.sem, 16)
                        for h in (2 * q, 2 * q + 1):
                            sp.dma_start(w2s[:, h, :, :],
                                         io["w2"][h].rearrange("(f p) n -> p f n", p=128)).then_inc(d_experts.sem, 16)
                if s == 2:
                    sp.wait_ge(c_av.sem, c_av.at(i.n - 2, 2))
                    sp.dma_start(xr[:, i.par, :, :], io["x"][i.n].rearrange("(t p) d -> p t d", p=128)).then_inc(d_cx[i.par].sem, 16)
                    sp.dma_start(cn[:, i.par, :, :], io["ctx"][i.n].rearrange("(t p) d -> p t d", p=128)).then_inc(d_cx[i.par].sem, 16)

            def stage_c(s, i):
                pass

            def stage_d(s, i):
                if s == 21:
                    sp.wait_ge(f_ln.sem, f_ln.at(i.n, 1))
                    sp.dma_start(out[i.n].rearrange("(t p) d -> p t d", p=128), acc[:, i.par, :, :]).then_inc(d_out[i.par].sem, 16)

            program(stage_a, stage_b, stage_c, stage_d, sp.Fori)
            for s_ in d_out:
                sp.wait_ge(s_.sem, s_.at(NB // 2 - 1, 16))

        @block.gpsimd
        def _(pool):
            for s_ in (own_ga, g_kv, g_q, own_gc, r_k, r_q, r_v):
                pool.sem_inc(s_.sem, s_.per * s_.lead)
            nc.gpsimd.memset(kdn[:, :, 32:96], 0.0).then_inc(s_zero.sem, 1)
            nc.gpsimd.memset(cnm[:, :, :, :], 0.0).then_inc(s_zero.sem, 1)
            nc.gpsimd.memset(high[:, :], 0xFFFFF000).then_inc(s_zero.sem, 1)
            pool.wait_ge(s_zero.sem, 3)
            pool.wait_ge(s_rot.sem, 2)
            TT = nc.gpsimd.tensor_tensor
            oa = Own(pool, own_ga)
            oc = Own(pool, own_gc)
            hv = lambda ap: ap.rearrange("p (h a d) -> p h a d", a=2, d=16)

            def stage_a(s, i):
                oa.batch(s, i.n)
                if s == 6:
                    pool.wait_ge(a_soft.sem, a_soft.at(i.n, 3))
                    pool.wait_ge(a_full.sem, a_full.at(i.n - 1, 11))
                    pool.wait_ge(g_spl.sem, g_spl.at(i.n - 1, 6))
                    a = oa.did(TT(ktab[:, :, 32:64], kr[:, :, :], ka[:, :, :], ALU.add))
                    b = oa.did(TT(ktab[:, :, 64:80], kr[:, :, 16:32], ka[:, :, 16:32], ALU.add))
                    b = oa.did(TT(ktab[:, :, 80:96], kr[:, :, 0:16], ka[:, :, 0:16], ALU.add))
                    c = oa.did(nc.gpsimd.tensor_copy(kdn[:, :, 0:32], ktab[:, :, 0:32]))
                    oa.wait(b)
                    d = oa.did(TT(kg1[:, :, :], ktab[:, :, 32:64], rot_c[:, 2, :, :], ALU.mult))
                    e = oa.did(TT(kg2[:, :, :], ktab[:, :, 64:96], rot_s[:, 2, :, :], ALU.mult))
                    oa.wait(e)
                    TT(kdn[:, :, 96:128], kg1[:, :, :], kg2[:, :, :], ALU.add).then_inc(g_kv.sem, 1)
                if s in (5, 7):
                    t = (s - 5) // 2
                    pool.wait_ge(a_soft.sem, a_soft.at(i.n, t + 1))
                    pool.wait_ge(a_full.sem, a_full.at(i.n, 0))
                    a = oa.did(TT(pr[:, t, :], pr[:, t, :], pa[:, t, :], ALU.add))
                    oa.wait(a)
                    n4 = hv(pr[:, t, :])
                    pool.wait_ge(g_q.sem, g_q.at(i.n, t))
                    for kind in range(2):
                        if kind == 1:
                            oa.wait(oa.k)
                        c4 = hv(rot_c[:, kind, t, :]).broadcast_to([128, NH, 2, 16])
                        s4 = hv(rot_s[:, kind, t, :]).broadcast_to([128, NH, 2, 16])
                        a = oa.did(TT(hv(g1[:, :]), n4, c4, ALU.mult))
                        for h in range(2):
                            b = oa.did(TT(hv(g2[:, :])[:, :, h, :], n4[:, :, 1 - h, :], s4[:, :, h, :], ALU.mult))
                        oa.wait(b)
                        u, v = (g[:, :].rearrange("p (h d) -> p h d", d=32) for g in (g1, g2))
                        if kind == 0:
                            oa.did(TT(qn[:, t, :, 32:64], u, v, ALU.add))
                            oa.did(TT(qn[:, t, :, 64:96], u, v, ALU.add))
                        else:
                            TT(qn[:, t, :, 96:128], u, v, ALU.add).then_inc(g_q.sem, 1)

            def stage_b(s, i):
                pass

            def rotate(dst, src, cos, sin, t1, t2, done):
                cs, sn = (C(n).rearrange("p (t c) -> p t c", t=2) for n in (cos, sin))
                pairs = lambda ap: ap.rearrange("p t (c e) -> p t c e", e=2)
                oc.did(TT(t1[:, :, :], src, cs, ALU.mult))
                oc_last = None
                TT(pairs(t2[:, :, :])[:, :, :, 0], pairs(src)[:, :, :, 1], pairs(sn)[:, :, :, 0], ALU.mult)
                oc_last = oc.did(TT(pairs(t2[:, :, :])[:, :, :, 1], pairs(src)[:, :, :, 0], pairs(sn)[:, :, :, 1], ALU.mult))
                oc.wait(oc_last)
                TT(dst, t1[:, :, :], t2[:, :, :], ALU.add).then_inc(done.sem, 1)

            def stage_c(s, i):
                oc.batch(s, i.n)
                if s == 0:
                    pool.wait_ge(d_cx[i.par].sem, d_cx[i.par].at(i.half, 32))
                    pool.wait_ge(c_full.sem, c_full.at(i.n - 1, 3))
                    pool.wait_ge(r_q.sem, r_q.at(i.n - 1, 1))
                    rotate(rkn[:, :, :], cn[:, i.par, :, :], "cos_k", "sin_k", r1, r2, r_k)
                    pool.wait_ge(c_av.sem, c_av.at(i.n - 1, 2))
                    pool.sem_inc(s_pass.sem, 1)
                    heads = lambda ap: ap.rearrange("p t (g v e) -> p t g v e", v=4, e=RD)
                    for v in range(4):
                        nc.gpsimd.tensor_copy(heads(cnm[:, :, v, :])[:, :, :, v, :],
                                              heads(cn[:, i.par, :, :])[:, :, :, v, :]).then_inc(r_v.sem, 1)
                if s == 3:
                    pool.wait_ge(c_x1.sem, c_x1.at(i.n, 1))
                    pool.wait_ge(r_k.sem, r_k.at(i.n, 1))
                    rotate(rqn[:, :, :], x1[:, :, :], "cos_q", "sin_q", r1, r2, r_q)

            def stage_d(s, i):
                pass

            program(stage_a, stage_b, stage_c, stage_d, pool.Fori)
            assert (oa.k, oc.k) == (own_ga.per, own_gc.per), ("own_ga", oa.k, own_ga.per)

        @block.tensor
        def _(pe):
            for s_ in (a_full, g_full, s_full, m_full, c_full, c_av, r_full, e_full, e_y):
                pe.sem_inc(s_.sem, s_.per * s_.lead)
            MM = nc.tensor.matmul
            ident = C("ident")

            def flip(dst, src, n, lo=0):
                return MM(dst, src, ident[lo:lo + n, lo:lo + n], is_transpose=True, start=True, stop=True)

            pe.wait_ge(d_weights.sem, WEIGHTS)
            for c in range(4):
                last = flip(bG[:, 64 * c:64 * c + 64], wuq[:, 128 * c:128 * c + 128], CQ)
            last.then_inc(w_full.sem, 1)
            for j, w in enumerate((wuk, wuv)):
                for c in range(4):
                    last = flip(bR[:, 32 * (4 * j + c):32 * (4 * j + c) + 32], w[:, 128 * c:128 * c + 128], CKV)
            last.then_inc(w_full.sem, 1)
            flip(bS[0:CQ, 0:128], wdq[:, :], 128)
            flip(bS[:, 128:136], gate[:, :], NE)
            flip(bS[:, 136:168], b1[:, :], 32).then_inc(w_full.sem, 1)
            pe.wait_ge(w_free.sem, 3)
            for h in range(NH):
                lo = 64 * (h % 2)
                last = MM((bM, bC)[h % 2][0:CQ, 32 * (h // 2):32 * (h // 2) + 32], wuqT[lo:lo + 64, h // 2, :], wukvT[lo:lo + 64, h // 2, :],
                          start=True, stop=True)
            last.then_inc(w_full.sem, 1)
            pe.wait_ge(d_out_weights.sem, OUT_WEIGHTS)
            for j in range(2):
                for h in range(j, NH, 2):
                    lo, r = 64 * j, 32 * j
                    last = MM(bW[j][r:r + CKV, 128 * (h // 2):128 * (h // 2) + 128], wukvT[lo:lo + 64, 4 + h // 2, :],
                              wout[lo:lo + 64, h // 2, :], start=True, stop=True)
                last.then_inc(w_full.sem, 1)
            pe.wait_ge(w_free.sem, 4)
            MM(bG[:, 0:256], wdqT[:, :], absq[:, :], start=True, stop=True)
            MM(bG[:, 256:512], wdqT[:, :], wqr[:, :], start=True, stop=True).then_inc(w_full.sem, 1)
            pe.wait_ge(w_free.sem, 7)
            pe.wait_ge(d_late.sem, LATE)

            def stage_a(s, i):
                p = i.par

                def bank(u):
                    if u >= 2:
                        pe.wait_ge(a_free.sem, a_free.at(i.n, u - 1))
                    else:
                        pe.wait_ge(a_free.sem, a_free.at(i.n - 1, 14 + u))
                    return bW[(u + p) % 2]

                full = lambda ins: ins.then_inc(a_full.sem, 1)
                if s == 0:
                    w = bank(0)
                    pe.wait_ge(d_x[p].sem, d_x[p].at(i.half, 16))
                    pe.wait_ge(w_free.sem, 7)
                    for t in range(2):
                        last = flip(w[:, 128 * t:128 * t + 128], xn[:, p, t, :], 128)
                    full(last)
                if s == 1:
                    w = bank(1)
                    pe.wait_ge(a_free.sem, a_free.at(i.n, 1))
                    for c in range(2):
                        last = MM(w[:, 192 * c:192 * c + 192], iwq[:, 128 * c:128 * c + 128], xT[:, 64:256],
                                  start=True, stop=True)
                    full(last)
                if s == 1.5:
                    w = bank(2)
                    full(MM(w[:, 0:192], iwk[:, :], xT[:, 0:192], start=True, stop=True))
                if s in (2.5, 3):
                    r = 0 if s == 2.5 else 1
                    w = bank(3 + r)
                    lo = 64 * r
                    pe.wait_ge(a_free.sem, a_free.at(i.n, 3))
                    for c in range(2):
                        last = MM(w[:, 128 * c:128 * c + 128], qiT[lo:lo + 64, c, 0:128], kiT[lo:lo + 64, 0:128],
                                  start=True, stop=True)
                    full(last)
                if s in (3.5, 4.5):
                    w = bank(int(s) + 2)
                    lo = 64 * (int(s) - 3)
                    pe.sem_inc(s_pass.sem, 1)
                    for c in range(2):
                        last = MM(w[0:64, 192 * c:192 * c + 192], qiT[lo:lo + 64, c, 128:192], kiT[lo:lo + 64, :],
                                  start=True, stop=True)
                    full(last)
                if s in (5, 5.5):
                    for t in [int(2 * s) - 10]:
                        w = bank(7 + t)
                        full(MM(w[:, :], xT[:, 128 * t:128 * t + 128], wq_all[:, :], start=True, stop=True))
                if s == 6:
                    w = bank(9)
                    for t in range(2):
                        MM(w[:, 64 * t:64 * t + 64], xT[:, 128 * t:128 * t + 128], wkv[:, :], start=True, stop=True)
                    for c in range(6):
                        last = MM(w[0:96, 128 + 32 * c:160 + 32 * c], xT[:, 32 * c:32 * c + 96], wkv[:, 0:32],
                                  start=True, stop=True)
                    full(last)
                if s == 9:
                    w = bank(10)
                    pe.wait_ge(g_kv.sem, g_kv.at(i.n, 1))
                    for t in range(2):
                        last = flip(w[:, 128 * t:128 * t + 128], kdn[:, t, :], 128)
                    full(last)
                if s in (12, 12.5, 14, 14.5):
                    t = (int(s) - 12) // 2
                    pe.wait_ge(g_q.sem, g_q.at(i.n, t + 1))
                    for hg in [int(2 * s) % 2]:
                        w = bank(11 + 2 * t + hg)
                        for h in range(4):
                            last = flip(w[:, 128 * h:128 * h + 128], qn[:, t, 4 * hg + h, :], 128)
                        full(last)

            def gather(i, tile):
                p, g = i.par, tile - T0
                if tile % 2 == 0:
                    pe.wait_ge(o_ready.sem, o_ready.at(i.n, g // 2 + 1))
                if g == 0:
                    pe.wait_ge(g_spl.sem, g_spl.at(i.n, 6))
                pe.wait_ge(g_out.sem, g_out.at(i.n, g))
                w = bG
                pair = g // 2
                if pair == 1:
                    products = [(kstk[:, p, 0, :], 0)]
                else:
                    products = [(kspl[:, p, part, :], 0) for part in range(2)]
                if pair >= 4:
                    products.append((kstk[:, p, 1, :], 1))
                for n, (table, kt) in enumerate(products):
                    last = MM(w[0:96, :], table, oh[:, pair % 2, kt, SLOTS * (tile % 2):SLOTS * (tile % 2) + SLOTS],
                              start=(n == 0), stop=(n == len(products) - 1))
                last.then_inc(g_full.sem, 1)

            def scores(i, tile):
                p, g = i.par, tile - T0
                pe.wait_ge(s_exp.sem, s_exp.at(i.n, tile))
                o = 0
                q = qall[:, p, 128 * tile:128 * tile + 128]
                if tile < T0:
                    MM(bS[:, o:o + 96], q, kd[:, p, 0:96], start=True, stop=True).then_inc(s_full.sem, 1)
                    return
                MM(bS[:, o:o + SW], pick_w, hide_m[:, tile % 2, :], start=True, stop=True,
                   skip_group_check=True)
                k0 = 32 * ((tile - T0) // 2)
                MM(bS[:, o:o + 96], q, kd[:, p, k0:k0 + 96], start=False, stop=True, skip_group_check=True)
                pe.wait_ge(g_out.sem, g_out.at(i.n, g + 1))
                for c in range(4):
                    last = MM(bS[32 * c:32 * c + 32, o + 96:o + SW], qall[0:96, p, 128 * tile + 32 * c:128 * tile + 32 * c + 32],
                              gs[:, g % 2, 128 * c:128 * c + 128], start=False, stop=True, skip_group_check=True)
                last.then_inc(s_full.sem, 1)

            def far_latents(i, tile):
                g = tile - T0
                for c in range(4):
                    o = LATENT + 32 * c
                    flip(bM[:, o:o + 32], gs[0:32, g % 2, 128 * c:128 * c + 128], 32)

            def turn(i, tile):
                pe.wait_ge(s_nrm.sem, s_nrm.at(i.n, tile + 1))
                w = ppn[:, tile % 2, :]
                if tile < T0:
                    return flip(bM[0:96, 0:128], w[:, 0:96], 128)
                flip(bM[:, 0:128], w[:, 0:128], 128)
                return flip(bM[:, 128:256], w[:, 96:SW], 128)

            def weigh(i, tile):
                g, p = tile - T0, i.par
                near = ckw[:, p, 0 if g < 0 else g // 2, :]
                for j in range(2):
                    last = MM(bM[32 * j:32 * j + 32, WEIGHED:WEIGHED + 64], near,
                              pts[0:96, 0:128].rearrange("p (q a b) -> p b a q", a=4, b=2)[:, j, :, :],
                              start=True, stop=True, skip_group_check=True)
                for c in range(4) if g >= 0 else ():
                    for j in range(2):
                        last = MM(bM[32 * j:32 * j + 32, WEIGHED:WEIGHED + 64].rearrange("p (a q) -> p a q", a=4)[:, :, 4 * c:4 * c + 4],
                                  vgs[:, g % 2, 32 * c:32 * c + 32],
                                  pts[:, 128 + 32 * c:160 + 32 * c].rearrange("p (q a b) -> p b a q", a=4, b=2)[:, j, :, :],
                                  start=False, stop=True, skip_group_check=True)
                return last

            def stage_b(s, i):
                if s < 0:
                    return
                if s == 0:
                    if i.first:
                        pe.wait_ge(s_mb.sem, 1)
                    pe.wait_ge(a_free.sem, a_free.at(i.n, 15))
                if s == int(s):
                    if s < NT:
                        scores(i, s)
                    if T0 <= s + 1 < NT:
                        gather(i, s + 1)
                    return
                if s > int(s) + 0.25:
                    return
                s = int(s)
                if 1 <= s <= NT + 1:
                    pe.wait_ge(m_out.sem, m_out.at(i.n, s - 1))
                    pe.sem_inc(s_pass.sem, 1)
                    if 2 <= s:
                        last = weigh(i, s - 2)
                    if T0 <= s < NT:
                        far_latents(i, s)
                    if s <= NT:
                        last = turn(i, s - 1)
                    last.then_inc(m_full.sem, 1)

            def stage_c(s, i):
                p = i.par

                def emptied(use, n=i.n):
                    u = C_AT[use]
                    f = c_freeA if C_BY[u] == "A" else c_freeV
                    pe.wait_ge(f.sem, f.at(n, C_BY[:u + 1].count(C_BY[u])))

                def bank(use):
                    u = C_AT[use]
                    emptied(C_USES[u - 1][0], i.n if u >= 1 else i.n - 1)
                    return bC

                full = lambda ins: ins.then_inc(c_full.sem, 1)
                if s == 0:
                    w = bank("out")
                    pe.wait_ge(m_out.sem, m_out.at(i.n, 17))
                    for t in range(2):
                        for h in range(4):
                            last = MM(w[:, 128 * t:128 * t + 128], ots[:, h, 128 * t:128 * t + 128], wvo[:, h, :],
                                      start=(h == 0), stop=(h == 3))
                    full(last)
                if s in (2, 3):
                    t = s - 2
                    w = bank(f"keys{t}")
                    pe.wait_ge(r_ks.sem, r_ks.at(i.n, 2))
                    for g in range(4):
                        last = flip(w[:, 128 * g:128 * g + 128], rks[:, t, g, :, :].rearrange("p a d -> p (a d)"), 128)
                    full(last)
                if s == 2.5:
                    w = bank("state")
                    full(MM(w[:, 0:128], rkn[:, 0, :], cn[:, p, 0, :], start=True, stop=True))
                if s == 4:
                    w = bank("query_dims")
                    pe.wait_ge(r_q.sem, r_q.at(i.n, 1))
                    full(flip(w[:, 0:128], rqn[:, 1, :], 128))
                if s in (9, 14):
                    t = s // 14
                    emptied(f"scores{4 * t + 3}")
                    pe.wait_ge(r_v.sem, r_v.at(i.n, 4))
                    pe.wait_ge(e_acc.sem, e_acc.at(i.n - 1, s - 4 + LEAD_D - LEAD_C))
                    o = 256 + 128 * t
                    if t == 1:
                        MM(bR[:, o:o + 128], st[:, :], qT[:, :], start=True, stop=True, skip_group_check=True)
                    for v in range(4):
                        for g in range(4):
                            last = MM(bR[32 * g:32 * g + 32, o:o + 128], cnm[:, t, v, 32 * g:32 * g + 32],
                                      sm[:, g, 128 * v:128 * v + 128], start=(t == 0 and v == 0), stop=True,
                                      skip_group_check=True)
                    last.then_inc(c_av.sem, 1)
                if s in (4.5, 9):
                    t = s // 9
                    w = bank(f"queries{int(t)}")
                    pe.wait_ge(r_qs.sem, r_qs.at(i.n, 2))
                    for g in range(4):
                        last = flip(w[:, 128 * g:128 * g + 128], rqs[:, int(t), g, :, :].rearrange("p a d -> p (a d)"), 128)
                    full(last)
                if s in SCORES_AT:
                    u = SCORES_AT.index(s)
                    t, g = u // 4, u % 4
                    w = bank(f"scores{u}")
                    full(MM(w[:, :], kS[:, t, g, :], qV[:, :, g, :], start=True, stop=True))
                if s == 14.5:
                    w = bank("retained")
                    pe.wait_ge(c_ret.sem, c_ret.at(i.n, 2))
                    for t in range(2):
                        last = flip(w[:, 128 * t:128 * t + 128], rT[:, 128 * t:128 * t + 128], 128)
                    full(last)
                if s == 17:
                    w = bank("tokens")
                    pe.wait_ge(c_x2.sem, c_x2.at(i.n, 1))
                    for t in range(2):
                        last = flip(w[:, 128 * t:128 * t + 128], x2[:, t, :], 128)
                    full(last)
            def stage_d(s, i):
                p = i.par
                if s == 0:
                    if i.first:
                        pe.wait_ge(d_experts.sem, EXPERTS)
                    pe.wait_ge(c_freeA.sem, c_freeA.at(i.n, C_BY.count("A")))
                    pe.wait_ge(e_acc.sem, e_acc.at(i.n - 1, 16))
                    for t in range(2):
                        last = MM(bR[:, 8 * t:8 * t + 8], x2T[:, p, 128 * t:128 * t + 128], gateT[:, :], start=True, stop=True)
                    last.then_inc(r_full.sem, 1)
                if s == 2:
                    pe.wait_ge(r_gg.sem, r_gg.at(i.n, 1))
                    for t in range(2):
                        last = flip(bR[0:NE, 128 * t:128 * t + 128], gg[:, t, :], 128)
                    last.then_inc(r_full.sem, 1)
                if s == 3:
                    pe.wait_ge(r_gt.sem, r_gt.at(i.n, 1))
                    for t in range(2):
                        last = MM(bR[:, 128 * t:128 * t + 128], gTs[:, 128 * t:128 * t + 128], b2[:, :], start=True, stop=True)
                    last.then_inc(r_full.sem, 1)
                if s in range(4, 2 * NE + 4):
                    e, t = (s - 4) // 2, s % 2
                    pe.wait_ge(e_relu.sem, e_relu.at(i.n, 2 * e + 2))
                    if s == 4:
                        pe.wait_ge(r_acc.sem, r_acc.at(i.n, 1))
                    else:
                        pe.wait_ge(e_acc.sem, e_acc.at(i.n, s - 4))
                    if s - LEAD_D + LEAD_C in (9, 14) and not i.last:
                        pe.wait_ge(c_ret.sem, c_ret.at(i.n + 1, 1 + (s - LEAD_D + LEAD_C) // 14))
                    for f in range(4):
                        last = MM(bR[:, 128 * t:128 * t + 128], hs[:, e % 2, f, 128 * t:128 * t + 128], w2s[:, e, f, :],
                                  start=(f == 0), stop=(f == 3))
                    last.then_inc(e_y.sem, 1)
                if s in range(1, 2 * NE + 1):
                    e, half = (s - 1) // 2, (s - 1) % 2
                    pe.wait_ge(e_relu.sem, e_relu.at(i.n, s - 1))
                    for f in (2 * half, 2 * half + 1):
                        last = MM(bH[:, 256 * (f % 2):256 * (f % 2) + 256], w1s[:, e, 128 * f:128 * f + 128], x2T[:, p, :],
                                  start=True, stop=True)
                    last.then_inc(e_full.sem, 1)

            program(stage_a, stage_b, stage_c, stage_d, pe.Fori)

        @block.scalar
        def _(act):
            for s_ in (a_free, a_soft, own_aa, s_exp, m_out, c_freeA, c_ret, ln_rs, own_ac, r_ex, r_gt, e_relu, own_ad, f_rs):
                act.sem_inc(s_.sem, s_.per * s_.lead)
            AC = nc.scalar.activation
            copy = nc.scalar.copy
            act.wait_ge(d_delta.sem, DELTA)
            AC(dl[:, 1, :], dl[:, 0, :], ACT.Exp, scale=-1.0).then_inc(s_sin.sem, 1)
            act.wait_ge(s_dl.sem, 1)
            AC(dl[:, 4, :], dl[:, 2, :], ACT.Sin).then_inc(s_sin.sem, 1)
            AC(dl[:, 5, :], dl[:, 3, :], ACT.Sin).then_inc(s_sin.sem, 1)
            nc.scalar.preload_act_table_set("natural_log_exp_and_others")

            def empty(k, pairs):
                act.wait_ge(w_full.sem, k)
                for dst, src in pairs:
                    last = copy(dst, src)
                last.then_inc(w_free.sem, 1)

            empty(1, [(wuqT[:, :, :], bG[:, 0:256].rearrange("p (c n) -> p c n", c=4))])
            empty(2, [(wukvT[:, :, :], bR[:, 0:256].rearrange("p (c n) -> p c n", c=8))])
            empty(3, [(wdqT[:, :], bS[0:CQ, 0:128]), (gateT[:, :], bS[:, 128:136]), (b1T[:, :], bS[:, 136:168])])
            act.wait_ge(w_full.sem, 4)
            heads = absq[:, :].rearrange("q (c j n) -> q j c n", j=2, n=CKV)
            for j in range(2):
                last = AC(heads[:, j, :, :], (bM, bC)[j][0:CQ, 0:128].rearrange("q (c n) -> q c n", c=4), ACT.Copy,
                          scale=SCALE)
            last.then_inc(w_free.sem, 1)
            for j in range(2):
                r = slice(32 * j, 32 * j + CKV)
                empty(5 + j, [(wvo[r, :, :], bW[j][r, :].rearrange("p (c n) -> p c n", c=4))])
            empty(7, [(wq_all[:, :], bG[:, :])])

            oa = Own(act, own_aa)
            oc = Own(act, own_ac)

            def stage_a(s, i):
                p = i.par
                full = lambda u: act.wait_ge(a_full.sem, a_full.at(i.n, u + 1))
                free = lambda ins: ins.then_inc(a_free.sem, 1)
                ring = lambda u: bW[(u + p) % 2]
                oa.batch(s, i.n)
                if s == 0:
                    full(0)
                    free(copy(xT[:, :], ring(0)[:, 0:256]))
                if s == 1:
                    full(1)
                    free(copy(qiT[:, :, :], ring(1)[:, 0:384].rearrange("p (c n) -> p c n", c=2)))
                if s == 1.5:
                    full(2)
                    free(copy(kiT[:, :], ring(2)[:, 0:192]))
                if s in (2.5, 3):
                    r = 0 if s == 2.5 else 1
                    full(3 + r)
                    if r == 0:
                        act.wait_ge(own_va.sem, own_va.at(i.n, 0))
                    free(AC(ra[:, r::2, :], ring(3 + r)[:, 0:256].rearrange("p (c n) -> p c n", c=2), ACT.Relu))
                if s in (3.5, 4.5):
                    s = int(s)
                    full(s + 2)
                    free(AC(rb[:, s - 3::2, :], ring(s + 2)[0:64, 0:384].rearrange("p (c n) -> p c n", c=2), ACT.Relu))
                    s = -1
                if s in (5, 5.5):
                    for t in [int(2 * s) - 10]:
                        full(7 + t)
                        w = ring(7 + t)
                        act.wait_ge(g_q.sem, g_q.at(i.n - 1, t + 1))
                        act.wait_ge(a_full.sem, a_full.at(i.n, 0))
                        copy(qn[:, t, :, 0:32], w[:, 0:256].rearrange("p (h c) -> p h c", c=32))
                        k = oa.did(AC(pa[:, t, :], w[:, 256:512], ACT.Abs))
                        free(AC(pr[:, t, :], w[:, 256:512], ACT.Relu))
                        oa.wait(k)
                        k = oa.did(AC(pa[:, t, :], pa[:, t, :], ACT.Exp, scale=-1.0))
                        oa.wait(k)
                        AC(pa[:, t, :], pa[:, t, :], ACT.Ln, bias=1.0).then_inc(a_soft.sem, 1)
                if s == 6:
                    full(9)
                    w = ring(9)
                    kv = w[:, 0:128].rearrange("p (t c) -> p t c", t=2)
                    act.wait_ge(g_spl.sem, g_spl.at(i.n, 0))
                    copy(ktab[:, :, 0:32], kv[:, :, 0:32])
                    act.wait_ge(m_full.sem, m_full.at(i.n - 2, 17))
                    copy(ckw[:, p, :, :], w[0:96, 128:320].rearrange("p (c n) -> p c n", c=6))
                    k = oa.did(AC(ka[:, :, :], kv[:, :, 32:64], ACT.Abs))
                    free(AC(kr[:, :, :], kv[:, :, 32:64], ACT.Relu))
                    oa.wait(k)
                    k = oa.did(AC(ka[:, :, :], ka[:, :, :], ACT.Exp, scale=-1.0))
                    oa.wait(k)
                    AC(ka[:, :, :], ka[:, :, :], ACT.Ln, bias=1.0).then_inc(a_soft.sem, 1)
                if s == 9:
                    full(10)
                    copy(kd[:, p, :], ring(10)[:, 0:256]).then_inc(a_free.sem, 1)
                if s in (12, 12.5, 14, 14.5):
                    t = (int(s) - 12) // 2
                    for hg in [int(2 * s) % 2]:
                        u = 11 + 2 * t + hg
                        full(u)
                        dst = qall[:, p, 1024 * t:1024 * t + 1024].rearrange("p (t h) -> p h t", h=NH)[:, 4 * hg:4 * hg + 4, :]
                        free(copy(dst, ring(u)[:, :].rearrange("p (h t) -> p h t", h=4)))

            def stage_b(s, i):
                p = i.par
                if s < 0:
                    return
                if s == int(s):
                    if s < NT:
                        act.wait_ge(s_max.sem, s_max.at(i.n, s + 1))
                        act.wait_ge(s_nrm.sem, s_nrm.at(i.n, s - 1))
                        w = 96 if s < T0 else SW
                        AC(pp[:, s % 2, 0:w], bS[:, 0:w], ACT.Exp, bias=nmx[:, s % 2:s % 2 + 1],
                           accum_out=lsum[:, s % 2:s % 2 + 1]).then_inc(s_exp.sem, 1)
                    return
                if s > int(s) + 0.25:
                    return
                s = int(s)
                if 1 <= s <= NT + 1:
                    act.wait_ge(m_full.sem, m_full.at(i.n, s))
                    if s <= T0:
                        last = copy(pts[0:96, 0:128], bM[0:96, 0:128])
                    elif s <= NT:
                        last = copy(pts[:, :], bM[:, 0:256])
                    if T0 <= s < NT:
                        last = copy(vgs[:, s % 2, :], bM[:, LATENT:LATENT + 128])
                    if 2 <= s:
                        t = s - 2
                        if t == 0:
                            act.wait_ge(c_full.sem, c_full.at(i.n - 1, 1))
                        last = copy(ots[:, :, TQ * t:TQ * t + TQ], bM[0:64, WEIGHED:WEIGHED + 64].rearrange("p (a q) -> p a q", a=4))
                    last.then_inc(m_out.sem, 1)

            def rsqrt_start(i, k):
                act.wait_ge(ln_st.sem, ln_st.at(i.n, k))
                m = oc.did(AC(lnv[:, 1, :], lnv[:, 0, :], ACT.Ln))
                oc.wait(m)
                AC(lnv[:, 2, :], lnv[:, 1, :], ACT.Exp, scale=-0.5).then_inc(ln_rs.sem, 1)

            def stage_c(s, i):
                full = lambda use: act.wait_ge(c_full.sem, c_full.at(i.n, C_AT[use] + 1))
                free = lambda ins: ins.then_inc(c_freeA.sem, 1)
                oc.batch(s, i.n)
                if s == 1:
                    rsqrt_start(i, 1)
                if s in (2, 3):
                    t = s - 2
                    full(f"keys{t}")
                    free(copy(kS[:, t, :, :], bC[:, :].rearrange("p (g c) -> p g c", g=4)))
                if s == 4:
                    full("query_dims")
                    free(copy(qT[:, :], bC[:, 0:128]))
                if s in (9, 14):
                    t = s // 14
                    act.wait_ge(c_av.sem, c_av.at(i.n, t + 1))
                    act.wait_ge(c_full.sem, c_full.at(i.n - 1, C_AT["retained"] + 1))
                    copy(rT[:, 128 * t:128 * t + 128], bR[:, 256 + 128 * t:384 + 128 * t]).then_inc(c_ret.sem, 1)
                if s in (4.5, 9):
                    full("queries0" if s == 4.5 else "queries1")
                    for v in range(4):
                        last = AC(qV[:, v, :, :], bC[:, :].rearrange("p (g c) -> p g c", g=4), ACT.Copy,
                                  scale=C("variant")[:, v:v + 1])
                    free(last)
                if s == 15:
                    rsqrt_start(i, 2)
                if s == 17:
                    full("tokens")
                    act.wait_ge(e_full.sem, e_full.at(i.n - 2, 16))
                    free(copy(x2T[:, i.par, :], bC[:, 0:256]))

            od = Own(act, own_ad)

            def stage_d(s, i):
                if s == 0:
                    act.wait_ge(r_lg.sem, r_lg.at(i.n, 1))
                    AC(ex[:, :, :], lg[:, :, :], ACT.Exp).then_inc(r_ex.sem, 1)
                if s == 2:
                    act.wait_ge(r_full.sem, r_full.at(i.n, 2))
                    copy(gTs[:, :], bR[0:NE, 0:256]).then_inc(r_gt.sem, 1)
                if s in range(1, 2 * NE + 1):
                    e, half = (s - 1) // 2, (s - 1) % 2
                    act.wait_ge(e_full.sem, e_full.at(i.n, s))
                    act.wait_ge(e_y.sem, e_y.at(i.n, max(0, 2 * e - 2)))
                    for f in (2 * half, 2 * half + 1):
                        last = AC(hs[:, e % 2, f, :], bH[:, 256 * (f % 2):256 * (f % 2) + 256], ACT.Relu,
                                  bias=b1T[:, 4 * e + f:4 * e + f + 1])
                    last.then_inc(e_relu.sem, 1)
                if s == 20:
                    act.wait_ge(f_st.sem, f_st.at(i.n, 1))
                    od.batch(-1, i.n)
                    od.wait(od.did(AC(fln[:, 1, :], fln[:, 0, :], ACT.Ln)))
                    AC(fln[:, 2, :], fln[:, 1, :], ACT.Exp, scale=-0.5).then_inc(f_rs.sem, 1)

            program(stage_a, stage_b, stage_c, stage_d, act.Fori)
            assert oa.k == own_aa.per and oc.k == own_ac.per, (oa.k, oc.k)

        @block.vector
        def _(dve):
            for s_ in (own_va, g_spl, r_ks, r_qs, top_a, top_b, a_slot, o_ready, g_out, s_max, s_rec, s_nrm, c_freeV, ln_st, own_vc,
                       c_x1, c_x2, r_lg, r_gg, r_acc, e_acc, own_vd, own_vf, f_st, f_ln):
                dve.sem_inc(s_.sem, s_.per * s_.lead)
            TT, TS, STT = nc.vector.tensor_tensor, nc.vector.tensor_scalar, nc.vector.scalar_tensor_tensor
            prep = Own(dve, s_prep)

            def link(ins):
                prep.wait(prep.did(ins))

            dve.wait_ge(s_zero.sem, 3)
            nc.vector.memset(rank_t[0:32, :], 1.0)
            dve.wait_ge(s_sin.sem, 1)
            link(TS(dl[:, 2, :], dl[:, 1, :], 1.0, None, ALU.add))
            link(nc.vector.reciprocal(dl[:, 1, :], dl[:, 2, :]))
            link(TS(dl[:, 2, :], dl[:, 1, :], -2 * np.pi, np.pi, ALU.mult, ALU.add))
            link(TS(dl[:, 2, :], dl[:, 2, :], 3.1415925, -3.1415925, ALU.min, ALU.max))
            TS(dl[:, 3, :], dl[:, 1, :], -np.pi, None, ALU.mult).then_inc(s_dl.sem, 1)
            dve.wait_ge(s_sin.sem, 3)
            link(TT(dl[:, 1, :], dl[:, 5, :], dl[:, 5, :], ALU.mult))
            link(TS(dl[:, 0, :], dl[:, 1, :], -2.0, 1.0, ALU.mult, ALU.add))
            link(TS(dl[:, 1, :], dl[:, 4, :], -1.0, None, ALU.mult))
            wide = lambda ap: ap.rearrange("p (g d) -> p g d", d=16)
            cd, sd = (dl[:, k:k + 1, 0:16].broadcast_to([128, 12, 16]) for k in (0, 1))
            rc, rs = (r[:, :, :, :].rearrange("p k t (h d) -> p (k t h) d", d=16) for r in (rot_c, rot_s))
            rt = wide(rot_t[:, :])
            dve.wait_ge(d_tables.sem, TABLES)
            link(TT(rc, wide(C("cos2")), cd, ALU.mult))
            link(TT(rt, wide(C("sin2")), sd, ALU.mult))
            link(TT(rc, rc, rt, ALU.subtract))
            link(TT(rs, wide(C("ssin2")), cd, ALU.mult))
            link(TT(rt, wide(C("scos2")), sd, ALU.mult))
            TT(rs, rs, rt, ALU.add).then_inc(s_rot.sem, 1)
            for lo in (32, 64):
                r = slice(lo, lo + 32)
                link(TS(rank_u[r, :], C("rank_a")[r, :], dl[r, 0, 16:17], None, ALU.mult))
                last = STT(rank_t[r, :], C("rank_b")[r, :], dl[r, 1, 16:17], rank_u[r, :], ALU.mult, ALU.add)
            last.then_inc(s_rot.sem, 1)
            nc.vector.tensor_copy(mbf[:, :], mraw[:, :]).then_inc(s_mb.sem, 1)
            dve.wait_ge(s_rot.sem, 2)
            dve.wait_ge(d_late.sem, LATE)
            assert prep.k == s_prep.per, prep.k

            ov, oc = Own(dve, own_va), Own(dve, own_vc)

            def settled():
                dve.sem_inc(s_pass.sem, 1)

            flat = lambda ap: ap.rearrange("p t c -> p (t c)")

            twice = lambda x: x[:, :, :].rearrange("p t (g o d) -> p (t g) o d", g=4, o=1).broadcast_to([128, 8, 2, 32])

            def split(top, rest, x, done, first):
                mask = high[:, 0:1].rearrange("p (a b c) -> p a b c", a=1, b=1) if len(x.shape) == 4 else high[:, 0:1]
                TT(top.bitcast(U32), x.bitcast(U32), mask.broadcast_to(list(x.shape)), ALU.bitwise_and).then_inc(done.sem, 1)
                dve.wait_ge(done.sem, first)
                TT(rest, x, top, ALU.subtract).then_inc(done.sem, 1)

            def weighted(raw, dst, cut, n):
                k = ov.did(TS(dst, raw[:, 0, :], idxw[0:n, 0:1], None, ALU.mult))
                for h in range(1, NIH):
                    ov.wait(k)
                    k = ov.did(STT(dst, raw[:, h, :], idxw[0:n, h:h + 1], dst, ALU.mult, ALU.add))
                ov.wait(k)
                ov.did(TT(dst, dst, cut, ALU.min))

            def top(i, k, sig_, s_, v, idx):
                r, what = k // 3, k % 3
                if k == 0:
                    dve.wait_ge(own_va.sem, own_va.at(i.n, 5 if sig_ is top_a else 10))
                else:
                    dve.wait_ge(sig_.sem, sig_.at(i.n, k))
                settled()
                v8_, i8_ = v[:, 8 * r:8 * r + 8], idx[:, 8 * r:8 * r + 8]
                if what == 0:
                    ins = nc.vector.max(v8_, s_)
                elif what == 1:
                    ins = nc.vector.max_index(i8_, v8_, s_)
                else:
                    ins = nc.vector.match_replace(s_, v8_, s_, TAKEN)
                ins.then_inc(sig_.sem, 1)

            def stage_a(s, i):
                ov.batch(s, i.n)
                if s == 4:
                    dve.wait_ge(a_free.sem, a_free.at(i.n, 5))
                    weighted(ra, sa[:, :], C("cut_a"), 128)
                if s == 5:
                    dve.wait_ge(a_free.sem, a_free.at(i.n, 7))
                    weighted(rb, sbb[:, :], C("cut_b", 64), 64)
                if s == 8:
                    dve.wait_ge(g_kv.sem, g_kv.at(i.n, 1))
                    dve.wait_ge(g_full.sem, g_full.at(i.n - 2, 12))
                    split(ktop[:, :], krest[:, :], flat(ktab[:, :, :]), g_spl, g_spl.at(i.n, 1))
                    dve.wait_ge(g_spl.sem, g_spl.at(i.n, 2))
                    two = lambda ap: ap.rearrange("p (t c) -> p t c", t=2)
                    nc.vector.tensor_copy(kspl[:, i.par, 0, :], ktop[:, 0:96]).then_inc(g_spl.sem, 1)
                    nc.vector.tensor_copy(kspl[:, i.par, 1, :], krest[:, 0:96]).then_inc(g_spl.sem, 1)
                    nc.vector.tensor_copy(kstk[0:64, i.par, :, :], two(ktop[0:64, :])).then_inc(g_spl.sem, 1)
                    nc.vector.tensor_copy(kstk[64:128, i.par, :, :], two(krest[0:64, :])).then_inc(g_spl.sem, 1)
                for d in range(2) if s == int(s) else ():
                    ka_, kb_ = 2 * (s - 5) + d, 2 * (s - 6) + d
                    if 0 <= ka_ < 11:
                        top(i, ka_, top_a, sa[:, :], va, ia)
                    if 0 <= kb_ < 11:
                        top(i, kb_, top_b, sbb[:, :], vb, ib)
                if s == 12:
                    dve.wait_ge(d_put[1 - i.par].sem, d_put[1 - i.par].at(i.half - 1 + i.par, 32))
                    dve.wait_ge(top_a.sem, top_a.at(i.n, 11))
                    nc.vector.tensor_copy(ja[:, :], ia[:, :]).then_inc(a_slot.sem, 1)
                    dve.wait_ge(top_b.sem, top_b.at(i.n, 11))
                    nc.vector.tensor_copy(jb[:, :], ib[:, :]).then_inc(a_slot.sem, 1)

            def stage_b(s, i):
                p = i.par
                if s < 0:
                    return
                if s in (1.25, 3.25, 5.25, 7.25, 9.25, 11.25):
                    s = int(s)
                    c = s // 2
                    if c == 0:
                        dve.wait_ge(d_idx[p].sem, d_idx[p].at(i.half, 16))
                    dve.wait_ge(g_full.sem, g_full.at(i.n, 2 * c - 2))
                    src = sidx[:, 2 * SLOTS * c:2 * SLOTS * (c + 1)]
                    keys = 1 if c == 1 else 0
                    last = TS(oh[:, c % 2, 0, :], src, C("key_no")[:, keys:keys + 1], None, ALU.is_equal)
                    if c >= 4:
                        last = TS(oh[:, c % 2, 1, :], src, C("key_no")[:, 2:3], None, ALU.is_equal)
                    last.then_inc(o_ready.sem, 1)
                    return
                if s == int(s) + 0.75 and s < NT:
                    t = int(s)
                    w = 96 if t < T0 else SW
                    dve.wait_ge(s_exp.sem, s_exp.at(i.n, t + 1))
                    nc.vector.reciprocal(rls[:, t % 2:t % 2 + 1], lsum[:, t % 2:t % 2 + 1]).then_inc(s_rec.sem, 1)
                    dve.wait_ge(m_full.sem, m_full.at(i.n, max(0, t - 1)))
                    dve.wait_ge(s_rec.sem, s_rec.at(i.n, t + 1))
                    TS(ppn[:, t % 2, 0:w], pp[:, t % 2, 0:w], rls[:, t % 2:t % 2 + 1], None,
                       ALU.mult).then_inc(s_nrm.sem, 1)
                if s != int(s):
                    return
                if s < NT:
                    dve.wait_ge(s_full.sem, s_full.at(i.n, s + 1))
                    w = 96 if s < T0 else SW
                    nc.vector.tensor_reduce(nmx[:, s % 2:s % 2 + 1], bS[:, 0:w], AX, ALU.max,
                                            negate=True).then_inc(s_max.sem, 1)
                if T0 <= s + 1 < NT:
                    g = s + 1 - T0
                    dve.wait_ge(m_full.sem, m_full.at(i.n, s - 1))
                    dve.wait_ge(g_full.sem, g_full.at(i.n, g + 1))
                    TT(gs[:, g % 2, :].rearrange("p (t j) -> p t j", j=FAR),
                       bG[0:96, :].rearrange("p (t j) -> p t j", j=FAR),
                       rank_t[:, :].rearrange("p (o j) -> p o j", o=1).broadcast_to([96, TQ, FAR]),
                       ALU.mult).then_inc(g_out.sem, 1)

            def moments(own, y, stats, m, ln, done):
                for t in range(2):
                    k = own.did(nc.vector.bn_stats(stats[:, t, :], y[:, t, :]))
                own.wait(k)
                settled()
                for t in range(2):
                    k = own.did(nc.vector.bn_aggr(m[:, t, :], stats[:, t, :]))
                own.wait(k)
                TS(ln[:, 0, :], m[:, :, 1], EPS, None, ALU.add).then_inc(done.sem, 1)

            def normalise(own, x, y, m, ln, done):
                own.wait(own.did(TT(ln[:, 3, :], ln[:, 2, :], ln[:, 2, :], ALU.mult)))
                own.wait(own.did(TT(ln[:, 4, :], ln[:, 3, :], ln[:, 0, :], ALU.mult)))
                own.wait(own.did(TS(ln[:, 3, :], ln[:, 4, :], -0.5, 1.5, ALU.mult, ALU.add)))
                own.wait(own.did(TT(ln[:, 5, :], ln[:, 3, :], ln[:, 2, :], ALU.mult)))
                own.did(TS(x[:, 0, :], y[:, 0, :], m[:, 0, 0:1], ln[:, 5, 0:1], ALU.subtract, ALU.mult))
                TS(x[:, 1, :], y[:, 1, :], m[:, 1, 0:1], ln[:, 5, 1:2], ALU.subtract, ALU.mult).then_inc(done.sem, 1)

            def stage_c(s, i):
                p = i.par
                full = lambda use: dve.wait_ge(c_full.sem, c_full.at(i.n, C_AT[use] + 1))
                free = lambda ins: ins.then_inc(c_freeV.sem, 1)
                freed = lambda use: dve.wait_ge(c_freeV.sem, c_freeV.at(i.n, C_BY[:C_AT[use] + 1].count("V")))
                two = lambda ap: ap.rearrange("p (t c) -> p t c", t=2)
                oc.batch(s, i.n)
                if s == 0:
                    full("out")
                    dve.wait_ge(d_cx[p].sem, d_cx[p].at(i.half, 32))
                    free(TT(y[:, :, :], two(bC[:, 0:256]), xr[:, p, :, :], ALU.add))
                    freed("out")
                    moments(oc, y, bst, mv, lnv, ln_st)
                if s == 1:
                    dve.wait_ge(r_k.sem, r_k.at(i.n, 1))
                    dve.wait_ge(c_full.sem, c_full.at(i.n - 1, C_AT["keys1"] + 1))
                    parts = rks[:, :, :, :, :].rearrange("p t g (a b) d -> p (t g) a b d", a=2)
                    split(parts[:, :, 0, :, :], parts[:, :, 1, :, :], twice(rkn), r_ks, r_ks.at(i.n, 1))
                if s == 4:
                    dve.wait_ge(r_q.sem, r_q.at(i.n, 1))
                    dve.wait_ge(c_full.sem, c_full.at(i.n - 1, C_AT["queries1"] + 1))
                    parts = rqs[:, :, :, :, :].rearrange("p t g (b a) d -> p (t g) a b d", a=2)
                    split(parts[:, :, 0, :, :], parts[:, :, 1, :, :], twice(rqn), r_qs, r_qs.at(i.n, 1))
                if s == 1:
                    dve.wait_ge(ln_rs.sem, ln_rs.at(i.n, 1))
                    normalise(oc, x1, y, mv, lnv, c_x1)
                if s == 2.5:
                    full("state")
                    free(TT(st[:, :], bC[:, 0:128], C("carry"), ALU.mult))
                if s in SCORES_AT:
                    u = SCORES_AT.index(s)
                    dve.wait_ge(c_av.sem, c_av.at(i.n, u // 4))
                    full(f"scores{u}")
                    free(TT(sm[:, u % 4, :].rearrange("p (v c) -> p v c", v=4), bC[:, :].rearrange("p (v c) -> p v c", v=4),
                            C("causal").rearrange("p (o c) -> p o c", o=1).broadcast_to([128, 4, 128]), ALU.mult))
                if s == 14.5:
                    full("retained")
                    dve.wait_ge(c_x1.sem, c_x1.at(i.n, 1))
                    free(TT(y[:, :, :], two(bC[:, 0:256]), x1[:, :, :], ALU.add))
                    freed("retained")
                    moments(oc, y, bst, mv, lnv, ln_st)
                if s == 15.5:
                    dve.wait_ge(ln_rs.sem, ln_rs.at(i.n, 2))
                    normalise(oc, x2, y, mv, lnv, c_x2)
            od, of = Own(dve, own_vd), Own(dve, own_vf)

            def over_experts(r):
                return mx2[:, r, :].rearrange("p (t o) -> p t o", o=1).broadcast_to([128, 2, NE])

            def router(i):
                dve.wait_ge(r_ex.sem, r_ex.at(i.n, 1))
                k = od.did(nc.vector.tensor_reduce(mx2[:, 1, :], ex[:, :, :], AX, ALU.add))
                od.wait(k)
                k = od.did(nc.vector.reciprocal(mx2[:, 2, :], mx2[:, 1, :]))
                od.wait(k)
                k = od.did(TT(pr8[:, :, :], ex[:, :, :], over_experts(2), ALU.mult))
                for t in range(2):
                    od.wait(k)
                    settled()
                    m = od.did(nc.vector.max(v8[:, t, :], pr8[:, t, :]))
                for t in range(2):
                    od.wait(m)
                    settled()
                    k = od.did(nc.vector.max_index(i8[:, t, :], v8[:, t, :], pr8[:, t, :]))
                od.wait(k)
                k = od.did(nc.vector.tensor_copy(f8[:, :, :], i8[:, :, :]))
                od.wait(k)
                for t in range(2):
                    for h, r in ((h1, 0), (h2, 1)):
                        k = od.did(TS(h[:, t, :], C("expert_no"), f8[:, t, r:r + 1], v8[:, t, r:r + 1],
                                      ALU.is_equal, ALU.mult))
                od.wait(k)
                TT(gg[:, :, :], h1[:, :, :], h2[:, :, :], ALU.add).then_inc(r_gg.sem, 1)

            def stage_d(s, i):
                p = i.par
                od.batch(s, i.n)
                if s == 0:
                    dve.wait_ge(r_full.sem, r_full.at(i.n, 1))
                    k = od.did(nc.vector.tensor_reduce(mx2[:, 0, :], bR[:, 0:16].rearrange("p (t e) -> p t e", t=2), AX, ALU.max))
                    od.wait(k)
                    TT(lg[:, :, :], bR[:, 0:16].rearrange("p (t e) -> p t e", t=2), over_experts(0), ALU.subtract).then_inc(r_lg.sem, 1)
                if s == 1:
                    router(i)
                if s == 3:
                    dve.wait_ge(r_full.sem, r_full.at(i.n, 3))
                    dve.wait_ge(c_x2.sem, c_x2.at(i.n, 1))
                    dve.wait_ge(d_out[p].sem, d_out[p].at(i.half - 1, 16))
                    TT(acc[:, p, :, :], bR[:, 0:256].rearrange("p (t c) -> p t c", t=2), x2[:, :, :], ALU.add).then_inc(r_acc.sem, 1)
                if s in range(4, 2 * NE + 4):
                    e, t = (s - 4) // 2, s % 2
                    dve.wait_ge(e_y.sem, e_y.at(i.n, s - 3))
                    if s < 6:
                        dve.wait_ge(r_acc.sem, r_acc.at(i.n, 1))
                    else:
                        dve.wait_ge(e_acc.sem, e_acc.at(i.n, s - 5))
                    STT(acc[:, p, t, :], bR[:, 128 * t:128 * t + 128], gg[:, t, e:e + 1], acc[:, p, t, :],
                        ALU.mult, ALU.add).then_inc(e_acc.sem, 1)
                if s == 20:
                    dve.wait_ge(e_acc.sem, e_acc.at(i.n, 16))
                    settled()
                    of.batch(-1, i.n)
                    moments(of, acc[:, p, :, :], fst, fmv, fln, f_st)
                if s == 21:
                    dve.wait_ge(f_rs.sem, f_rs.at(i.n, 1))
                    normalise(of, acc[:, p, :, :], acc[:, p, :, :], fmv, fln, f_ln)

            program(stage_a, stage_b, stage_c, stage_d, dve.Fori)
            assert ov.k == own_va.per and oc.k == own_vc.per, (ov.k, oc.k)


WEIGHTS, OUT_WEIGHTS, DELTA, LATE, TABLES, EXPERTS = 16 * 7, 16 * 2, 16 * 2, 16 * 5, 16 * 4, 16 * 12

_INS = ["x", "ctx_1024"] + ["L0_attn_" + n for n in (
    "W_dkv", "W_uk", "W_uv", "W_dq", "W_uq", "W_qr", "W_kr", "W_out", "idx_wq", "idx_wk", "idx_w", "raw_delta",
)] + ["L0_ffn_" + n for n in ("gate_w", "w1", "b1", "w2", "b2")]


def kernel(**inputs):
    import concourse.bacc as bacc
    from concourse.bass_utils import run_bass_kernel_spmd

    nc = bacc.Bacc("TRN2", target_bir_lowering=False, num_devices=1)
    arrays, io = {}, {}
    for name in _INS:
        a = np.ascontiguousarray(inputs[name])
        arrays["in_" + name] = a
        short = name.replace("L0_attn_", "").replace("L0_ffn_", "").replace("ctx_1024", "ctx")
        io[short] = nc.dram_tensor("in_" + name, a.shape, mybir.dt.from_np(a.dtype), kind="ExternalInput").ap()
    out = nc.dram_tensor("out", (NB, L, DM), F32, kind="ExternalOutput").ap()
    build(nc, io, out)
    r = run_bass_kernel_spmd(nc, [arrays], core_ids=[0])
    return r.results[0]["out"]
```
